# Optimizing a Trainium2 kernel written in Bass

```python
import numpy as np
import jax
import jax.numpy as jnp

def _softmax(x, axis=-1):
    return jax.nn.softmax(x, axis=axis)

def _gelu(x):
    return jax.nn.gelu(x, approximate=True)

def _silu(x):
    return jax.nn.silu(x)

def _sigmoid(x):
    return jax.nn.sigmoid(x)

def _layernorm(x, axis=-1, eps=1e-05):
    m = jnp.mean(x, axis=axis, keepdims=True)
    v = jnp.var(x, axis=axis, keepdims=True)
    return (x - m) / jnp.sqrt(v + eps)

def _scatter_add(tgt, idx, src, axis=0):
    return tgt.at[idx].add(src)

def _segment_sum(src, seg, n):
    return jax.ops.segment_sum(src, seg, n)
kernel_name = 'mk_seq_postln_d1_jaxref_r4_d7243d'

def setup_inputs(seed: int=0):
    np.random.seed(seed)
    _w = jnp.asarray

    def _L0_attn_setup():
        import jax, jax.numpy as jnp
        import numpy as np
        DECAY = 0.95
        EPS = 1e-05
        B, T, D, L = (4, 1024, 256, 2)

        def _layer_norm(x, w, b):
            mu = jnp.mean(x, axis=-1, keepdims=True)
            var = jnp.mean(jnp.square(x - mu), axis=-1, keepdims=True)
            return (x - mu) * jax.lax.rsqrt(var + EPS) * w + b

        def _time_mix_layer(x, ln_w, ln_b, Wk, Wv, Wr, Wo):
            normed = _layer_norm(x, ln_w, ln_b)
            k = jnp.einsum('btd,ed->bte', normed, Wk)
            v = jnp.einsum('btd,ed->bte', normed, Wv)
            r = jax.nn.sigmoid(jnp.einsum('btd,ed->bte', normed, Wr))
            kv = k * v

            def step(state, kv_t):
                state = DECAY * state + (1.0 - DECAY) * kv_t
                return (state, state)
            init = jnp.zeros((x.shape[0], x.shape[2]), dtype=x.dtype)
            _, states = jax.lax.scan(step, init, jnp.swapaxes(kv, 0, 1))
            y = r * jnp.swapaxes(states, 0, 1)
            y = jnp.einsum('btd,ed->bte', y, Wo)
            return x + y
        key = jax.random.key(seed)
        ks = jax.random.split(key, 7)
        scale = 1.0 / np.sqrt(D)
        return {'h': jax.random.normal(ks[0], (B, T, D), dtype=jnp.float32), 'ln_w': jnp.ones((L, D), dtype=jnp.float32), 'ln_b': jnp.zeros((L, D), dtype=jnp.float32), 'Wk': jax.random.normal(ks[1], (L, D, D), dtype=jnp.float32) * scale, 'Wv': jax.random.normal(ks[2], (L, D, D), dtype=jnp.float32) * scale, 'Wr': jax.random.normal(ks[3], (L, D, D), dtype=jnp.float32) * scale, 'Wo': jax.random.normal(ks[4], (L, D, D), dtype=jnp.float32) * scale}
    _L0_attn_in = _L0_attn_setup()

    def _L0_ffn_setup():
        import jax, jax.numpy as jnp
        import numpy as np
        B, S, D = (4, 256, 256)
        E, K = (8, 2)
        H = 2 * D
        key = jax.random.key(seed)
        ks = jax.random.split(key, 5)
        x = jax.random.normal(ks[0], (B, S, D), dtype=jnp.float32)
        Wg = jax.random.normal(ks[1], (E, D), dtype=jnp.float32) * 0.02
        W1 = jax.random.normal(ks[2], (E, H, D), dtype=jnp.float32) * 0.02
        W2 = jax.random.normal(ks[3], (E, H, D), dtype=jnp.float32) * 0.02
        W3 = jax.random.normal(ks[4], (E, D, H), dtype=jnp.float32) * 0.02
        return {'x': x, 'Wg': Wg, 'W1': W1, 'W2': W2, 'W3': W3}
    _L0_ffn_in = _L0_ffn_setup()
    _d = {'L0_attn_h': _L0_attn_in['h'], 'L0_attn_ln_w': _L0_attn_in['ln_w'], 'L0_attn_ln_b': _L0_attn_in['ln_b'], 'L0_attn_Wk': _L0_attn_in['Wk'], 'L0_attn_Wv': _L0_attn_in['Wv'], 'L0_attn_Wr': _L0_attn_in['Wr'], 'L0_attn_Wo': _L0_attn_in['Wo'], 'L0_ffn_Wg': _L0_ffn_in['Wg'], 'L0_ffn_W1': _L0_ffn_in['W1'], 'L0_ffn_W2': _L0_ffn_in['W2'], 'L0_ffn_W3': _L0_ffn_in['W3']}
    _x0 = _d['L0_attn_h']
    _d['L0_attn_h'] = jax.random.normal(jax.random.fold_in(jax.random.key(seed), 1), (4, 2048, 256), dtype=_x0.dtype)
    del _x0
    return _d

def reference(L0_attn_h, L0_attn_ln_w, L0_attn_ln_b, L0_attn_Wk, L0_attn_Wv, L0_attn_Wr, L0_attn_Wo, L0_ffn_Wg, L0_ffn_W1, L0_ffn_W2, L0_ffn_W3):

    def _L0_attn_ref(h, ln_w, ln_b, Wk, Wv, Wr, Wo):
        import jax, jax.numpy as jnp
        import numpy as np
        DECAY = 0.95
        EPS = 1e-05
        B, T, D, L = (4, 1024, 256, 2)

        def _layer_norm(x, w, b):
            mu = jnp.mean(x, axis=-1, keepdims=True)
            var = jnp.mean(jnp.square(x - mu), axis=-1, keepdims=True)
            return (x - mu) * jax.lax.rsqrt(var + EPS) * w + b

        def _time_mix_layer(x, ln_w, ln_b, Wk, Wv, Wr, Wo):
            normed = _layer_norm(x, ln_w, ln_b)
            k = jnp.einsum('btd,ed->bte', normed, Wk)
            v = jnp.einsum('btd,ed->bte', normed, Wv)
            r = jax.nn.sigmoid(jnp.einsum('btd,ed->bte', normed, Wr))
            kv = k * v

            def step(state, kv_t):
                state = DECAY * state + (1.0 - DECAY) * kv_t
                return (state, state)
            init = jnp.zeros((x.shape[0], x.shape[2]), dtype=x.dtype)
            _, states = jax.lax.scan(step, init, jnp.swapaxes(kv, 0, 1))
            y = r * jnp.swapaxes(states, 0, 1)
            y = jnp.einsum('btd,ed->bte', y, Wo)
            return x + y
        out = h
        for i in range(Wk.shape[0]):
            out = _time_mix_layer(out, ln_w[i], ln_b[i], Wk[i], Wv[i], Wr[i], Wo[i])
        return out

    def _L0_ffn_ref(x, Wg, W1, W2, W3):
        import jax, jax.numpy as jnp
        import numpy as np
        B, S, D = (4, 256, 256)
        E, K = (8, 2)
        H = 2 * D
        gate_out = jnp.einsum('bsd,ed->bse', x, Wg)
        top_v, top_i = jax.lax.top_k(gate_out, K)
        probs = jax.nn.softmax(top_v, axis=-1)
        out = jnp.zeros_like(x)
        for e in range(E):
            w_e = jnp.sum(probs * (top_i == e), axis=-1)
            h1 = jnp.einsum('bsd,hd->bsh', x, W1[e])
            h2 = jnp.einsum('bsd,hd->bsh', x, W2[e])
            g = h1 * jax.nn.sigmoid(h1) * h2
            y = jnp.einsum('bsh,dh->bsd', g, W3[e])
            out = out + y * w_e[..., None]
        return out
    x = L0_attn_h
    x = _layernorm(x + _L0_attn_ref(x, L0_attn_ln_w, L0_attn_ln_b, L0_attn_Wk, L0_attn_Wv, L0_attn_Wr, L0_attn_Wo), axis=-1)
    x = _layernorm(x + _L0_ffn_ref(x, L0_ffn_Wg, L0_ffn_W1, L0_ffn_W2, L0_ffn_W3), axis=-1)
    return x

_drawn_inputs = setup_inputs


def setup_inputs(seed=0):
    import zlib

    import numpy as np

    out = dict(_drawn_inputs(seed))
    spreads = {'L0_attn_ln_w': (1.0, 0.6), 'L0_attn_ln_b': (0.0, 0.741)}
    factors = {'L0_ffn_Wg': 3.825, 'L0_ffn_W1': 3.367, 'L0_ffn_W2': 3.324, 'L0_ffn_W3': 3.329}
    for name, (base, spread) in spreads.items():
        noise = np.random.default_rng([zlib.crc32(name.encode()), seed]).standard_normal(out[name].shape)
        drawn = base * np.exp(spread * noise) if base else spread * noise
        out[name] = jnp.asarray(drawn.astype(out[name].dtype))
    for name, factor in factors.items():
        out[name] = (out[name] * factor).astype(out[name].dtype)
    return out
```

```python
from contextlib import ExitStack

import concourse.bass as bass
from concourse import mybir

P = 128
ALU = mybir.AluOpType
ACT = mybir.ActivationFunctionType
F32 = mybir.dt.float32
F32R = mybir.dt.float32r
BF16 = mybir.dt.bfloat16
I32 = mybir.dt.int32
U32 = mybir.dt.uint32
AX_X = mybir.AxisListType.X

B, T, D = 4, 2048, 256
LAYERS = 2
E, H = 8, 512
DECAY, EPS = 0.95, 1e-5
CH = 512
Q = CH // P
DC = D // P
HC = H // P
TOKENS = B * T
CHUNKS = TOKENS // CH
LIST = TOKENS
SLOTS = E * LIST + CH
BLOCKS = 2 * TOKENS // CH + E - 1
WCOLS = 2 * DC * H + HC * D
SCAT = 16 * 2 * Q
RANK_AT = 64


def within(s, low, high):
    return not isinstance(s, int) or low <= s <= high


def at(s, n):
    return isinstance(s, int) and s == n


def attention_phase(nc, h, w_att, ln_wb, w_gate, w_ffn, x_src, x_acc, slot_list, ident, w_raw_all, table, s_fw):
    with ExitStack() as ctx:
        def sb(name, shape, dt=F32):
            return ctx.enter_context(nc.sbuf_tensor(name, shape, dt))

        def sem(name):
            return ctx.enter_context(nc.semaphore(name))

        ring = [ctx.enter_context(nc.psum_tensor(f"ring{i}", [P, CH], F32)) for i in range(4)]
        tp = [ctx.enter_context(nc.psum_tensor(f"tp{i}", [P, CH], F32)) for i in range(DC)]
        out1 = [ctx.enter_context(nc.psum_tensor(f"out1_{i}", [P, 2, D], F32)) for i in range(2)]

        before = sb("before", [P, P], BF16)
        ones = sb("ones", [P, P], BF16)
        decay = sb("decay", [P, CH])
        neg_half = sb("neg_half", [P, Q])
        warm = sb("warm", [P, Q])
        expert_no = sb("expert_no", [P, 2, Q, E])
        w_raw = w_raw_all[:, 0:LAYERS * DC * 4 * D].rearrange("p (l c m) -> p l c m", l=LAYERS, c=DC)
        w_hi = sb("w_hi", [P, LAYERS, DC, 4 * D], F32R)
        w_lo = sb("w_lo", [P, LAYERS, DC, 4 * D], F32R)
        lnp = sb("lnp", [P, 2, LAYERS, DC])
        wg = sb("wg", [P, DC, E])
        bias = sb("bias", [P, LAYERS, 3, DC])
        x_in = sb("x_in", [P, 2, Q, D])
        normed = [sb(f"normed{l}", [P, Q, D]) for l in range(2)]
        xh = [sb(f"xh{l}", [P, DC, CH], F32R) for l in range(2)]
        xl = [sb(f"xl{l}", [P, DC, CH], F32R) for l in range(2)]
        k_sb = sb("k_sb", [P, DC, CH])
        kv = sb("kv", [P, DC, CH])
        state = [sb(f"state{l}", [P, DC, CH]) for l in range(2)]
        r_sb = [sb(f"r_sb{l}", [P, DC, CH]) for l in range(2)]
        y = [sb(f"y{l}", [P, DC, CH]) for l in range(2)]
        yh = [sb(f"yh{l}", [P, DC, CH], F32R) for l in range(2)]
        yl = [sb(f"yl{l}", [P, DC, CH], F32R) for l in range(2)]
        carry = sb("carry", [P, LAYERS, DC, CHUNKS + B])
        xr = sb("xr", [P, Q, D])
        u = sb("u", [P, 2, Q, D])
        z = sb("z", [P, Q, D])
        x1 = sb("x1", [P, 2, Q, D])
        x1T = sb("x1T", [P, DC, CH])
        stats = [sb(f"stats{i}", [P, Q, 6]) for i in range(3)]
        mv = [sb(f"mv{i}", [P, Q, 2]) for i in range(3)]
        ve = [sb(f"ve{i}", [P, Q]) for i in range(3)]
        nm = [sb(f"nm{i}", [P, Q]) for i in range(3)]
        rs = [sb(f"rs{i}", [P, Q]) for i in range(3)]
        nb = [sb(f"nb{i}", [P, Q]) for i in range(3)]
        g = sb("g", [P, Q, E])
        top = sb("top", [P, Q, E])
        pick = sb("pick", [P, Q, E], U32)
        pick_f = sb("pick_f", [P, 2, Q])
        sel = sb("sel", [P, 2, Q, E])
        picked = sb("picked", [P, Q, E], BF16)
        gap = sb("gap", [P, Q])
        slot = sb("slot", [P, Q, E])
        base = sb("base", [P, E])
        own = sb("own", [P, 2, Q, E])
        slot_f = sb("slot_f", [P, 2, Q])
        slot_u = [sb(f"slot_u{i}", [P, Q, 2], U32) for i in range(2)]
        pairs = [sb(f"pairs{i}", [P, Q, 2, 2]) for i in range(2)]
        pad = sb("pad", [P, SLOTS // P, 2], I32)
        block_no = sb("block_no", [1, BLOCKS])
        start = sb("start", [1, E])
        used = sb("used", [1, E])
        used_i = sb("used_i", [1, E], I32)
        one_row = sb("one_row", [1, E])
        end = sb("end", [1, E])
        skip = sb("skip", [1, E])
        past = sb("past", [1, BLOCKS, E])
        hop = sb("hop", [1, BLOCKS, E])
        rows = sb("rows", [1, 2, BLOCKS])

        s_blank, s_ident, s_before, s_expert_no = (sem("blanks_ready"), sem("identity_ready"), sem("before_ready"),
                                                  sem("expert_no_ready"))
        s_base, s_half, s_ones, s_decay, s_zeros = (sem("base_ready"), sem("neg_half_ready"), sem("ones_ready"),
                                                    sem("decay_ready"), sem("zeros_ready"))
        s_w = [sem("weights_loaded0"), sem("weights_loaded1")]
        s_lnp, s_wg, s_pad, s_padst = sem("ln_loaded"), sem("gate_loaded"), sem("pad_ready"), sem("pad_stored")
        s_bias = sem("bias_products")
        s_biassb = [sem("bias_ready0"), sem("bias_ready1")]
        s_whi = [sem("weights_hi0"), sem("weights_hi1")]
        s_wlo = [sem("weights_lo0"), sem("weights_lo1")]
        s_x = [sem("x_loaded0"), sem("x_loaded1")]
        s_bn = [sem(f"tile_stats{i}") for i in range(3)]
        s_mv = [sem(f"mean_var{i}") for i in range(3)]
        s_ve = [sem(f"var_eps{i}") for i in range(3)]
        s_rs = [sem(f"rstd{i}") for i in range(3)]
        s_nb = [sem(f"norm_bias{i}") for i in range(3)]
        s_n = [sem("normed_0"), sem("normed_1")]
        s_pt = [sem(f"transposed{i}") for i in range(3)]
        s_xh = [sem("xh_ready0"), sem("xh_ready1")]
        s_xl = [sem("xl_ready0"), sem("xl_ready1")]
        s_pg = [sem("projected0"), sem("projected1")]
        s_k = [sem("k_ready0"), sem("k_ready1")]
        s_kv = [sem("kv_ready0"), sem("kv_ready1")]
        s_r = [sem("r_ready0"), sem("r_ready1")]
        s_sn = [sem("scanned0"), sem("scanned1")]
        s_cy = [sem("carried0"), sem("carried1")]
        s_y = [sem("y_ready0"), sem("y_ready1")]
        s_yh = [sem("yh_ready0"), sem("yh_ready1")]
        s_yl = [sem("yl_ready0"), sem("yl_ready1")]
        s_po = [sem("out_product0"), sem("out_product1")]
        s_res, s_u, s_z, s_x1 = sem("residual_ready"), sem("u_ready"), sem("z_ready"), sem("x1_ready")
        s_st = [sem("x1_stored0"), sem("x1_stored1")]
        s_x1T, s_g, s_rt, s_gap, s_prob = sem("x1T_ready"), sem("gates"), sem("router_steps"), sem("gap_ready"), sem("probs_ready")
        s_top = sem("gates_ranked")
        s_picked, s_rank, s_slot = sem("picked_ready"), sem("rank_product"), sem("slots_ready")
        s_ids = sem("ids_ready")
        s_sc = [sem("scattered0"), sem("scattered1")]
        s_tab, s_table = sem("table_steps"), sem("table_ready")
        s_met = sem("waits_met")

        block = ctx.enter_context(nc.Block())

        ROUTER = 6
        LAST = CHUNKS + 4

        def run(eng, step):
            for s in range(6):
                step(s, s // 2, s % 2)
            with eng.Fori(3, CHUNKS // 2 - 1) as it:
                step(it * 2, it, 0)
                step(it * 2 + 1, it, 1)
            for s in range(CHUNKS - 2, LAST):
                step(s, s // 2, s % 2)

        def bank(l, e, m, j):
            return ring[(2 * j + 8 * l + 3 * e + m) % 4][:, :]

        @block.sync
        def _(sp):
            def load(n, par):
                row = n * P if isinstance(n, int) else sp.snap(n * P)
                if within(n, 2, CHUNKS):
                    sp.wait_ge(s_u, n - 1)
                sp.dma_start(x_in[:, par, :, :], h[bass.ds(row, P), :]
                             .rearrange("p (q d) -> p q d", q=Q)).then_inc(s_x[par], 16)

            load(0, 0)
            sp.dma_start(lnp[:, :, :, :], ln_wb).then_inc(s_lnp, 16)
            for l in range(LAYERS):
                sp.dma_start(w_raw[:, l, :, :], w_att[:, l, :, :]).then_inc(s_w[l], 16)
                if l == 0:
                    load(1, 1)
            sp.dma_start(wg[:, :, :], w_gate).then_inc(s_wg, 16)
            sp.wait_ge(s_pad, 2)
            sp.dma_start(slot_list.rearrange("(p n) c -> p n c", p=P), pad[:, :, :]).then_inc(s_padst, 16)
            sp.wait_ge(s_zeros, 1)
            for dst in (x_src, x_acc):
                sp.dma_start(dst[TOKENS:TOKENS + CH, :].rearrange("(p q) d -> p q d", p=P), z[:, :, :]).then_inc(s_padst, 16)

            def step(s, half, j):
                if within(s, 1, CHUNKS - 2):
                    load(s + 1, 1 - j)
                if within(s, 2, CHUNKS + 1):
                    row = (s - 2) * CH if isinstance(s, int) else sp.snap(s * CH - 2 * CH)
                    sp.wait_ge(s_x1, s - 1)
                    for dst in (x_src, x_acc):
                        sp.dma_start(dst[bass.ds(row, CH), :].rearrange("(p q) d -> p q d", p=P),
                                     x1[:, j, :, :]).then_inc(s_st[j], 16)

            run(sp, step)
            sp.wait_ge(s_table, 1)
            for l in range(LAYERS):
                sp.wait_ge(s_bias, l + 1)
                sp.wait_ge(s_whi[l], DC + 1)
                sp.wait_ge(s_wlo[l], DC + 1)
            for b in range(2):
                w_row = sp.value_load(table[0:1, 0, b:b + 1], min_val=0, max_val=(E - 1) * P)
                sp.dma_start(w_raw_all[:, b * WCOLS:(b + 1) * WCOLS], w_ffn[bass.ds(w_row, P), :]).then_inc(s_fw[b], 16)
            sp.wait_ge(s_wg, 16)
            sp.wait_ge(s_padst, 48)
            for par in range(2):
                sp.wait_ge(s_st[par], 32 * (CHUNKS // 2))
                sp.wait_ge(s_sc[par], SCAT * (CHUNKS // 2))

        @block.scalar
        def _(act):
            act.wait_ge(s_half, 1)
            nc.scalar.activation(warm[:, :], neg_half[:, :], ACT.Sigmoid)

            def split_weights(l):
                act.wait_ge(s_lnp, 16)
                act.wait_ge(s_w[l], 16)
                for dc in range(DC):
                    nc.scalar.activation(w_hi[:, l, dc, 0:3 * D], w_raw[:, l, dc, 0:3 * D], ACT.Copy,
                                         scale=lnp[:, 0, l, dc:dc + 1]).then_inc(s_whi[l], 1)
                nc.scalar.activation(w_hi[:, l, :, 3 * D:4 * D], w_raw[:, l, :, 3 * D:4 * D], ACT.Copy).then_inc(s_whi[l], 1)

            def normalize(i, src, dst, n, done):
                act.wait_ge(s_nb[i], n + 1)
                for q in range(Q):
                    last = nc.scalar.activation(dst[:, q, :], src[:, q, :], ACT.Identity,
                                                bias=nb[i][:, q:q + 1], scale=rs[i][:, q:q + 1])
                last.then_inc(done, 1)

            def x_hi(l, n):
                for dc in range(DC):
                    act.wait_ge(s_pt[l], n * 2 + dc + 1)
                    nc.scalar.activation(xh[l][:, dc, :], tp[dc][:, :], ACT.Copy).then_inc(s_xh[l], 1)

            def keep_k(l, n, e, j, free_sem, free_at):
                act.wait_ge(s_pg[l], n * 6 + 3 * e + 1)
                if free_sem is not None:
                    act.wait_ge(free_sem, free_at)
                nc.scalar.activation(k_sb[:, e, :], bank(l, e, 0, j), ACT.Identity,
                                     bias=bias[:, l, 0, e:e + 1], scale=1.0 - DECAY).then_inc(s_k[l], 1)

            def gate_r(l, n, e, j):
                act.wait_ge(s_pg[l], n * 6 + 3 * e + 3)
                if within(n, 1, CHUNKS):
                    act.wait_ge(s_y[l], n * 2 + e - 1)
                nc.scalar.activation(r_sb[l][:, e, :], bank(l, e, 2, j), ACT.Sigmoid,
                                     bias=bias[:, l, 2, e:e + 1]).then_inc(s_r[l], 1)

            def y_hi(l, n, e):
                act.wait_ge(s_y[l], n * 2 + e + 1)
                if within(n, 1, CHUNKS):
                    act.wait_ge(s_po[l], n * 2)
                nc.scalar.activation(yh[l][:, e, :], y[l][:, e, :], ACT.Copy).then_inc(s_yh[l], 1)

            def keep_x1T(s):
                for dc in range(DC):
                    act.wait_ge(s_pt[2], s * 2 + dc - 5)
                    if within(s, 4, CHUNKS + 2):
                        act.wait_ge(s_g, s - 3)
                    nc.scalar.activation(x1T[:, dc, :], tp[dc][:, :], ACT.Copy).then_inc(s_x1T, 1)

            def normalize3(s, half, j):
                if within(s, 4, CHUNKS + 1):
                    act.wait_ge(s_st[j], half * 32 - 32)
                    act.wait_ge(s_pt[2], s * 2 - 6)
                normalize(2, z, x1[:, j, :, :], s - 2, s_x1)

            normalize(0, x_in[:, 0, :, :], normed[0], 0, s_n[0])
            split_weights(0)
            x_hi(0, 0)
            act.wait_ge(s_pt[0], 2)
            normalize(0, x_in[:, 1, :, :], normed[0], 1, s_n[0])
            act.wait_ge(s_biassb[0], 2)

            def step(s, half, j):
                layer1, layer2 = within(s, 0, CHUNKS - 1), within(s, 1, CHUNKS)
                if layer1:
                    for e in range(DC):
                        if at(s, 0):
                            keep_k(0, s, e, j, None, 0)
                        elif at(s, 1):
                            keep_k(0, s, e, j, s_kv[0], 2)
                        else:
                            keep_k(0, s, e, j, s_kv[1], s * 2 + e - 3)
                        if e == 1 and layer2:
                            if within(s, 2, CHUNKS):
                                act.wait_ge(s_pt[1], s * 2 - 2)
                            normalize(1, xr, normed[1], s - 1, s_n[1])
                        gate_r(0, s, e, j)
                elif layer2:
                    act.wait_ge(s_pt[1], s * 2 - 2)
                    normalize(1, xr, normed[1], s - 1, s_n[1])
                if at(s, 0):
                    x_hi(0, 1)
                if at(s, CHUNKS):
                    keep_x1T(s)
                if layer2:
                    x_hi(1, s - 1)
                if at(s, CHUNKS):
                    normalize3(s, half, j)
                if layer1:
                    for e in range(DC):
                        y_hi(0, s, e)
                if at(s, 0):
                    split_weights(1)
                    act.wait_ge(s_biassb[1], 2)
                if within(s, 1, CHUNKS - 2):
                    act.wait_ge(s_pt[0], s * 2 + 2)
                    normalize(0, x_in[:, 1 - j, :, :], normed[0], s + 1, s_n[0])
                if within(s, 3, CHUNKS + 2) and not at(s, CHUNKS):
                    keep_x1T(s)
                if layer2:
                    if at(s, CHUNKS):
                        keep_k(1, s - 1, 0, j, s_kv[1], 2 * s - 3)
                    else:
                        keep_k(1, s - 1, 0, j, s_kv[0], s * 2 + 1)
                if within(s, 2, CHUNKS + 1) and not at(s, CHUNKS):
                    normalize3(s, half, j)
                if layer2:
                    gate_r(1, s - 1, 0, j)
                if within(s, 1, CHUNKS - 2):
                    x_hi(0, s + 1)
                if layer2:
                    if at(s, CHUNKS):
                        keep_k(1, s - 1, 1, j, s_kv[1], 2 * s - 2)
                    else:
                        keep_k(1, s - 1, 1, j, s_kv[0], s * 2 + 2)
                    y_hi(1, s - 1, 0)
                if within(s, 3, CHUNKS + 2):
                    act.wait_ge(s_gap, s - 2)
                    if within(s, 5, CHUNKS + 2):
                        act.wait_ge(s_sc[1 - j], (half - 2 + j) * SCAT)
                    nc.scalar.activation(pairs[1 - j][:, :, 0, 1], gap[:, :], ACT.Sigmoid)
                    nc.scalar.activation(pairs[1 - j][:, :, 1, 1], gap[:, :], ACT.Sigmoid, scale=-1.0).then_inc(s_prob, 1)
                if layer2:
                    gate_r(1, s - 1, 1, j)
                    y_hi(1, s - 1, 1)

            run(act, step)

        @block.gpsimd
        def _(pool):
            nc.gpsimd.memset(ident[:, :], 0.0).then_inc(s_blank, 1)
            nc.gpsimd.memset(before[:, :], 0.0).then_inc(s_blank, 1)
            nc.gpsimd.memset(pad[:, :, :], 0).then_inc(s_blank, 1)
            pool.wait_ge(s_blank, 3)
            nc.gpsimd.affine_select(out=ident[:, :], in_=ident[:, :], compare_op=ALU.not_equal, fill=1.0,
                                    base=0, pattern=[[-1, P]], channel_multiplier=1).then_inc(s_ident, 1)
            nc.gpsimd.affine_select(out=before[:, :], in_=before[:, :], compare_op=ALU.is_ge, fill=1.0,
                                    base=0, pattern=[[-1, P]], channel_multiplier=1).then_inc(s_before, 1)
            nc.gpsimd.iota(pad[:, :, 0], [[1, SLOTS // P]], base=0,
                           channel_multiplier=SLOTS // P).then_inc(s_pad, 1)
            nc.gpsimd.iota(expert_no[:, :, :, :], [[0, 2], [0, Q], [1, E]], base=0, channel_multiplier=0,
                           allow_small_or_imprecise_dtypes=True).then_inc(s_expert_no, 1)
            nc.gpsimd.iota(base[:, :], [[LIST, E]], base=0, channel_multiplier=0,
                           allow_small_or_imprecise_dtypes=True).then_inc(s_base, 1)
            for j in range(2):
                nc.gpsimd.iota(pairs[j][:, :, :, 0].bitcast(I32), [[1, Q], [0, 2]], base=CH * j - 2 * CH,
                               channel_multiplier=Q).then_inc(s_ids, 1)

            nc.gpsimd.iota(block_no[:, :], [[1, BLOCKS]], base=0, channel_multiplier=0,
                           allow_small_or_imprecise_dtypes=True).then_inc(s_tab, 1)
            nc.gpsimd.iota(start[:, :], [[LIST, E]], base=0, channel_multiplier=0,
                           allow_small_or_imprecise_dtypes=True).then_inc(s_tab, 1)

            def rstd(i, n):
                pool.wait_ge(s_ve[i], n * 2 + 2)
                if within(n, 1, CHUNKS):
                    pool.wait_ge((s_n[0], s_n[1], s_x1)[i], n)
                nc.gpsimd.tensor_tensor(rs[i][:, :], ve[i][:, :], neg_half[:, :], ALU.pow).then_inc(s_rs[i], 1)
                pool.wait_ge(s_rs[i], n + 1)
                nc.gpsimd.tensor_tensor(nb[i][:, :], rs[i][:, :], nm[i][:, :], ALU.mult).then_inc(s_nb[i], 1)

            def gated(l, n, e):
                pool.wait_ge(s_sn[l], n * 2 + e + 1)
                pool.wait_ge(s_r[l], n * 2 + e + 1)
                if within(n, 1, CHUNKS):
                    pool.wait_ge(s_yh[l], n * 2 + e - 1)
                    pool.wait_ge(s_yl[l], n * 2 + e - 1)
                nc.gpsimd.tensor_tensor(y[l][:, e, :], state[l][:, e, :], r_sb[l][:, e, :],
                                        ALU.mult).then_inc(s_y[l], 1)

            def y_lo(l, n, e):
                pool.wait_ge(s_y[l], n * 2 + e + 1)
                pool.wait_ge(s_yh[l], n * 2 + e + 1)
                if within(n, 1, CHUNKS):
                    pool.wait_ge(s_po[l], n * 2)
                nc.gpsimd.tensor_tensor(yl[l][:, e, :], y[l][:, e, :], yh[l][:, e, :].bitcast(F32),
                                        ALU.subtract).then_inc(s_yl[l], 1)

            def open_scatter(s, half, j):
                if not within(s, 4, CHUNKS + 3):
                    return
                if within(s, 6, CHUNKS + 3):
                    pool.wait_ge(s_sc[j], (half - 2) * SCAT)
                pool.wait_ge(s_ids, s - 2)
                pool.sem_inc(s_met, 1)
                ids = pairs[j][:, :, :, 0].bitcast(I32)
                nc.gpsimd.tensor_scalar(ids, ids, 2 * CH, None, ALU.add).then_inc(s_ids, 1)
                pool.wait_ge(s_ids, s - 1)
                pool.wait_ge(s_prob, s - 3)
                pool.wait_ge(s_slot, s - 3)
                pool.wait_ge(s_padst, 48)
                pool.sem_inc(s_met, 1)

            def scatter(s, j, first, count):
                if not within(s, 4, CHUNKS + 3):
                    return
                for i in range(first, first + count):
                    q, c = i // 2, i % 2
                    nc.gpsimd.indirect_dma_start(
                        slot_list, bass.IndirectOffsetOnAxis(slot_u[j][:, q, c:c + 1], 0),
                        pairs[j][:, q, c, :].bitcast(I32), None).then_inc(s_sc[j], 16)

            pool.wait_ge(s_half, 1)
            rstd(0, 0)
            rstd(0, 1)

            def step(s, half, j):
                layer1, layer2 = within(s, 0, CHUNKS - 1), within(s, 1, CHUNKS)
                if at(s, CHUNKS):
                    rstd(1, s - 1)
                    open_scatter(s, half, j)
                    scatter(s, j, 0, 2)
                    rstd(2, s - 2)
                    scatter(s, j, 2, 3)
                    gated(1, s - 1, 0)
                    scatter(s, j, 5, 1)
                    y_lo(1, s - 1, 0)
                    scatter(s, j, 6, 2)
                    gated(1, s - 1, 1)
                    y_lo(1, s - 1, 1)
                    return
                if at(s, CHUNKS + 1):
                    open_scatter(s, half, j)
                    scatter(s, j, 0, 6)
                    rstd(2, s - 2)
                    scatter(s, j, 6, 2)
                    return
                open_scatter(s, half, j)
                scatter(s, j, 0, 2)
                if layer2:
                    rstd(1, s - 1)
                if layer1:
                    gated(0, s, 0)
                scatter(s, j, 2, 2)
                if layer1:
                    gated(0, s, 1)
                    y_lo(0, s, 0)
                if within(s, 1, CHUNKS - 2):
                    rstd(0, s + 1)
                if layer1:
                    y_lo(0, s, 1)
                scatter(s, j, 4, 1)
                if within(s, 2, CHUNKS + 1):
                    rstd(2, s - 2)
                scatter(s, j, 5, 1)
                if layer2:
                    gated(1, s - 1, 0)
                scatter(s, j, 6, 1)
                if layer2:
                    y_lo(1, s - 1, 0)
                scatter(s, j, 7, 1)
                if layer2:
                    gated(1, s - 1, 1)
                    y_lo(1, s - 1, 1)

            run(pool, step)

        @block.vector
        def _(dve):
            nc.vector.memset(neg_half[:, :], -0.5).then_inc(s_half, 1)
            nc.vector.memset(z[:, :, :], 0.0).then_inc(s_zeros, 1)
            nc.vector.memset(decay[:, :], DECAY).then_inc(s_decay, 1)
            nc.vector.memset(ones[:, :], 1.0).then_inc(s_ones, 1)
            nc.vector.memset(one_row[:, :], 1.0).then_inc(s_tab, 1)
            for l in range(LAYERS):
                nc.vector.memset(carry[:, l, :, :], 0.0).then_inc(s_cy[l], 2)

            def norm_stats(i, src, n):
                for q in range(Q):
                    nc.vector.bn_stats(stats[i][:, q, :], src[:, q, :]).then_inc(s_bn[i], 1)
                dve.wait_ge(s_bn[i], n * Q + Q)
                if within(n, 1, CHUNKS):
                    dve.wait_ge(s_nb[i], n)
                dve.sem_inc(s_met, 1)
                for q in range(Q):
                    nc.vector.bn_aggr(mv[i][:, q, :], stats[i][:, q, :]).then_inc(s_mv[i], 1)
                dve.wait_ge(s_mv[i], n * Q + Q)
                nc.vector.tensor_scalar(ve[i][:, :], mv[i][:, :, 1], EPS, None, ALU.add).then_inc(s_ve[i], 1)
                nc.vector.tensor_scalar(nm[i][:, :], mv[i][:, :, 0], -1.0, None, ALU.mult).then_inc(s_ve[i], 1)

            def x_lo(l, n):
                for dc in range(DC):
                    dve.wait_ge(s_xh[l], n * 2 + dc + 1)
                    nc.vector.tensor_tensor(xl[l][:, dc, :], tp[dc][:, :], xh[l][:, dc, :].bitcast(F32),
                                            ALU.subtract).then_inc(s_xl[l], 1)

            def low_weights(l):
                dve.wait_ge(s_lnp, 16)
                dve.wait_ge(s_w[l], 16)
                for dc in range(DC):
                    dve.wait_ge(s_whi[l], dc + 1)
                    nc.vector.scalar_tensor_tensor(w_lo[:, l, dc, 0:3 * D], w_raw[:, l, dc, 0:3 * D],
                                                   lnp[:, 0, l, dc:dc + 1], w_hi[:, l, dc, 0:3 * D].bitcast(F32),
                                                   ALU.mult, ALU.subtract).then_inc(s_wlo[l], 1)
                dve.wait_ge(s_whi[l], DC + 1)
                nc.vector.tensor_tensor(w_lo[:, l, :, 3 * D:4 * D], w_raw[:, l, :, 3 * D:4 * D],
                                        w_hi[:, l, :, 3 * D:4 * D].bitcast(F32), ALU.subtract).then_inc(s_wlo[l], 1)

            def keep_bias(l):
                dve.wait_ge(s_bias, l + 1)
                nc.vector.tensor_copy(bias[:, l, :, :], out1[1][:, 0, l * 3 * DC:(l + 1) * 3 * DC]
                                      .rearrange("p (m e) -> p m e", m=3)).then_inc(s_biassb[l], 1)
                dve.wait_ge(s_biassb[l], 1)
                nc.vector.tensor_scalar(bias[:, l, 0, :], bias[:, l, 0, :], 1.0 - DECAY, None, ALU.mult).then_inc(s_biassb[l], 1)

            dve.wait_ge(s_x[0], 16)
            norm_stats(0, x_in[:, 0, :, :], 0)
            low_weights(0)
            x_lo(0, 0)
            keep_bias(0)
            dve.wait_ge(s_x[1], 16)
            norm_stats(0, x_in[:, 1, :, :], 1)
            dve.wait_ge(s_pad, 1)
            nc.vector.tensor_scalar(pad[:, :, 0], pad[:, :, 0], CH - 1, TOKENS, ALU.bitwise_and,
                                    ALU.bitwise_or).then_inc(s_pad, 1)
            dve.wait_ge(s_decay, 1)
            dve.wait_ge(s_expert_no, 1)
            dve.wait_ge(s_base, 1)

            def recur(l, n, e, j):
                dve.wait_ge(s_pg[l], n * 6 + 3 * e + 2)
                dve.wait_ge(s_k[l], n * 2 + e + 1)
                nc.vector.scalar_tensor_tensor(
                    kv[:, e, :], bank(l, e, 1, j), bias[:, l, 1, e:e + 1],
                    k_sb[:, e, :], ALU.add, ALU.mult).then_inc(s_kv[l], 1)
                dve.wait_ge(s_kv[l], n * 2 + e + 1)
                if within(n, 1, CHUNKS):
                    dve.wait_ge(s_y[l], n * 2 + e - 1)
                dve.wait_ge(s_cy[l], n * 2 + 2)
                nc.vector.tensor_tensor_scan(state[l][:, e, :], decay[:, :], kv[:, e, :],
                                             carry[:, l, e, bass.ds(n, 1)], ALU.mult, ALU.add).then_inc(s_sn[l], 1)
                dve.wait_ge(s_sn[l], n * 2 + e + 1)
                nc.vector.tensor_copy(carry[:, l, e, bass.ds(n + B, 1)], state[l][:, e, CH - 1:CH]).then_inc(s_cy[l], 1)

            def link(m, k, ins):
                ins.then_inc(s_rt, 1)
                dve.wait_ge(s_rt, m * ROUTER + k)

            def choose(m):
                dve.wait_ge(s_g, m + 1)
                link(m, 1, nc.vector.tensor_copy(g[:, :, :], out1[0][:, 0, 0:Q * E].rearrange("p (q e) -> p q e", q=Q)))
                dve.sem_inc(s_met, 1)
                for q in range(Q):
                    nc.vector.max(top[:, q, :], g[:, q, :]).then_inc(s_top, 1)
                dve.wait_ge(s_top, m * (2 * Q) + Q)
                dve.sem_inc(s_met, 1)
                for q in range(Q):
                    nc.vector.max_index(pick[:, q, :], top[:, q, :], g[:, q, :]).then_inc(s_top, 1)
                dve.wait_ge(s_top, m * (2 * Q) + 2 * Q)
                link(m, 2, nc.vector.tensor_copy(pick_f[:, :, :], pick[:, :, 0:2].rearrange("p q c -> p c q")))
                if within(m, 1, CHUNKS):
                    dve.wait_ge(s_prob, m)
                nc.vector.tensor_tensor(gap[:, :], top[:, :, 0], top[:, :, 1], ALU.subtract).then_inc(s_gap, 1)
                link(m, 3, nc.vector.tensor_tensor(sel[:, :, :, :], expert_no[:, :, :, :],
                                                   pick_f[:, :, :].unsqueeze(3).to_broadcast([P, 2, Q, E]), ALU.is_equal))
                if within(m, 1, CHUNKS):
                    dve.wait_ge(s_rank, m)
                nc.vector.tensor_tensor(picked[:, :, :], sel[:, 0, :, :], sel[:, 1, :, :], ALU.add).then_inc(s_picked, 1)

            def place(m, half, j):
                ranks = out1[0][:, 0, RANK_AT:RANK_AT + Q * E].rearrange("p (q e) -> p q e", q=Q)
                total = out1[0][:, 0, RANK_AT + Q * E:RANK_AT + Q * E + E]
                dve.wait_ge(s_rank, m + 1)
                link(m, 4, nc.vector.tensor_tensor(slot[:, :, :], ranks, base[:, :].unsqueeze(1).to_broadcast([P, Q, E]), ALU.add))
                nc.vector.tensor_tensor(base[:, :], total, base[:, :], ALU.add).then_inc(s_base, 1)
                link(m, 5, nc.vector.tensor_tensor(own[:, :, :, :], sel[:, :, :, :],
                                                   slot[:, :, :].unsqueeze(1).to_broadcast([P, 2, Q, E]), ALU.mult))
                dve.wait_ge(s_base, m + 2)
                link(m, 6, nc.vector.reduce_sum(slot_f[:, :, :], own[:, :, :, :], AX_X))
                if within(m, 2, CHUNKS):
                    dve.wait_ge(s_sc[1 - j], (half - 2 + j) * SCAT)
                nc.vector.tensor_copy(slot_u[1 - j][:, :, :], slot_f[:, :, :].rearrange("p c q -> p q c")).then_inc(s_slot, 1)

            def residual1(s, j):
                for i, b in enumerate((1, 0)):
                    dve.wait_ge(s_po[0], s * 2 + i - 1)
                    if within(s, 2, CHUNKS):
                        dve.wait_ge(s_u, s - 1)
                    nc.vector.tensor_tensor(xr[:, 2 * b:2 * b + 2, :], out1[b][:, :, :],
                                            x_in[:, 1 - j, 2 * b:2 * b + 2, :], ALU.add).then_inc(s_res, 1)
                dve.wait_ge(s_res, s * 2)

            def add_input(s, j):
                if within(s, 3, CHUNKS):
                    dve.wait_ge(s_z, s * 2 - 4)
                nc.vector.tensor_tensor(u[:, 1 - j, :, :], xr[:, :, :], x_in[:, 1 - j, :, :], ALU.add).then_inc(s_u, 1)

            def residual2(s, j):
                for b in range(2):
                    dve.wait_ge(s_po[1], s * 2 + b - 3)
                    dve.wait_ge(s_u, s - 1)
                    if at(s, 2):
                        dve.wait_ge(s_padst, 48)
                    else:
                        dve.wait_ge(s_x1, s - 2)
                    src = ring[(2 * j + 6 + b) % 4][:, :].rearrange("p (q d) -> p q d", q=2)
                    nc.vector.tensor_tensor(z[:, 2 * b:2 * b + 2, :], src, u[:, j, 2 * b:2 * b + 2, :],
                                            ALU.add).then_inc(s_z, 1)
                dve.wait_ge(s_z, s * 2 - 2)
                norm_stats(2, z, s - 2)

            def step(s, half, j):
                layer1, layer2 = within(s, 0, CHUNKS - 1), within(s, 1, CHUNKS)
                if layer2:
                    residual1(s, j)
                    if not at(s, CHUNKS):
                        add_input(s, j)
                    norm_stats(1, xr, s - 1)
                if at(s, CHUNKS):
                    residual2(s, j)
                if layer1:
                    for e in range(DC):
                        recur(0, s, e, j)
                if within(s, 1, CHUNKS - 2):
                    dve.wait_ge(s_x[1 - j], half * 16 + 16 * (1 + j))
                    norm_stats(0, x_in[:, 1 - j, :, :], s + 1)
                if at(s, 0):
                    x_lo(0, 1)
                    low_weights(1)
                    keep_bias(1)
                if layer2:
                    x_lo(1, s - 1)
                if at(s, CHUNKS):
                    add_input(s, j)
                if at(s, CHUNKS + 1):
                    choose(s - 3)
                if within(s, 2, CHUNKS + 1) and not at(s, CHUNKS):
                    residual2(s, j)
                if layer2:
                    recur(1, s - 1, 0, j)
                if within(s, 3, CHUNKS + 2) and not at(s, CHUNKS + 1):
                    choose(s - 3)
                if within(s, 1, CHUNKS - 2):
                    x_lo(0, s + 1)
                if layer2:
                    recur(1, s - 1, 1, j)
                if within(s, 3, CHUNKS + 2):
                    place(s - 3, half, j)

            run(dve, step)
            count = [3]

            def table_link(ins):
                count[0] += 1
                ins.then_inc(s_tab, 1)
                dve.wait_ge(s_tab, count[0])

            dve.wait_ge(s_tab, 3)
            dve.wait_ge(s_base, CHUNKS + 1)

            def by_block(x):
                return x.unsqueeze(1).to_broadcast([1, BLOCKS, E])

            table_link(nc.vector.tensor_tensor(used[:, :], base[0:1, :], start[:, :], ALU.subtract))
            table_link(nc.vector.tensor_scalar(used_i[:, :], used[:, :], CH - 1.0, None, ALU.add))
            table_link(nc.vector.tensor_scalar(used_i[:, :], used_i[:, :], CH.bit_length() - 1, None, ALU.logical_shift_right))
            table_link(nc.vector.tensor_copy(used[:, :], used_i[:, :]))
            table_link(nc.vector.tensor_tensor_scan(end[:, :], one_row[:, :], used[:, :], 0.0, ALU.mult, ALU.add))
            table_link(nc.vector.tensor_scalar(skip[:, :], used[:, :], -float(CH), float(LIST), ALU.mult, ALU.add))
            table_link(nc.vector.tensor_tensor(past[:, :, :], block_no[:, :].unsqueeze(2).to_broadcast([1, BLOCKS, E]),
                                         by_block(end[:, :]), ALU.is_ge))
            table_link(nc.vector.tensor_tensor(hop[:, :, :], past[:, :, :], by_block(skip[:, :]), ALU.mult))
            table_link(nc.vector.reduce_sum(rows[:, 0, :], past[:, :, :], AX_X))
            table_link(nc.vector.reduce_sum(rows[:, 1, :], hop[:, :, :], AX_X))
            table_link(nc.vector.scalar_tensor_tensor(rows[:, 1, :], block_no[:, :], float(CH), rows[:, 1, :], ALU.mult, ALU.add))
            table_link(nc.vector.tensor_scalar(rows[:, 0, :], rows[:, 0, :], E - 1.0, float(P), ALU.min, ALU.mult))
            table_link(nc.vector.tensor_scalar(rows[:, 1, :], rows[:, 1, :], float(E * LIST), None, ALU.min))
            nc.vector.tensor_copy(table[:, :, :], rows[:, :, :]).then_inc(s_table, 1)

        @block.tensor
        def _(pe):
            def transpose(i, n, src):
                for dc in range(DC):
                    for q in range(Q):
                        last = nc.tensor.transpose(tp[dc][:, q * P:(q + 1) * P], src[:, q, dc * P:(dc + 1) * P], ident[:, :])
                    last.then_inc(s_pt[i], 1)

            def bias_products(l):
                pe.wait_ge(s_lnp, 16)
                pe.wait_ge(s_w[l], 16)
                for m in range(3):
                    for e in range(DC):
                        c = (l * 3 + m) * DC + e
                        for dc in range(DC):
                            last = nc.tensor.matmul(out1[1][:, 0, c:c + 1], w_raw[:, l, dc, m * D + e * P:m * D + (e + 1) * P],
                                                    lnp[:, 1, l, dc:dc + 1], start=dc == 0, stop=dc == DC - 1)
                last.then_inc(s_bias, 1)

            def project(l, s, n, e, j, products=(0, 1, 2)):
                pe.wait_ge(s_xh[l], n * 2 + 2)
                pe.wait_ge(s_xl[l], n * 2 + 2)
                for m in products:
                    slot_no = 8 * l + 3 * e + m
                    if at(s, 0) and slot_no < 4:
                        holder = None
                    elif at(s, 1) and slot_no < 4:
                        holder, count = ((s_r[0], 1), (s_k[0], 2), (s_kv[0], 2), (s_r[0], 2))[slot_no]
                    elif at(s, 1) and slot_no in (10, 11):
                        holder, count = ((s_r[0], 3), (s_k[0], 4))[slot_no - 10]
                    elif at(s, CHUNKS) and slot_no in (8, 9):
                        holder, count = ((s_r[1], 2 * s - 3), (s_k[1], 2 * s - 2))[slot_no - 8]
                    else:
                        holder, count = {
                            0: (s_r[1], s * 2 - 3), 1: (s_k[1], s * 2 - 2), 2: (s_kv[1], s * 2 - 2), 3: (s_r[1], s * 2 - 2),
                            4: (s_k[0], s * 2 + 1), 5: (s_kv[0], s * 2 + 1),
                            8: (s_kv[0], s * 2 + 2), 9: (s_r[0], s * 2 + 2), 10: (s_z, s * 2 - 3), 11: (s_z, s * 2 - 2),
                            12: (s_k[1], s * 2 - 1), 13: (s_kv[1], s * 2 - 1)}[slot_no]
                    if holder is not None:
                        pe.wait_ge(holder, count)
                    out = bank(l, e, m, j)
                    col = m * D + e * P
                    for dc in range(DC):
                        hi, lo = w_hi[:, l, dc, col:col + P], w_lo[:, l, dc, col:col + P]
                        nc.tensor.matmul(out, hi, xh[l][:, dc, :], start=dc == 0, stop=False)
                        nc.tensor.matmul(out, hi, xl[l][:, dc, :], start=False, stop=False)
                        last = nc.tensor.matmul(out, lo, xh[l][:, dc, :], start=False, stop=dc == DC - 1)
                    last.then_inc(s_pg[l], 1)

            def output(l, out, q0):
                for i in range(2):
                    q = q0 + i
                    for dc in range(DC):
                        a, b = yh[l][:, dc, q * P:(q + 1) * P], yl[l][:, dc, q * P:(q + 1) * P]
                        hi, lo = w_hi[:, l, dc, 3 * D:4 * D], w_lo[:, l, dc, 3 * D:4 * D]
                        nc.tensor.matmul(out[:, i * D:(i + 1) * D], a, hi, start=dc == 0, stop=False)
                        nc.tensor.matmul(out[:, i * D:(i + 1) * D], a, lo, start=False, stop=False)
                        last = nc.tensor.matmul(out[:, i * D:(i + 1) * D], b, hi, start=False, stop=dc == DC - 1)
                last.then_inc(s_po[l], 1)

            def rows2(s, last_users):
                pe.wait_ge(s_n[1], s)
                for holder, count in last_users:
                    pe.wait_ge(holder, count)
                transpose(1, s - 1, normed[1])

            def output2(s, j):
                pe.wait_ge(s_yh[1], s * 2 - 2)
                pe.wait_ge(s_yl[1], s * 2 - 2)
                for b in range(2):
                    if within(s, 0, CHUNKS - 1):
                        pe.wait_ge((s_r[0], s_k[0])[b], s * 2 + 1 + b)
                    else:
                        pe.wait_ge((s_kv[1], s_r[1])[b], s * 2 - 2)
                    output(1, ring[(2 * j + 6 + b) % 4][:, :], 2 * b)

            def rows3(s, j, last_user, count):
                pe.wait_ge(s_x1, s - 2)
                pe.wait_ge(last_user, count)
                transpose(2, s - 3, x1[:, 1 - j, :, :])

            def gates(s, last_user, count):
                pe.wait_ge(s_x1T, s * 2 - 4)
                pe.wait_ge(last_user, count)
                for q in range(Q):
                    for dc in range(DC):
                        last = nc.tensor.matmul(out1[0][:, 0, q * E:(q + 1) * E], x1T[:, dc, q * P:(q + 1) * P],
                                                wg[:, dc, :], start=dc == 0, stop=dc == DC - 1)
                last.then_inc(s_g, 1)

            bias_products(0)
            pe.wait_ge(s_ident, 1)
            pe.wait_ge(s_n[0], 1)
            transpose(0, 0, normed[0])
            pe.wait_ge(s_whi[0], DC + 1)
            pe.wait_ge(s_wlo[0], DC + 1)

            def step(s, half, j):
                layer1, layer2 = within(s, 0, CHUNKS - 1), within(s, 1, CHUNKS)
                if layer1:
                    for e in range(DC):
                        project(0, s, s, e, j)
                if at(s, 0):
                    pe.wait_ge(s_n[0], 2)
                    pe.wait_ge(s_xl[0], 2)
                    transpose(0, 1, normed[0])
                    bias_products(1)
                    pe.wait_ge(s_before, 1)
                    pe.wait_ge(s_ones, 1)
                if at(s, 1):
                    pe.wait_ge(s_whi[1], DC + 1)
                    pe.wait_ge(s_wlo[1], DC + 1)
                if at(s, CHUNKS):
                    output2(s, j)
                    rows3(s, j, s_xl[0], 2 * s)
                    rows2(s, ((s_x1T, s * 2 - 4),))
                    project(1, s, s - 1, 0, j)
                    gates(s, s_res, s * 2)
                elif at(s, CHUNKS + 1):
                    rows3(s, j, s_xl[1], 2 * s - 2)
                    gates(s, s_slot, s - 3)
                    output2(s, j)
                elif at(s, CHUNKS + 2):
                    rows3(s, j, s_x1T, 2 * s - 6)
                    gates(s, s_slot, s - 3)
                else:
                    if layer2:
                        rows2(s, ((s_xl[0], s * 2 + 2),))
                    if within(s, 2, CHUNKS):
                        output2(s, j)
                    if within(s, 3, CHUNKS):
                        rows3(s, j, s_xl[1], s * 2)
                    if layer2:
                        project(1, s, s - 1, 0, j)
                    if at(s, 3):
                        pe.wait_ge(s_wg, 16)
                    if within(s, 3, CHUNKS):
                        gates(s, s_res, s * 2)
                if within(s, 1, CHUNKS - 2):
                    pe.wait_ge(s_n[0], s + 2)
                    if within(s, 1, 2) and isinstance(s, int):
                        pe.wait_ge(s_xl[1], 2 * s)
                    else:
                        pe.wait_ge(s_x1T, s * 2 - 4)
                    transpose(0, s + 1, normed[0])
                if layer2:
                    project(1, s, s - 1, 1, j, (0, 1))
                if within(s, 3, CHUNKS + 2):
                    pe.wait_ge(s_picked, s - 2)
                    ranks = out1[0][:, 0, RANK_AT:RANK_AT + Q * E]
                    flat = picked[:, :, :].rearrange("p q e -> p (q e)")
                    nc.tensor.matmul(ranks, before[:, :], flat, start=True, stop=False)
                    for d in range(1, Q):
                        nc.tensor.matmul(ranks[:, d * E:Q * E], ones[:, :], flat[:, 0:(Q - d) * E], start=False, stop=d == Q - 1)
                    for q in range(Q):
                        last = nc.tensor.matmul(out1[0][:, 0, RANK_AT + Q * E:RANK_AT + Q * E + E], ones[:, :],
                                                picked[:, q, :], start=q == 0, stop=q == Q - 1)
                    last.then_inc(s_rank, 1)
                if layer2:
                    project(1, s, s - 1, 1, j, (2,))
                if layer1:
                    pe.wait_ge(s_yh[0], s * 2 + 2)
                    pe.wait_ge(s_yl[0], s * 2 + 2)
                    if within(s, 1, CHUNKS):
                        pe.wait_ge(s_res, s * 2)
                    else:
                        pe.wait_ge(s_biassb[0], 2)
                        pe.wait_ge(s_biassb[1], 2)
                    output(0, out1[1][:, :, :].rearrange("p q d -> p (q d)"), 2)
                    if within(s, 3, CHUNKS):
                        pe.wait_ge(s_slot, s - 2)
                    output(0, out1[0][:, :, :].rearrange("p q d -> p (q d)"), 0)

            run(pe, step)


def expert_phase(nc, w_ffn, x_src, x_acc, slot_list, ident, w_raw_all, table, s_w):
    with ExitStack() as ctx:
        def sb(name, shape, dt=F32):
            return ctx.enter_context(nc.sbuf_tensor(name, shape, dt))

        def sem(name):
            return ctx.enter_context(nc.semaphore(name))

        ring = [ctx.enter_context(nc.psum_tensor(f"fring{i}", [P, CH], F32)) for i in range(4)]
        tp = [ctx.enter_context(nc.psum_tensor(f"ftp{i}", [P, CH], F32)) for i in range(DC)]
        yp = [ctx.enter_context(nc.psum_tensor(f"fy{i}", [P, 2, D], F32)) for i in range(2)]

        w_raw = w_raw_all[:, :].rearrange("p (j c) -> p j c", j=2)
        w_hi = sb("fw_hi", [P, 2, WCOLS], F32R)
        w_lo = sb("fw_lo", [P, 2, WCOLS], F32R)
        pair_in = [sb(f"pair_in{i}", [P, Q, 2], I32) for i in range(2)]
        pair_out = [sb(f"pair_out{i}", [P, Q, 2], I32) for i in range(2)]
        xg = [sb(f"xg{i}", [P, Q, D]) for i in range(2)]
        xh = sb("fxh", [P, DC, CH], F32R)
        xl = sb("fxl", [P, DC, CH], F32R)
        silu = sb("silu", [P, 2, CH])
        gated = sb("gated", [P, 2, CH])
        gh = sb("gh", [P, 2, HC, CH], F32R)
        gl = sb("gl", [P, 2, HC, CH], F32R)
        y = [sb(f"fy_sb{i}", [P, Q, D]) for i in range(2)]

        s_met = sem("fwaits_met")
        s_pair = [sem("pairs_loaded0"), sem("pairs_loaded1")]
        s_xg = [sem("rows_gathered0"), sem("rows_gathered1")]
        s_keep = sem("pairs_kept")
        s_add = [sem("rows_added0"), sem("rows_added1")]
        s_pt, s_xh, s_xl = sem("ftransposed"), sem("fxh_ready"), sem("fxl_ready")
        s_h, s_silu, s_g, s_gh, s_gl = sem("h_product"), sem("silu_ready"), sem("gated_ready"), sem("gh_ready"), sem("gl_ready")
        s_y, s_yv = sem("y_product"), sem("y_weighted")
        s_whi = [sem(f"whi_ready{i}") for i in range(3)]
        s_wlo = [sem(f"wlo_ready{i}") for i in range(3)]
        part = [(0, DC * H), (DC * H, 2 * DC * H), (2 * DC * H, WCOLS)]

        block = ctx.enter_context(nc.Block())

        def run(eng, step):
            for s in range(-1, 2):
                step(s, s // 2, s % 2)
            with eng.Fori(1, (BLOCKS - 2) // 2) as it:
                step(it * 2, it, 0)
                step(it * 2 + 1, it, 1)
            for s in range((BLOCKS - 2) // 2 * 2, BLOCKS + 2):
                step(s, s // 2, s % 2)

        @block.sync
        def _(sp):
            def load(b, half, j):
                column = slice(b, b + 1) if isinstance(b, int) else bass.ds(b, 1)
                slot_row = sp.value_load(table[0:1, 1, column], min_val=0, max_val=SLOTS - CH)
                if within(b, 2, BLOCKS):
                    w_row = sp.value_load(table[0:1, 0, column], min_val=0, max_val=(E - 1) * P)
                if within(b, 2, BLOCKS):
                    sp.wait_ge(s_keep, b - 1)
                sp.dma_start(pair_in[j][:, :, :], slot_list[bass.ds(slot_row, CH), :]
                             .rearrange("(p q) c -> p q c", p=P)).then_inc(s_pair[j], 16)
                if within(b, 2, BLOCKS):
                    sp.wait_ge(s_whi[2], b - 1)
                    sp.wait_ge(s_wlo[2], b - 1)
                    sp.wait_ge(s_wlo[0], b - 1)
                    sp.wait_ge(s_wlo[1], b - 1)
                    sp.dma_start(w_raw[:, j, :], w_ffn[bass.ds(w_row, P), :]).then_inc(s_w[j], 16)

            def step(s, half, j):
                if at(s, -1):
                    load(0, 0, 0)
                    load(1, 0, 1)
                elif within(s, 0, BLOCKS - 3):
                    load(s + 2, half + 1, j)

            run(sp, step)
            for par in range(2):
                sp.wait_ge(s_add[par], 16 * Q * ((BLOCKS + 1 - par) // 2))

        @block.gpsimd
        def _(pool):
            def gather(b, half, j):
                pool.wait_ge(s_pair[j], half * 16 + 16)
                if within(b, 2, BLOCKS):
                    pool.wait_ge(s_pt, b * 2 - 2)
                pool.sem_inc(s_met, 1)
                for q in range(Q):
                    nc.gpsimd.indirect_dma_start(
                        xg[j][:, q, :], None, x_src,
                        bass.IndirectOffsetOnAxis(pair_in[j][:, q, 0:1].bitcast(U32), 0)).then_inc(s_xg[j], 16)

            def step(s, half, j):
                if within(s, -1, BLOCKS - 2):
                    gather(s + 1, half + j, 1 - j)
                if within(s, 2, BLOCKS + 1):
                    if within(s, 3, BLOCKS + 1):
                        pool.wait_ge(s_add[1 - j], (half - 1 + j) * (16 * Q))
                    pool.wait_ge(s_yv, s * Q - Q)
                    pool.sem_inc(s_met, 1)
                    for q in range(Q):
                        nc.gpsimd.indirect_dma_start(
                            x_acc, bass.IndirectOffsetOnAxis(pair_out[j][:, q, 0:1].bitcast(U32), 0),
                            y[j][:, q, :], None, compute_op=ALU.add).then_inc(s_add[j], 16)
                if within(s, 0, BLOCKS - 2):
                    low, high = part[0]
                    pool.wait_ge(s_whi[0], s + 2)
                    nc.gpsimd.tensor_tensor(w_lo[:, 1 - j, low:high], w_raw[:, 1 - j, low:high],
                                            w_hi[:, 1 - j, low:high].bitcast(F32), ALU.subtract).then_inc(s_wlo[0], 1)

            run(pool, step)

        @block.scalar
        def _(act):
            def w_half(i, b, half, j):
                low, high = part[i]
                act.wait_ge(s_w[j], half * 16 + 16)
                if within(b, 2, BLOCKS):
                    if i < 2:
                        act.wait_ge(s_h, b * (2 * HC) - 2 * HC)
                    else:
                        act.wait_ge(s_y, b * 2 - 2)
                nc.scalar.activation(w_hi[:, j, low:high], w_raw[:, j, low:high], ACT.Copy).then_inc(s_whi[i], 1)

            def act_silu(b, j, hb):
                act.wait_ge(s_h, b * (2 * HC) + 2 * hb + 1)
                if hb >= 2:
                    act.wait_ge(s_g, b * HC + hb - 1)
                elif within(b, 1, BLOCKS):
                    act.wait_ge(s_g, b * HC + hb - 1)
                nc.scalar.activation(silu[:, hb % 2, :], ring[2 * (hb % 2)][:, :], ACT.Silu).then_inc(s_silu, 1)

            def g_hi(b, j, hb):
                act.wait_ge(s_g, b * HC + hb + 1)
                if within(b, 2, BLOCKS):
                    act.wait_ge(s_y, b * 2 - 2)
                nc.scalar.activation(gh[:, j, hb, :], gated[:, hb % 2, :], ACT.Copy).then_inc(s_gh, 1)

            def x_hi(b):
                for dc in range(DC):
                    act.wait_ge(s_pt, b * 2 + dc + 1)
                    nc.scalar.activation(xh[:, dc, :], tp[dc][:, :], ACT.Copy).then_inc(s_xh, 1)

            def step(s, half, j):
                here, nxt = within(s, 0, BLOCKS - 1), within(s, -1, BLOCKS - 2)
                if here:
                    act_silu(s, j, 0)
                if nxt:
                    w_half(0, s + 1, half + j, 1 - j)
                if here:
                    act_silu(s, j, 1)
                    g_hi(s, j, 0)
                    w_half(2, s, half, j)
                    act_silu(s, j, 2)
                    g_hi(s, j, 1)
                if nxt:
                    w_half(1, s + 1, half + j, 1 - j)
                if here:
                    act_silu(s, j, 3)
                    g_hi(s, j, 2)
                if nxt:
                    x_hi(s + 1)
                if here:
                    g_hi(s, j, 3)

            run(act, step)

        @block.vector
        def _(dve):
            def w_low(i, b, half, j):
                low, high = part[i]
                dve.wait_ge(s_whi[i], b + 1)
                nc.vector.tensor_tensor(w_lo[:, j, low:high], w_raw[:, j, low:high],
                                        w_hi[:, j, low:high].bitcast(F32), ALU.subtract).then_inc(s_wlo[i], 1)

            def gate(b, hb):
                dve.wait_ge(s_h, b * (2 * HC) + 2 * hb + 2)
                dve.wait_ge(s_silu, b * HC + hb + 1)
                if hb >= 2 or within(b, 1, BLOCKS):
                    dve.wait_ge(s_gl, b * HC + hb - 1)
                nc.vector.tensor_tensor(gated[:, hb % 2, :], ring[2 * (hb % 2) + 1][:, :], silu[:, hb % 2, :],
                                        ALU.mult).then_inc(s_g, 1)

            def g_lo(b, j, hb):
                dve.wait_ge(s_gh, b * HC + hb + 1)
                nc.vector.tensor_tensor(gl[:, j, hb, :], gated[:, hb % 2, :], gh[:, j, hb, :].bitcast(F32),
                                        ALU.subtract).then_inc(s_gl, 1)

            def x_lo(b):
                for dc in range(DC):
                    dve.wait_ge(s_xh, b * 2 + dc + 1)
                    nc.vector.tensor_tensor(xl[:, dc, :], tp[dc][:, :], xh[:, dc, :].bitcast(F32),
                                            ALU.subtract).then_inc(s_xl, 1)

            def keep(b, half, j):
                dve.wait_ge(s_pair[j], half * 16 + 16)
                dve.wait_ge(s_xg[j], (half + 1) * (16 * Q))
                if within(b, 2, BLOCKS):
                    dve.wait_ge(s_add[j], half * (16 * Q))
                nc.vector.tensor_copy(pair_out[j][:, :, :], pair_in[j][:, :, :]).then_inc(s_keep, 1)

            def weigh(b, half, j):
                dve.wait_ge(s_keep, b + 1)
                if within(b, 2, BLOCKS):
                    dve.wait_ge(s_add[j], half * (16 * Q))
                for q in range(Q):
                    dve.wait_ge(s_y, b * 2 + q // 2 + 1)
                    nc.vector.tensor_scalar(y[j][:, q, :], yp[q // 2][:, q % 2, :], pair_out[j][:, q, 1:2].bitcast(F32),
                                            None, ALU.mult).then_inc(s_yv, 1)

            def step(s, half, j):
                here, nxt = within(s, 0, BLOCKS - 1), within(s, -1, BLOCKS - 2)
                if here:
                    gate(s, 0)
                    gate(s, 1)
                    g_lo(s, j, 0)
                    w_low(2, s, half, j)
                    gate(s, 2)
                    g_lo(s, j, 1)
                if at(s, -1):
                    w_low(0, 0, 0, 0)
                if nxt:
                    w_low(1, s + 1, half + j, 1 - j)
                if here:
                    gate(s, 3)
                    g_lo(s, j, 2)
                    keep(s, half, j)
                if nxt:
                    x_lo(s + 1)
                if here:
                    g_lo(s, j, 3)
                if within(s, 1, BLOCKS):
                    weigh(s - 1, half - 1 + j, 1 - j)

            run(dve, step)

        @block.tensor
        def _(pe):
            def hidden(b, j, hb):
                for i in range(2):
                    if hb >= 2 or within(b, 1, BLOCKS):
                        if i == 0:
                            pe.wait_ge(s_silu, b * HC + hb - 1)
                        else:
                            pe.wait_ge(s_g, b * HC + hb - 1)
                    out = ring[2 * (hb % 2) + i][:, :]
                    for dc in range(DC):
                        col = part[i][0] + dc * H + hb * P
                        hi, lo = w_hi[:, j, col:col + P], w_lo[:, j, col:col + P]
                        nc.tensor.matmul(out, hi, xh[:, dc, :], start=dc == 0, stop=False)
                        nc.tensor.matmul(out, hi, xl[:, dc, :], start=False, stop=False)
                        last = nc.tensor.matmul(out, lo, xh[:, dc, :], start=False, stop=dc == DC - 1)
                    last.then_inc(s_h, 1)

            def step(s, half, j):
                if within(s, 0, BLOCKS - 1):
                    pe.wait_ge(s_xh, s * 2 + 2)
                    pe.wait_ge(s_xl, s * 2 + 2)
                    for i in range(2):
                        pe.wait_ge(s_whi[i], s + 1)
                        pe.wait_ge(s_wlo[i], s + 1)
                    for hb in range(HC):
                        hidden(s, j, hb)
                if within(s, -1, BLOCKS - 2):
                    pe.wait_ge(s_xg[1 - j], (half + 1 + j) * (16 * Q))
                    if within(s, 0, BLOCKS):
                        pe.wait_ge(s_xl, s * 2 + 2)
                    for dc in range(DC):
                        for q in range(Q):
                            last = nc.tensor.transpose(tp[dc][:, q * P:(q + 1) * P], xg[1 - j][:, q, dc * P:(dc + 1) * P],
                                                       ident[:, :])
                        last.then_inc(s_pt, 1)
                if within(s, 1, BLOCKS):
                    b = s - 1
                    pe.wait_ge(s_gh, b * HC + HC)
                    pe.wait_ge(s_gl, b * HC + HC)
                    pe.wait_ge(s_whi[2], b + 1)
                    pe.wait_ge(s_wlo[2], b + 1)
                    for q in range(Q):
                        if within(s, 2, BLOCKS):
                            pe.wait_ge(s_yv, b * Q - 2 + 2 * (q // 2))
                        out = yp[q // 2][:, q % 2, :]
                        for hc in range(HC):
                            col = part[2][0] + hc * D
                            hi, lo = w_hi[:, 1 - j, col:col + D], w_lo[:, 1 - j, col:col + D]
                            a, c = gh[:, 1 - j, hc, q * P:(q + 1) * P], gl[:, 1 - j, hc, q * P:(q + 1) * P]
                            nc.tensor.matmul(out, a, hi, start=hc == 0, stop=False)
                            nc.tensor.matmul(out, a, lo, start=False, stop=False)
                            last = nc.tensor.matmul(out, c, hi, start=False, stop=hc == HC - 1)
                        if q % 2:
                            last.then_inc(s_y, 1)

            run(pe, step)


def norm_phase(nc, x_acc, out):
    DEPTH = 4
    with ExitStack() as ctx:
        def sb(name, shape, dt=F32):
            return ctx.enter_context(nc.sbuf_tensor(name, shape, dt))

        def sem(name):
            return ctx.enter_context(nc.semaphore(name))

        a = [sb(f"acc{i}", [P, Q, D]) for i in range(DEPTH)]
        o = [sb(f"o{i}", [P, Q, D]) for i in range(DEPTH)]
        stats = sb("nstats", [P, DEPTH, Q, 6])
        mv = sb("nmv", [P, DEPTH, Q, 2])
        ve = sb("nve", [P, DEPTH, Q])
        rs = sb("nrs", [P, DEPTH, Q])
        neg_half = sb("nneg_half", [P, Q])
        s_in = [sem(f"acc_loaded{i}") for i in range(DEPTH)]
        s_out = [sem(f"out_stored{i}") for i in range(DEPTH)]
        s_half, s_bn, s_mv, s_ve, s_rs, s_o = (sem("nneg_half_ready"), sem("nstats_ready"), sem("nmean_var"),
                                               sem("nvar_eps"), sem("nrstd"), sem("normed_rows"))
        s_met = sem("nwaits_met")
        block = ctx.enter_context(nc.Block())

        def run(eng, step, first):
            for n in range(DEPTH):
                step(n, 0, n)
            with eng.Fori(1, CHUNKS // DEPTH) as it:
                for j in range(DEPTH):
                    step(it * DEPTH + j, it, j)

        @block.sync
        def _(sp):
            def step(n, turn, j):
                row = n * CH if isinstance(n, int) else sp.snap(n * CH)
                if within(n, DEPTH, CHUNKS):
                    sp.wait_ge(s_o, n - DEPTH + 1)
                sp.dma_start(a[j][:, :, :], x_acc[bass.ds(row, CH), :]
                             .rearrange("(p q) d -> p q d", p=P)).then_inc(s_in[j], 16)

            run(sp, step, 0)

        @block.scalar
        def _(act):
            def step(n, turn, j):
                row = n * P if isinstance(n, int) else act.snap(n * P)
                act.wait_ge(s_o, n + 1)
                act.dma_start(out[bass.ds(row, P), :], o[j][:, :, :].rearrange("p q d -> p (q d)")).then_inc(s_out[j], 16)

            run(act, step, 0)
            for j in range(DEPTH):
                act.wait_ge(s_out[j], 16 * (CHUNKS // DEPTH))

        @block.gpsimd
        def _(pool):
            pool.wait_ge(s_half, 1)

            def step(n, turn, j):
                pool.wait_ge(s_ve, n + 1)
                nc.gpsimd.tensor_tensor(rs[:, j, :], ve[:, j, :], neg_half[:, :], ALU.pow).then_inc(s_rs, 1)

            run(pool, step, 0)

        @block.vector
        def _(dve):
            nc.vector.memset(neg_half[:, :], -0.5).then_inc(s_half, 1)

            def stat(n, turn, j):
                dve.wait_ge(s_in[j], turn * 16 + 16)
                for q in range(Q):
                    nc.vector.bn_stats(stats[:, j, q, :], a[j][:, q, :]).then_inc(s_bn, 1)
                dve.wait_ge(s_bn, n * Q + Q)
                dve.sem_inc(s_met, 1)
                for q in range(Q):
                    nc.vector.bn_aggr(mv[:, j, q, :], stats[:, j, q, :]).then_inc(s_mv, 1)
                dve.wait_ge(s_mv, n * Q + Q)
                nc.vector.tensor_scalar(ve[:, j, :], mv[:, j, :, 1], EPS, None, ALU.add).then_inc(s_ve, 1)

            def scale(n, turn, j):
                dve.wait_ge(s_rs, n + 1)
                if within(n, DEPTH, CHUNKS):
                    dve.wait_ge(s_out[j], turn * 16)
                for q in range(Q):
                    last = nc.vector.tensor_scalar(o[j][:, q, :], a[j][:, q, :], mv[:, j, q, 0:1], rs[:, j, q:q + 1],
                                                   ALU.subtract, ALU.mult)
                last.then_inc(s_o, 1)

            stat(0, 0, 0)
            for n in range(1, DEPTH):
                stat(n, 0, n)
                scale(n - 1, 0, n - 1)
            stat(DEPTH, 1, 0)
            scale(DEPTH - 1, 0, DEPTH - 1)
            with dve.Fori(1, CHUNKS // DEPTH - 1) as it:
                for j in range(DEPTH):
                    if j < DEPTH - 1:
                        stat(it * DEPTH + j + 1, it, j + 1)
                    else:
                        stat(it * DEPTH + DEPTH, it + 1, 0)
                    scale(it * DEPTH + j, it, j)
            last = CHUNKS // DEPTH - 1
            for j in range(DEPTH):
                if j < DEPTH - 1:
                    stat(last * DEPTH + j + 1, last, j + 1)
                scale(last * DEPTH + j, last, j)


def build(nc, h, w_att, ln_wb, w_gate, w_ffn, out):
    x_src = nc.dram_tensor("x_src", (TOKENS + CH, D), F32).ap()
    x_acc = nc.dram_tensor("x_acc", (TOKENS + CH, D), F32).ap()
    slot_list = nc.dram_tensor("slot_list", (SLOTS, 2), I32).ap()
    with (nc.sbuf_tensor("ident", [P, P], F32) as ident,
          nc.sbuf_tensor("w_raw", [P, 2 * WCOLS], F32) as w_raw,
          nc.sbuf_tensor("table", [1, 2, BLOCKS], I32) as table,
          nc.semaphore("fw_loaded0") as s_fw0, nc.semaphore("fw_loaded1") as s_fw1):
        attention_phase(nc, h, w_att, ln_wb, w_gate, w_ffn, x_src, x_acc, slot_list, ident, w_raw, table, (s_fw0, s_fw1))
        expert_phase(nc, w_ffn, x_src, x_acc, slot_list, ident, w_raw, table, (s_fw0, s_fw1))
        norm_phase(nc, x_acc, out)


def kernel(L0_attn_h, L0_attn_ln_w, L0_attn_ln_b, L0_attn_Wk, L0_attn_Wv, L0_attn_Wr, L0_attn_Wo,
           L0_ffn_Wg, L0_ffn_W1, L0_ffn_W2, L0_ffn_W3):
    import concourse.bacc as bacc
    import numpy as np
    from concourse.bass_utils import run_bass_kernel_spmd

    def by_partition(a, rows):
        a = np.asarray(a)
        a = a.reshape(a.shape[:-2] + (rows // P, P, a.shape[-1]))
        return np.ascontiguousarray(np.moveaxis(a, -2, 0))

    PIECES = T // CH
    x = np.asarray(L0_attn_h).reshape(B, PIECES, Q, P, D).transpose(1, 0, 3, 2, 4).reshape(CHUNKS * P, Q * D)
    att = np.concatenate([np.asarray(w).transpose(0, 2, 1) for w in (L0_attn_Wk, L0_attn_Wv, L0_attn_Wr, L0_attn_Wo)], axis=2)
    wb = np.stack([np.asarray(L0_attn_ln_w), np.asarray(L0_attn_ln_b)]).reshape(2, LAYERS, DC, P).transpose(3, 0, 1, 2)
    w1, w2, w3 = (by_partition(np.asarray(w).transpose(0, 2, 1), rows).transpose(1, 0, 2, 3).reshape(E * P, -1)
                  for w, rows in ((L0_ffn_W1, D), (L0_ffn_W2, D), (L0_ffn_W3, H)))
    arrays = {
        "h": np.ascontiguousarray(x),
        "w_att": by_partition(att, D),
        "ln_wb": np.ascontiguousarray(wb),
        "w_gate": by_partition(np.asarray(L0_ffn_Wg).T, D),
        "w_ffn": np.ascontiguousarray(np.concatenate([w1, w2, w3], axis=1)),
    }
    nc = bacc.Bacc("TRN2", target_bir_lowering=False, num_devices=1)
    args = [nc.dram_tensor(name, a.shape, F32, kind="ExternalInput").ap() for name, a in arrays.items()]
    out = nc.dram_tensor("out", (CHUNKS * P, Q * D), F32, kind="ExternalOutput").ap()
    build(nc, *args, out)
    result = run_bass_kernel_spmd(nc, [arrays], core_ids=[0]).results[0]["out"]
    return result.reshape(PIECES, B, P, Q, D).transpose(1, 0, 3, 2, 4).reshape(B, T, D)
```

```python
from contextlib import ExitStack

import concourse.bass as bass
from concourse import mybir

P = 128
ALU = mybir.AluOpType
ACT = mybir.ActivationFunctionType
F32 = mybir.dt.float32
F32R = mybir.dt.float32r
BF16 = mybir.dt.bfloat16
I32 = mybir.dt.int32
U32 = mybir.dt.uint32
AX_X = mybir.AxisListType.X

B, T, D = 4, 2048, 256
LAYERS = 2
E, H = 8, 512
DECAY, EPS = 0.95, 1e-5
CH = 512
Q = CH // P
DC = D // P
HC = H // P
TOKENS = B * T
CHUNKS = TOKENS // CH
LIST = TOKENS
SLOTS = E * LIST + CH
SMALL = CH // 2
BIG = (2 * TOKENS - E * (CH - 1)) // CH // 2 * 2
BLOCKS = BIG + (2 * TOKENS - E) // SMALL + E - BIG * (CH // SMALL)
WCOLS = 2 * DC * H + HC * D
PART = ((0, DC * H), (DC * H, 2 * DC * H), (2 * DC * H, WCOLS))
SCAT = 16 * 2 * Q
RANK_AT = 64


def within(s, low, high):
    return not isinstance(s, int) or low <= s <= high


def at(s, n):
    return isinstance(s, int) and s == n


def attention_phase(nc, h, w_att, ln_wb, w_gate, w_ffn, x_src, x_acc, slot_list, ident, w_raw_all, table, s_fw):
    with ExitStack() as ctx:
        def sb(name, shape, dt=F32):
            return ctx.enter_context(nc.sbuf_tensor(name, shape, dt))

        def sem(name):
            return ctx.enter_context(nc.semaphore(name))

        ring = [ctx.enter_context(nc.psum_tensor(f"ring{i}", [P, CH], F32)) for i in range(4)]
        tp = [ctx.enter_context(nc.psum_tensor(f"tp{i}", [P, CH], F32)) for i in range(DC)]
        out1 = [ctx.enter_context(nc.psum_tensor(f"out1_{i}", [P, 2, D], F32)) for i in range(2)]

        before = sb("before", [P, P], BF16)
        ones = sb("ones", [P, P], BF16)
        decay = sb("decay", [P, CH])
        neg_half = sb("neg_half", [P, Q])
        warm = sb("warm", [P, Q])
        expert_no = sb("expert_no", [P, 2, Q, E])
        w_raw = w_raw_all[:, 0:LAYERS * DC * 4 * D].rearrange("p (l c m) -> p l c m", l=LAYERS, c=DC)
        w_hi = sb("w_hi", [P, LAYERS, DC, 4 * D], F32R)
        w_lo = sb("w_lo", [P, LAYERS, DC, 4 * D], F32R)
        lnp = sb("lnp", [P, 2, LAYERS, DC])
        wg = sb("wg", [P, DC, E])
        bias = sb("bias", [P, LAYERS, 3, DC])
        x_in = sb("x_in", [P, 2, Q, D])
        normed = [sb(f"normed{l}", [P, Q, D]) for l in range(2)]
        xh = [sb(f"xh{l}", [P, DC, CH], F32R) for l in range(2)]
        xl = [sb(f"xl{l}", [P, DC, CH], F32R) for l in range(2)]
        k_sb = sb("k_sb", [P, DC, CH])
        kv = sb("kv", [P, DC, CH])
        state = [sb(f"state{l}", [P, DC, CH]) for l in range(2)]
        r_sb = [sb(f"r_sb{l}", [P, DC, CH]) for l in range(2)]
        y = [sb(f"y{l}", [P, DC, CH]) for l in range(2)]
        yh = [sb(f"yh{l}", [P, DC, CH], F32R) for l in range(2)]
        yl = [sb(f"yl{l}", [P, DC, CH], F32R) for l in range(2)]
        carry = sb("carry", [P, LAYERS, DC, CHUNKS + B])
        xr = sb("xr", [P, Q, D])
        u = sb("u", [P, 2, Q, D])
        z = sb("z", [P, Q, D])
        x1 = sb("x1", [P, 2, Q, D])
        x1T = sb("x1T", [P, DC, CH])
        stats = [sb(f"stats{i}", [P, Q, 6]) for i in range(3)]
        mv = [sb(f"mv{i}", [P, Q, 2]) for i in range(3)]
        ve = [sb(f"ve{i}", [P, Q]) for i in range(3)]
        nm = [sb(f"nm{i}", [P, Q]) for i in range(3)]
        rs = [sb(f"rs{i}", [P, Q]) for i in range(3)]
        nb = [sb(f"nb{i}", [P, Q]) for i in range(3)]
        g = sb("g", [P, Q, E])
        top = sb("top", [P, Q, E])
        pick = sb("pick", [P, Q, E], U32)
        pick_f = sb("pick_f", [P, 2, Q])
        sel = sb("sel", [P, 2, Q, E])
        picked = sb("picked", [P, Q, E], BF16)
        gap = sb("gap", [P, Q])
        slot = sb("slot", [P, Q, E])
        base = sb("base", [P, E])
        own = sb("own", [P, 2, Q, E])
        slot_f = sb("slot_f", [P, 2, Q])
        slot_u = [sb(f"slot_u{i}", [P, Q, 2], U32) for i in range(2)]
        pairs = [sb(f"pairs{i}", [P, Q, 2, 2]) for i in range(2)]
        pad = sb("pad", [P, SLOTS // P, 2], I32)
        block_no = sb("block_no", [1, BLOCKS])
        start = sb("start", [1, E])
        used = sb("used", [1, E])
        used_i = sb("used_i", [1, E], I32)
        one_row = sb("one_row", [1, E])
        full = sb("full", [1, E])
        before_e = sb("before_e", [1, E])
        taken = sb("taken", [1, E + 1])
        end = sb("end", [1, 2, E])
        skip = sb("skip", [1, 2, E])
        past = sb("past", [1, BLOCKS, E])
        hop = sb("hop", [1, BLOCKS, E])
        rows = sb("rows", [1, 2, BLOCKS])

        s_blank, s_ident, s_before, s_expert_no = (sem("blanks_ready"), sem("identity_ready"), sem("before_ready"),
                                                  sem("expert_no_ready"))
        s_base, s_half, s_ones, s_decay, s_zeros = (sem("base_ready"), sem("neg_half_ready"), sem("ones_ready"),
                                                    sem("decay_ready"), sem("zeros_ready"))
        s_w = [sem("weights_loaded0"), sem("weights_loaded1")]
        s_lnp, s_wg, s_pad, s_padst = sem("ln_loaded"), sem("gate_loaded"), sem("pad_ready"), sem("pad_stored")
        s_bias = sem("bias_products")
        s_biassb = [sem("bias_ready0"), sem("bias_ready1")]
        s_whi = [sem("weights_hi0"), sem("weights_hi1")]
        s_wlo = [sem("weights_lo0"), sem("weights_lo1")]
        s_x = [sem("x_loaded0"), sem("x_loaded1")]
        s_bn = [sem(f"tile_stats{i}") for i in range(3)]
        s_mv = [sem(f"mean_var{i}") for i in range(3)]
        s_ve = [sem(f"var_eps{i}") for i in range(3)]
        s_rs = [sem(f"rstd{i}") for i in range(3)]
        s_nb = [sem(f"norm_bias{i}") for i in range(3)]
        s_n = [sem("normed_0"), sem("normed_1")]
        s_pt = [sem(f"transposed{i}") for i in range(3)]
        s_xh = [sem("xh_ready0"), sem("xh_ready1")]
        s_xl = [sem("xl_ready0"), sem("xl_ready1")]
        s_pg = [sem("projected0"), sem("projected1")]
        s_k = [sem("k_ready0"), sem("k_ready1")]
        s_kv = [sem("kv_ready0"), sem("kv_ready1")]
        s_r = [sem("r_ready0"), sem("r_ready1")]
        s_sn = [sem("scanned0"), sem("scanned1")]
        s_cy = [sem("carried0"), sem("carried1")]
        s_y = [sem("y_ready0"), sem("y_ready1")]
        s_yh = [sem("yh_ready0"), sem("yh_ready1")]
        s_yl = [sem("yl_ready0"), sem("yl_ready1")]
        s_po = [sem("out_product0"), sem("out_product1")]
        s_res, s_u, s_z, s_x1 = sem("residual_ready"), sem("u_ready"), sem("z_ready"), sem("x1_ready")
        s_st = [sem("x1_stored0"), sem("x1_stored1")]
        s_x1T, s_g, s_rt, s_gap, s_prob = sem("x1T_ready"), sem("gates"), sem("router_steps"), sem("gap_ready"), sem("probs_ready")
        s_top = sem("gates_ranked")
        s_picked, s_rank, s_slot = sem("picked_ready"), sem("rank_product"), sem("slots_ready")
        s_ids = sem("ids_ready")
        s_sc = [sem("scattered0"), sem("scattered1")]
        s_tab, s_table = sem("table_steps"), sem("table_ready")
        s_met = sem("waits_met")

        block = ctx.enter_context(nc.Block())

        ROUTER = 6
        LAST = CHUNKS + 4

        def run(eng, step):
            for s in range(6):
                step(s, s // 2, s % 2)
            with eng.Fori(3, CHUNKS // 2 - 1) as it:
                step(it * 2, it, 0)
                step(it * 2 + 1, it, 1)
            for s in range(CHUNKS - 2, LAST):
                step(s, s // 2, s % 2)

        def bank(l, e, m, j):
            return ring[(2 * j + 8 * l + 3 * e + m) % 4][:, :]

        def gated(eng, l, n, e):
            eng.wait_ge(s_sn[l], n * 2 + e + 1)
            eng.wait_ge(s_r[l], n * 2 + e + 1)
            if within(n, 1, CHUNKS):
                eng.wait_ge(s_yh[l], n * 2 + e - 1)
                eng.wait_ge(s_yl[l], n * 2 + e - 1)
            eng.tensor_tensor(y[l][:, e, :], state[l][:, e, :], r_sb[l][:, e, :], ALU.mult).then_inc(s_y[l], 1)

        def y_lo(eng, l, n, e):
            eng.wait_ge(s_y[l], n * 2 + e + 1)
            eng.wait_ge(s_yh[l], n * 2 + e + 1)
            if within(n, 1, CHUNKS):
                eng.wait_ge(s_po[l], n * 2)
            eng.tensor_tensor(yl[l][:, e, :], y[l][:, e, :], yh[l][:, e, :].bitcast(F32),
                              ALU.subtract).then_inc(s_yl[l], 1)

        @block.sync
        def _(sp):
            def load(n, par):
                row = n * P if isinstance(n, int) else sp.snap(n * P)
                if within(n, 2, CHUNKS):
                    sp.wait_ge(s_u, n - 1)
                sp.dma_start(x_in[:, par, :, :], h[bass.ds(row, P), :]
                             .rearrange("p (q d) -> p q d", q=Q)).then_inc(s_x[par], 16)

            load(0, 0)
            sp.dma_start(lnp[:, :, :, :], ln_wb).then_inc(s_lnp, 16)
            for l in range(LAYERS):
                sp.dma_start(w_raw[:, l, :, :], w_att[:, l, :, :]).then_inc(s_w[l], 16)
                if l == 0:
                    load(1, 1)
            sp.dma_start(wg[:, :, :], w_gate).then_inc(s_wg, 16)
            sp.wait_ge(s_pad, 2)
            sp.dma_start(slot_list.rearrange("(p n) c -> p n c", p=P), pad[:, :, :]).then_inc(s_padst, 16)
            sp.wait_ge(s_zeros, 1)
            for dst in (x_src, x_acc):
                sp.dma_start(dst[TOKENS:TOKENS + CH, :].rearrange("(p q) d -> p q d", p=P), z[:, :, :]).then_inc(s_padst, 16)

            def step(s, half, j):
                if within(s, 1, CHUNKS - 2):
                    load(s + 1, 1 - j)
                if within(s, 2, CHUNKS + 1):
                    row = (s - 2) * CH if isinstance(s, int) else sp.snap(s * CH - 2 * CH)
                    sp.wait_ge(s_x1, s - 1)
                    for dst in (x_src, x_acc):
                        sp.dma_start(dst[bass.ds(row, CH), :].rearrange("(p q) d -> p q d", p=P),
                                     x1[:, j, :, :]).then_inc(s_st[j], 16)

            run(sp, step)
            sp.wait_ge(s_table, 1)
            for l in range(LAYERS):
                sp.wait_ge(s_bias, l + 1)
                sp.wait_ge(s_whi[l], DC + 1)
                sp.wait_ge(s_wlo[l], DC + 1)
            w_row = sp.value_load(table[0:1, 0, 0:1], min_val=0, max_val=(E - 1) * P)
            for i, (low, high) in enumerate(PART):
                sp.dma_start(w_raw_all[:, low:high], w_ffn[bass.ds(w_row, P), low:high]).then_inc(s_fw[i][0], 16)
            sp.wait_ge(s_wg, 16)
            sp.wait_ge(s_padst, 48)
            for par in range(2):
                sp.wait_ge(s_st[par], 32 * (CHUNKS // 2))
                sp.wait_ge(s_sc[par], SCAT * (CHUNKS // 2))

        @block.scalar
        def _(act):
            act.wait_ge(s_half, 1)
            nc.scalar.activation(warm[:, :], neg_half[:, :], ACT.Sigmoid)

            def split_weights(l):
                act.wait_ge(s_lnp, 16)
                act.wait_ge(s_w[l], 16)
                for dc in range(DC):
                    nc.scalar.activation(w_hi[:, l, dc, 0:3 * D], w_raw[:, l, dc, 0:3 * D], ACT.Copy,
                                         scale=lnp[:, 0, l, dc:dc + 1]).then_inc(s_whi[l], 1)
                nc.scalar.activation(w_hi[:, l, :, 3 * D:4 * D], w_raw[:, l, :, 3 * D:4 * D], ACT.Copy).then_inc(s_whi[l], 1)

            def normalize(i, src, dst, n, done):
                act.wait_ge(s_nb[i], n + 1)
                for q in range(Q):
                    last = nc.scalar.activation(dst[:, q, :], src[:, q, :], ACT.Identity,
                                                bias=nb[i][:, q:q + 1], scale=rs[i][:, q:q + 1])
                last.then_inc(done, 1)

            def x_hi(l, n):
                for dc in range(DC):
                    act.wait_ge(s_pt[l], n * 2 + dc + 1)
                    nc.scalar.activation(xh[l][:, dc, :], tp[dc][:, :], ACT.Copy).then_inc(s_xh[l], 1)

            def keep_k(l, n, e, j, free_sem, free_at):
                act.wait_ge(s_pg[l], n * 6 + 3 * e + 1)
                if free_sem is not None:
                    act.wait_ge(free_sem, free_at)
                nc.scalar.activation(k_sb[:, e, :], bank(l, e, 0, j), ACT.Identity,
                                     bias=bias[:, l, 0, e:e + 1], scale=1.0 - DECAY).then_inc(s_k[l], 1)

            def gate_r(l, n, e, j):
                act.wait_ge(s_pg[l], n * 6 + 3 * e + 3)
                if within(n, 1, CHUNKS):
                    act.wait_ge(s_y[l], n * 2 + e - 1)
                nc.scalar.activation(r_sb[l][:, e, :], bank(l, e, 2, j), ACT.Sigmoid,
                                     bias=bias[:, l, 2, e:e + 1]).then_inc(s_r[l], 1)

            def y_hi(l, n, e):
                act.wait_ge(s_y[l], n * 2 + e + 1)
                if within(n, 1, CHUNKS):
                    act.wait_ge(s_po[l], n * 2)
                nc.scalar.activation(yh[l][:, e, :], y[l][:, e, :], ACT.Copy).then_inc(s_yh[l], 1)

            def keep_x1T(s):
                for dc in range(DC):
                    act.wait_ge(s_pt[2], s * 2 + dc - 5)
                    if within(s, 4, CHUNKS + 2):
                        act.wait_ge(s_g, s - 3)
                    nc.scalar.activation(x1T[:, dc, :], tp[dc][:, :], ACT.Copy).then_inc(s_x1T, 1)

            def normalize3(s, half, j):
                if within(s, 4, CHUNKS + 1):
                    act.wait_ge(s_st[j], half * 32 - 32)
                    act.wait_ge(s_pt[2], s * 2 - 6)
                normalize(2, z, x1[:, j, :, :], s - 2, s_x1)

            normalize(0, x_in[:, 0, :, :], normed[0], 0, s_n[0])
            split_weights(0)
            x_hi(0, 0)
            act.wait_ge(s_pt[0], 2)
            normalize(0, x_in[:, 1, :, :], normed[0], 1, s_n[0])
            act.wait_ge(s_biassb[0], 2)

            def step(s, half, j):
                layer1, layer2 = within(s, 0, CHUNKS - 1), within(s, 1, CHUNKS)
                if layer1:
                    for e in range(DC):
                        if e == 1 and layer2:
                            if within(s, 2, CHUNKS):
                                act.wait_ge(s_pt[1], s * 2 - 2)
                            normalize(1, xr, normed[1], s - 1, s_n[1])
                        if at(s, 0):
                            keep_k(0, s, e, j, None, 0)
                        elif at(s, 1):
                            keep_k(0, s, e, j, s_kv[0], 2)
                        else:
                            keep_k(0, s, e, j, s_kv[1], s * 2 + e - 3)
                        gate_r(0, s, e, j)
                elif layer2:
                    act.wait_ge(s_pt[1], s * 2 - 2)
                    normalize(1, xr, normed[1], s - 1, s_n[1])
                if at(s, 0):
                    x_hi(0, 1)
                if at(s, CHUNKS):
                    keep_x1T(s)
                if layer2:
                    x_hi(1, s - 1)
                if at(s, CHUNKS):
                    normalize3(s, half, j)
                if layer1:
                    for e in range(DC):
                        y_hi(0, s, e)
                if at(s, 0):
                    split_weights(1)
                    act.wait_ge(s_biassb[1], 2)
                if within(s, 3, CHUNKS + 2) and not at(s, CHUNKS) and not at(s, CHUNKS + 1):
                    keep_x1T(s)
                if within(s, 1, CHUNKS - 2):
                    act.wait_ge(s_pt[0], s * 2 + 2)
                    normalize(0, x_in[:, 1 - j, :, :], normed[0], s + 1, s_n[0])
                if layer2:
                    if at(s, CHUNKS):
                        keep_k(1, s - 1, 0, j, s_kv[1], 2 * s - 3)
                    else:
                        keep_k(1, s - 1, 0, j, s_kv[0], s * 2 + 1)
                if within(s, 2, CHUNKS + 1) and not at(s, CHUNKS):
                    normalize3(s, half, j)
                if layer2:
                    gate_r(1, s - 1, 0, j)
                if within(s, 1, CHUNKS - 2):
                    x_hi(0, s + 1)
                if layer2:
                    if at(s, CHUNKS):
                        keep_k(1, s - 1, 1, j, s_kv[1], 2 * s - 2)
                    else:
                        keep_k(1, s - 1, 1, j, s_kv[0], s * 2 + 2)
                    y_hi(1, s - 1, 0)
                if within(s, 3, CHUNKS + 2):
                    act.wait_ge(s_gap, s - 2)
                    if within(s, 5, CHUNKS + 2):
                        act.wait_ge(s_sc[1 - j], (half - 2 + j) * SCAT)
                    nc.scalar.activation(pairs[1 - j][:, :, 0, 1], gap[:, :], ACT.Sigmoid)
                    nc.scalar.activation(pairs[1 - j][:, :, 1, 1], gap[:, :], ACT.Sigmoid, scale=-1.0).then_inc(s_prob, 1)
                if layer2:
                    gate_r(1, s - 1, 1, j)
                    if at(s, CHUNKS):
                        keep_x1T(s + 1)
                    y_hi(1, s - 1, 1)

            run(act, step)

        @block.gpsimd
        def _(pool):
            nc.gpsimd.memset(ident[:, :], 0.0).then_inc(s_blank, 1)
            nc.gpsimd.memset(before[:, :], 0.0).then_inc(s_blank, 1)
            nc.gpsimd.memset(pad[:, :, :], 0).then_inc(s_blank, 1)
            pool.wait_ge(s_blank, 3)
            nc.gpsimd.affine_select(out=ident[:, :], in_=ident[:, :], compare_op=ALU.not_equal, fill=1.0,
                                    base=0, pattern=[[-1, P]], channel_multiplier=1).then_inc(s_ident, 1)
            nc.gpsimd.affine_select(out=before[:, :], in_=before[:, :], compare_op=ALU.is_ge, fill=1.0,
                                    base=0, pattern=[[-1, P]], channel_multiplier=1).then_inc(s_before, 1)
            nc.gpsimd.iota(pad[:, :, 0], [[1, SLOTS // P]], base=0,
                           channel_multiplier=SLOTS // P).then_inc(s_pad, 1)
            nc.gpsimd.iota(expert_no[:, :, :, :], [[0, 2], [0, Q], [1, E]], base=0, channel_multiplier=0,
                           allow_small_or_imprecise_dtypes=True).then_inc(s_expert_no, 1)
            nc.gpsimd.iota(base[:, :], [[LIST, E]], base=0, channel_multiplier=0,
                           allow_small_or_imprecise_dtypes=True).then_inc(s_base, 1)
            for j in range(2):
                nc.gpsimd.iota(pairs[j][:, :, :, 0].bitcast(I32), [[1, Q], [0, 2]], base=CH * j - 2 * CH,
                               channel_multiplier=Q).then_inc(s_ids, 1)

            nc.gpsimd.iota(block_no[:, :], [[1, BLOCKS]], base=0, channel_multiplier=0,
                           allow_small_or_imprecise_dtypes=True).then_inc(s_tab, 1)
            nc.gpsimd.iota(start[:, :], [[LIST, E]], base=0, channel_multiplier=0,
                           allow_small_or_imprecise_dtypes=True).then_inc(s_tab, 1)

            def rstd(i, n):
                pool.wait_ge(s_ve[i], n * 2 + 2)
                if within(n, 1, CHUNKS):
                    pool.wait_ge((s_n[0], s_n[1], s_x1)[i], n)
                nc.gpsimd.tensor_tensor(rs[i][:, :], ve[i][:, :], neg_half[:, :], ALU.pow).then_inc(s_rs[i], 1)
                pool.wait_ge(s_rs[i], n + 1)
                nc.gpsimd.tensor_tensor(nb[i][:, :], rs[i][:, :], nm[i][:, :], ALU.mult).then_inc(s_nb[i], 1)

            def open_scatter(s, half, j):
                if not within(s, 4, CHUNKS + 3):
                    return
                if within(s, 6, CHUNKS + 3):
                    pool.wait_ge(s_sc[j], (half - 2) * SCAT)
                pool.wait_ge(s_ids, s - 2)
                pool.sem_inc(s_met, 1)
                ids = pairs[j][:, :, :, 0].bitcast(I32)
                nc.gpsimd.tensor_scalar(ids, ids, 2 * CH, None, ALU.add).then_inc(s_ids, 1)
                pool.wait_ge(s_ids, s - 1)
                pool.wait_ge(s_prob, s - 3)
                pool.wait_ge(s_slot, s - 3)
                pool.wait_ge(s_padst, 48)
                pool.sem_inc(s_met, 1)

            def scatter(s, j, first, count):
                if not within(s, 4, CHUNKS + 3):
                    return
                for i in range(first, first + count):
                    q, c = i // 2, i % 2
                    nc.gpsimd.indirect_dma_start(
                        slot_list, bass.IndirectOffsetOnAxis(slot_u[j][:, q, c:c + 1], 0),
                        pairs[j][:, q, c, :].bitcast(I32), None).then_inc(s_sc[j], 16)

            pool.wait_ge(s_half, 1)
            rstd(0, 0)
            rstd(0, 1)

            def step(s, half, j):
                layer1, layer2 = within(s, 0, CHUNKS - 1), within(s, 1, CHUNKS)
                if at(s, CHUNKS):
                    rstd(1, s - 1)
                    open_scatter(s, half, j)
                    scatter(s, j, 0, 2)
                    rstd(2, s - 2)
                    scatter(s, j, 2, 6)
                    return
                if at(s, CHUNKS + 1):
                    open_scatter(s, half, j)
                    scatter(s, j, 0, 6)
                    rstd(2, s - 2)
                    scatter(s, j, 6, 2)
                    return
                if layer2:
                    rstd(1, s - 1)
                open_scatter(s, half, j)
                scatter(s, j, 0, 2)
                if layer1:
                    gated(pool, 0, s, 0)
                scatter(s, j, 2, 2)
                if layer1:
                    gated(pool, 0, s, 1)
                    y_lo(pool, 0, s, 0)
                if within(s, 1, CHUNKS - 2):
                    rstd(0, s + 1)
                if layer1:
                    y_lo(pool, 0, s, 1)
                scatter(s, j, 4, 1)
                if within(s, 2, CHUNKS + 1):
                    rstd(2, s - 2)
                scatter(s, j, 5, 1)
                if layer2:
                    gated(pool, 1, s - 1, 0)
                scatter(s, j, 6, 1)
                if layer2:
                    y_lo(pool, 1, s - 1, 0)
                scatter(s, j, 7, 1)
                if layer2:
                    gated(pool, 1, s - 1, 1)
                    y_lo(pool, 1, s - 1, 1)

            run(pool, step)

        @block.vector
        def _(dve):
            nc.vector.memset(neg_half[:, :], -0.5).then_inc(s_half, 1)
            nc.vector.memset(z[:, :, :], 0.0).then_inc(s_zeros, 1)
            nc.vector.memset(decay[:, :], DECAY).then_inc(s_decay, 1)
            nc.vector.memset(ones[:, :], 1.0).then_inc(s_ones, 1)
            nc.vector.memset(one_row[:, :], 1.0).then_inc(s_tab, 1)
            for l in range(LAYERS):
                nc.vector.memset(carry[:, l, :, :], 0.0).then_inc(s_cy[l], 2)

            def norm_stats(i, src, n):
                for q in range(Q):
                    nc.vector.bn_stats(stats[i][:, q, :], src[:, q, :]).then_inc(s_bn[i], 1)
                dve.wait_ge(s_bn[i], n * Q + Q)
                if within(n, 1, CHUNKS):
                    dve.wait_ge(s_nb[i], n)
                dve.sem_inc(s_met, 1)
                for q in range(Q):
                    nc.vector.bn_aggr(mv[i][:, q, :], stats[i][:, q, :]).then_inc(s_mv[i], 1)
                dve.wait_ge(s_mv[i], n * Q + Q)
                nc.vector.tensor_scalar(ve[i][:, :], mv[i][:, :, 1], EPS, None, ALU.add).then_inc(s_ve[i], 1)
                nc.vector.tensor_scalar(nm[i][:, :], mv[i][:, :, 0], -1.0, None, ALU.mult).then_inc(s_ve[i], 1)

            def x_lo(l, n):
                for dc in range(DC):
                    dve.wait_ge(s_xh[l], n * 2 + dc + 1)
                    nc.vector.tensor_tensor(xl[l][:, dc, :], tp[dc][:, :], xh[l][:, dc, :].bitcast(F32),
                                            ALU.subtract).then_inc(s_xl[l], 1)

            def low_weights(l):
                dve.wait_ge(s_lnp, 16)
                dve.wait_ge(s_w[l], 16)
                for dc in range(DC):
                    dve.wait_ge(s_whi[l], dc + 1)
                    nc.vector.scalar_tensor_tensor(w_lo[:, l, dc, 0:3 * D], w_raw[:, l, dc, 0:3 * D],
                                                   lnp[:, 0, l, dc:dc + 1], w_hi[:, l, dc, 0:3 * D].bitcast(F32),
                                                   ALU.mult, ALU.subtract).then_inc(s_wlo[l], 1)
                dve.wait_ge(s_whi[l], DC + 1)
                nc.vector.tensor_tensor(w_lo[:, l, :, 3 * D:4 * D], w_raw[:, l, :, 3 * D:4 * D],
                                        w_hi[:, l, :, 3 * D:4 * D].bitcast(F32), ALU.subtract).then_inc(s_wlo[l], 1)

            def keep_bias(l):
                dve.wait_ge(s_bias, l + 1)
                nc.vector.tensor_copy(bias[:, l, :, :], out1[1][:, 0, l * 3 * DC:(l + 1) * 3 * DC]
                                      .rearrange("p (m e) -> p m e", m=3)).then_inc(s_biassb[l], 1)
                dve.wait_ge(s_biassb[l], 1)
                nc.vector.tensor_scalar(bias[:, l, 0, :], bias[:, l, 0, :], 1.0 - DECAY, None, ALU.mult).then_inc(s_biassb[l], 1)

            dve.wait_ge(s_x[0], 16)
            norm_stats(0, x_in[:, 0, :, :], 0)
            low_weights(0)
            x_lo(0, 0)
            keep_bias(0)
            dve.wait_ge(s_x[1], 16)
            norm_stats(0, x_in[:, 1, :, :], 1)
            dve.wait_ge(s_pad, 1)
            nc.vector.tensor_scalar(pad[:, :, 0], pad[:, :, 0], CH - 1, TOKENS, ALU.bitwise_and,
                                    ALU.bitwise_or).then_inc(s_pad, 1)
            dve.wait_ge(s_decay, 1)
            dve.wait_ge(s_expert_no, 1)
            dve.wait_ge(s_base, 1)

            def recur(l, n, e, j):
                dve.wait_ge(s_pg[l], n * 6 + 3 * e + 2)
                dve.wait_ge(s_k[l], n * 2 + e + 1)
                nc.vector.scalar_tensor_tensor(
                    kv[:, e, :], bank(l, e, 1, j), bias[:, l, 1, e:e + 1],
                    k_sb[:, e, :], ALU.add, ALU.mult).then_inc(s_kv[l], 1)
                dve.wait_ge(s_kv[l], n * 2 + e + 1)
                if within(n, 1, CHUNKS):
                    dve.wait_ge(s_y[l], n * 2 + e - 1)
                dve.wait_ge(s_cy[l], n * 2 + 2)
                nc.vector.tensor_tensor_scan(state[l][:, e, :], decay[:, :], kv[:, e, :],
                                             carry[:, l, e, bass.ds(n, 1)], ALU.mult, ALU.add).then_inc(s_sn[l], 1)
                dve.wait_ge(s_sn[l], n * 2 + e + 1)
                nc.vector.tensor_copy(carry[:, l, e, bass.ds(n + B, 1)], state[l][:, e, CH - 1:CH]).then_inc(s_cy[l], 1)

            def link(m, k, ins):
                ins.then_inc(s_rt, 1)
                dve.wait_ge(s_rt, m * ROUTER + k)

            def choose(m):
                dve.wait_ge(s_g, m + 1)
                link(m, 1, nc.vector.tensor_copy(g[:, :, :], out1[0][:, 0, 0:Q * E].rearrange("p (q e) -> p q e", q=Q)))
                dve.sem_inc(s_met, 1)
                for q in range(Q):
                    nc.vector.max(top[:, q, :], g[:, q, :]).then_inc(s_top, 1)
                dve.wait_ge(s_top, m * (2 * Q) + Q)
                dve.sem_inc(s_met, 1)
                for q in range(Q):
                    nc.vector.max_index(pick[:, q, :], top[:, q, :], g[:, q, :]).then_inc(s_top, 1)
                dve.wait_ge(s_top, m * (2 * Q) + 2 * Q)
                link(m, 2, nc.vector.tensor_copy(pick_f[:, :, :], pick[:, :, 0:2].rearrange("p q c -> p c q")))
                if within(m, 1, CHUNKS):
                    dve.wait_ge(s_prob, m)
                nc.vector.tensor_tensor(gap[:, :], top[:, :, 0], top[:, :, 1], ALU.subtract).then_inc(s_gap, 1)
                link(m, 3, nc.vector.tensor_tensor(sel[:, :, :, :], expert_no[:, :, :, :],
                                                   pick_f[:, :, :].unsqueeze(3).to_broadcast([P, 2, Q, E]), ALU.is_equal))
                if within(m, 1, CHUNKS):
                    dve.wait_ge(s_rank, m)
                nc.vector.tensor_tensor(picked[:, :, :], sel[:, 0, :, :], sel[:, 1, :, :], ALU.add).then_inc(s_picked, 1)

            def place(m, half, j):
                ranks = out1[0][:, 0, RANK_AT:RANK_AT + Q * E].rearrange("p (q e) -> p q e", q=Q)
                total = out1[0][:, 0, RANK_AT + Q * E:RANK_AT + Q * E + E]
                dve.wait_ge(s_rank, m + 1)
                link(m, 4, nc.vector.tensor_tensor(slot[:, :, :], ranks, base[:, :].unsqueeze(1).to_broadcast([P, Q, E]), ALU.add))
                nc.vector.tensor_tensor(base[:, :], total, base[:, :], ALU.add).then_inc(s_base, 1)
                link(m, 5, nc.vector.tensor_tensor(own[:, :, :, :], sel[:, :, :, :],
                                                   slot[:, :, :].unsqueeze(1).to_broadcast([P, 2, Q, E]), ALU.mult))
                dve.wait_ge(s_base, m + 2)
                link(m, 6, nc.vector.reduce_sum(slot_f[:, :, :], own[:, :, :, :], AX_X))
                if within(m, 2, CHUNKS):
                    dve.wait_ge(s_sc[1 - j], (half - 2 + j) * SCAT)
                nc.vector.tensor_copy(slot_u[1 - j][:, :, :], slot_f[:, :, :].rearrange("p c q -> p q c")).then_inc(s_slot, 1)

            def residual1(s, j):
                for i, b in enumerate((1, 0)):
                    dve.wait_ge(s_po[0], s * 2 + i - 1)
                    if within(s, 2, CHUNKS):
                        dve.wait_ge(s_u, s - 1)
                    nc.vector.tensor_tensor(xr[:, 2 * b:2 * b + 2, :], out1[b][:, :, :],
                                            x_in[:, 1 - j, 2 * b:2 * b + 2, :], ALU.add).then_inc(s_res, 1)
                dve.wait_ge(s_res, s * 2)

            def add_input(s, j):
                if within(s, 3, CHUNKS):
                    dve.wait_ge(s_z, s * 2 - 4)
                nc.vector.tensor_tensor(u[:, 1 - j, :, :], xr[:, :, :], x_in[:, 1 - j, :, :], ALU.add).then_inc(s_u, 1)

            def residual2(s, j):
                for b in range(2):
                    dve.wait_ge(s_po[1], s * 2 + b - 3)
                    dve.wait_ge(s_u, s - 1)
                    if at(s, 2):
                        dve.wait_ge(s_padst, 48)
                    else:
                        dve.wait_ge(s_x1, s - 2)
                    src = ring[(2 * j + 6 + b) % 4][:, :].rearrange("p (q d) -> p q d", q=2)
                    nc.vector.tensor_tensor(z[:, 2 * b:2 * b + 2, :], src, u[:, j, 2 * b:2 * b + 2, :],
                                            ALU.add).then_inc(s_z, 1)
                dve.wait_ge(s_z, s * 2 - 2)
                norm_stats(2, z, s - 2)

            def step(s, half, j):
                layer1, layer2 = within(s, 0, CHUNKS - 1), within(s, 1, CHUNKS)
                if layer2:
                    residual1(s, j)
                    norm_stats(1, xr, s - 1)
                    if not at(s, CHUNKS):
                        add_input(s, j)
                if at(s, CHUNKS):
                    residual2(s, j)
                if layer1:
                    for e in range(DC):
                        recur(0, s, e, j)
                if at(s, 0):
                    x_lo(0, 1)
                    keep_bias(1)
                    low_weights(1)
                if layer2:
                    x_lo(1, s - 1)
                if within(s, 1, CHUNKS - 2):
                    dve.wait_ge(s_x[1 - j], half * 16 + 16 * (1 + j))
                    norm_stats(0, x_in[:, 1 - j, :, :], s + 1)
                if at(s, CHUNKS):
                    add_input(s, j)
                if within(s, 2, CHUNKS + 1) and not at(s, CHUNKS):
                    residual2(s, j)
                if at(s, CHUNKS):
                    choose(s - 3)
                    for e in range(DC):
                        recur(1, s - 1, e, j)
                        gated(dve, 1, s - 1, e)
                        y_lo(dve, 1, s - 1, e)
                elif layer2:
                    recur(1, s - 1, 0, j)
                if within(s, 3, CHUNKS + 2) and not at(s, CHUNKS):
                    choose(s - 3)
                if within(s, 1, CHUNKS - 2):
                    x_lo(0, s + 1)
                if within(s, 3, CHUNKS + 2):
                    place(s - 3, half, j)
                if layer2 and not at(s, CHUNKS):
                    recur(1, s - 1, 1, j)

            run(dve, step)
            count = [3]

            def table_link(ins):
                count[0] += 1
                ins.then_inc(s_tab, 1)
                dve.wait_ge(s_tab, count[0])

            def running_sum(dst, src):
                table_link(nc.vector.tensor_tensor_scan(dst, one_row[:, :], src, 0.0, ALU.mult, ALU.add))

            def shift(dst, add, bits):
                table_link(nc.vector.tensor_scalar(used_i[:, :], used[:, :], float(add), None, ALU.add))
                table_link(nc.vector.tensor_scalar(used_i[:, :], used_i[:, :], bits, None, ALU.logical_shift_right))
                table_link(nc.vector.tensor_copy(dst, used_i[:, :]))

            dve.wait_ge(s_tab, 3)
            dve.wait_ge(s_base, CHUNKS + 1)
            table_link(nc.vector.tensor_tensor(used[:, :], base[0:1, :], start[:, :], ALU.subtract))
            shift(full[:, :], 0, CH.bit_length() - 1)
            running_sum(end[:, 0, :], full[:, :])
            table_link(nc.vector.memset(taken[:, :], 0.0))
            table_link(nc.vector.tensor_tensor(before_e[:, :], end[:, 0, :], full[:, :], ALU.subtract))
            table_link(nc.vector.tensor_scalar(before_e[:, :], before_e[:, :], -1.0, float(BIG), ALU.mult, ALU.add))
            table_link(nc.vector.tensor_scalar(before_e[:, :], before_e[:, :], 0.0, None, ALU.max))
            table_link(nc.vector.tensor_tensor(taken[:, 0:E], before_e[:, :], full[:, :], ALU.min))
            running_sum(end[:, 0, :], taken[:, 0:E])

            def passed(kind, first, n):
                table_link(nc.vector.tensor_tensor(
                    past[:, first:first + n, :], block_no[:, 0:n].unsqueeze(2).to_broadcast([1, n, E]),
                    end[:, kind, :].unsqueeze(1).to_broadcast([1, n, E]), ALU.is_ge))
                table_link(nc.vector.reduce_sum(rows[:, 0, first:first + n], past[:, first:first + n, :], AX_X))
                table_link(nc.vector.tensor_scalar(rows[:, 0, first:first + n], rows[:, 0, first:first + n],
                                                   E - 1.0, float(P), ALU.min, ALU.mult))
                nc.vector.tensor_copy(table[:, 0, first:first + n], rows[:, 0, first:first + n]).then_inc(s_table, 1)

            def first_slots(kind, first, n, slots):
                table_link(nc.vector.tensor_tensor(
                    hop[:, first:first + n, :], past[:, first:first + n, :],
                    skip[:, kind, :].unsqueeze(1).to_broadcast([1, n, E]), ALU.mult))
                table_link(nc.vector.reduce_sum(rows[:, 1, first:first + n], hop[:, first:first + n, :], AX_X))
                table_link(nc.vector.scalar_tensor_tensor(rows[:, 1, first:first + n], block_no[:, 0:n], float(slots),
                                                          rows[:, 1, first:first + n], ALU.mult, ALU.add))

            passed(0, 0, BIG)
            table_link(nc.vector.tensor_scalar(skip[:, 0, :], taken[:, 0:E], -float(CH), float(LIST), ALU.mult, ALU.add))
            first_slots(0, 0, BIG, CH)
            shift(full[:, :], SMALL - 1, SMALL.bit_length() - 1)
            table_link(nc.vector.scalar_tensor_tensor(used[:, :], taken[:, 0:E], -float(CH // SMALL), full[:, :], ALU.mult, ALU.add))
            running_sum(end[:, 1, :], used[:, :])
            table_link(nc.vector.scalar_tensor_tensor(skip[:, 1, :], taken[:, 1:E + 1], float(CH), skip[:, 0, :], ALU.mult, ALU.add))
            table_link(nc.vector.scalar_tensor_tensor(skip[:, 1, :], used[:, :], -float(SMALL), skip[:, 1, :], ALU.mult, ALU.add))
            passed(1, BIG, BLOCKS - BIG)
            first_slots(1, BIG, BLOCKS - BIG, SMALL)
            table_link(nc.vector.scalar_tensor_tensor(rows[:, 1, BIG:BLOCKS], taken[:, 0:1].to_broadcast([1, BLOCKS - BIG]),
                                                      float(CH), rows[:, 1, BIG:BLOCKS], ALU.mult, ALU.add))
            table_link(nc.vector.tensor_scalar(rows[:, 1, :], rows[:, 1, :], float(E * LIST), None, ALU.min))
            nc.vector.tensor_copy(table[:, 1, :], rows[:, 1, :]).then_inc(s_table, 1)
            dve.wait_ge(s_table, 3)

        @block.tensor
        def _(pe):
            def transpose(i, n, src):
                for dc in range(DC):
                    for q in range(Q):
                        last = nc.tensor.transpose(tp[dc][:, q * P:(q + 1) * P], src[:, q, dc * P:(dc + 1) * P], ident[:, :])
                    last.then_inc(s_pt[i], 1)

            def bias_products(l, products=(0, 1, 2)):
                pe.wait_ge(s_lnp, 16)
                pe.wait_ge(s_w[l], 16)
                for m in products:
                    for e in range(DC):
                        c = (l * 3 + m) * DC + e
                        for dc in range(DC):
                            last = nc.tensor.matmul(out1[1][:, 0, c:c + 1], w_raw[:, l, dc, m * D + e * P:m * D + (e + 1) * P],
                                                    lnp[:, 1, l, dc:dc + 1], start=dc == 0, stop=dc == DC - 1)
                if products[-1] == 2:
                    last.then_inc(s_bias, 1)

            def project(l, s, n, e, j, products=(0, 1, 2)):
                pe.wait_ge(s_xh[l], n * 2 + 2)
                pe.wait_ge(s_xl[l], n * 2 + 2)
                for m in products:
                    slot_no = 8 * l + 3 * e + m
                    if at(s, 0) and slot_no < 4:
                        holder = None
                    elif at(s, 1) and slot_no < 4:
                        holder, count = ((s_r[0], 1), (s_k[0], 2), (s_kv[0], 2), (s_r[0], 2))[slot_no]
                    elif at(s, 1) and slot_no in (10, 11):
                        holder, count = ((s_r[0], 3), (s_k[0], 4))[slot_no - 10]
                    elif at(s, CHUNKS) and slot_no in (8, 9):
                        holder, count = ((s_r[1], 2 * s - 3), (s_k[1], 2 * s - 2))[slot_no - 8]
                    else:
                        holder, count = {
                            0: (s_r[1], s * 2 - 3), 1: (s_k[1], s * 2 - 2), 2: (s_kv[1], s * 2 - 2), 3: (s_r[1], s * 2 - 2),
                            4: (s_k[0], s * 2 + 1), 5: (s_kv[0], s * 2 + 1),
                            8: (s_kv[0], s * 2 + 2), 9: (s_r[0], s * 2 + 2), 10: (s_z, s * 2 - 3), 11: (s_z, s * 2 - 2),
                            12: (s_k[1], s * 2 - 1), 13: (s_kv[1], s * 2 - 1)}[slot_no]
                    if holder is not None:
                        pe.wait_ge(holder, count)
                    out = bank(l, e, m, j)
                    col = m * D + e * P
                    for dc in range(DC):
                        hi, lo = w_hi[:, l, dc, col:col + P], w_lo[:, l, dc, col:col + P]
                        nc.tensor.matmul(out, hi, xh[l][:, dc, :], start=dc == 0, stop=False)
                        nc.tensor.matmul(out, hi, xl[l][:, dc, :], start=False, stop=False)
                        last = nc.tensor.matmul(out, lo, xh[l][:, dc, :], start=False, stop=dc == DC - 1)
                    last.then_inc(s_pg[l], 1)

            def output(l, out, q0):
                for i in range(2):
                    q = q0 + i
                    for dc in range(DC):
                        a, b = yh[l][:, dc, q * P:(q + 1) * P], yl[l][:, dc, q * P:(q + 1) * P]
                        hi, lo = w_hi[:, l, dc, 3 * D:4 * D], w_lo[:, l, dc, 3 * D:4 * D]
                        nc.tensor.matmul(out[:, i * D:(i + 1) * D], a, hi, start=dc == 0, stop=False)
                        nc.tensor.matmul(out[:, i * D:(i + 1) * D], a, lo, start=False, stop=False)
                        last = nc.tensor.matmul(out[:, i * D:(i + 1) * D], b, hi, start=False, stop=dc == DC - 1)
                last.then_inc(s_po[l], 1)

            def rows2(s, last_users):
                pe.wait_ge(s_n[1], s)
                for holder, count in last_users:
                    pe.wait_ge(holder, count)
                transpose(1, s - 1, normed[1])

            def output2(s, j):
                pe.wait_ge(s_yh[1], s * 2 - 2)
                pe.wait_ge(s_yl[1], s * 2 - 2)
                for b in range(2):
                    if within(s, 0, CHUNKS - 1):
                        pe.wait_ge((s_r[0], s_k[0])[b], s * 2 + 1 + b)
                    else:
                        pe.wait_ge((s_kv[1], s_r[1])[b], s * 2 - 2)
                    output(1, ring[(2 * j + 6 + b) % 4][:, :], 2 * b)

            def rows3(s, j, last_user, count):
                pe.wait_ge(s_x1, s - 2)
                pe.wait_ge(last_user, count)
                transpose(2, s - 3, x1[:, 1 - j, :, :])

            def gates(s, last_user, count):
                pe.wait_ge(s_x1T, s * 2 - 4)
                pe.wait_ge(last_user, count)
                for q in range(Q):
                    for dc in range(DC):
                        last = nc.tensor.matmul(out1[0][:, 0, q * E:(q + 1) * E], x1T[:, dc, q * P:(q + 1) * P],
                                                wg[:, dc, :], start=dc == 0, stop=dc == DC - 1)
                last.then_inc(s_g, 1)

            bias_products(0, (0, 1))
            pe.wait_ge(s_ident, 1)
            pe.wait_ge(s_n[0], 1)
            transpose(0, 0, normed[0])
            bias_products(0, (2,))
            pe.wait_ge(s_whi[0], DC + 1)
            pe.wait_ge(s_wlo[0], DC + 1)

            def step(s, half, j):
                layer1, layer2 = within(s, 0, CHUNKS - 1), within(s, 1, CHUNKS)
                if layer1:
                    for e in range(DC):
                        project(0, s, s, e, j)
                if at(s, 0):
                    pe.wait_ge(s_n[0], 2)
                    pe.wait_ge(s_xl[0], 2)
                    transpose(0, 1, normed[0])
                    bias_products(1)
                    pe.wait_ge(s_before, 1)
                    pe.wait_ge(s_ones, 1)
                if at(s, 1):
                    pe.wait_ge(s_whi[1], DC + 1)
                    pe.wait_ge(s_wlo[1], DC + 1)
                if at(s, CHUNKS):
                    output2(s, j)
                    rows3(s, j, s_xl[0], 2 * s)
                    rows2(s, ((s_x1T, s * 2 - 4),))
                    gates(s, s_res, s * 2)
                    project(1, s, s - 1, 0, j)
                elif at(s, CHUNKS + 1):
                    rows3(s, j, s_xl[1], 2 * s - 2)
                    output2(s, j)
                    gates(s, s_slot, s - 3)
                elif at(s, CHUNKS + 2):
                    rows3(s, j, s_x1T, 2 * s - 6)
                    gates(s, s_slot, s - 3)
                else:
                    if layer2:
                        rows2(s, ((s_xl[0], s * 2 + 2),))
                    if within(s, 2, CHUNKS):
                        output2(s, j)
                    if within(s, 3, CHUNKS):
                        rows3(s, j, s_xl[1], s * 2)
                    if layer2:
                        project(1, s, s - 1, 0, j)
                    if at(s, 3):
                        pe.wait_ge(s_wg, 16)
                    if within(s, 3, CHUNKS):
                        gates(s, s_res, s * 2)
                if within(s, 1, CHUNKS - 2):
                    pe.wait_ge(s_n[0], s + 2)
                    if within(s, 1, 2) and isinstance(s, int):
                        pe.wait_ge(s_xl[1], 2 * s)
                    else:
                        pe.wait_ge(s_x1T, s * 2 - 4)
                    transpose(0, s + 1, normed[0])
                if layer2:
                    project(1, s, s - 1, 1, j, (0, 1))
                if within(s, 3, CHUNKS + 2):
                    pe.wait_ge(s_picked, s - 2)
                    ranks = out1[0][:, 0, RANK_AT:RANK_AT + Q * E]
                    flat = picked[:, :, :].rearrange("p q e -> p (q e)")
                    nc.tensor.matmul(ranks, before[:, :], flat, start=True, stop=False)
                    for d in range(1, Q):
                        nc.tensor.matmul(ranks[:, d * E:Q * E], ones[:, :], flat[:, 0:(Q - d) * E], start=False, stop=d == Q - 1)
                    for q in range(Q):
                        last = nc.tensor.matmul(out1[0][:, 0, RANK_AT + Q * E:RANK_AT + Q * E + E], ones[:, :],
                                                picked[:, q, :], start=q == 0, stop=q == Q - 1)
                    last.then_inc(s_rank, 1)
                if layer2:
                    project(1, s, s - 1, 1, j, (2,))
                if layer1:
                    pe.wait_ge(s_yh[0], s * 2 + 2)
                    pe.wait_ge(s_yl[0], s * 2 + 2)
                    if within(s, 1, CHUNKS):
                        pe.wait_ge(s_res, s * 2)
                    else:
                        pe.wait_ge(s_biassb[0], 2)
                        pe.wait_ge(s_biassb[1], 2)
                    output(0, out1[1][:, :, :].rearrange("p q d -> p (q d)"), 2)
                    if within(s, 3, CHUNKS):
                        pe.wait_ge(s_slot, s - 2)
                    output(0, out1[0][:, :, :].rearrange("p q d -> p (q d)"), 0)

            run(pe, step)


def expert_phase(nc, w_ffn, x_src, x_acc, slot_list, ident, w_raw_all, table, s_w):
    with ExitStack() as ctx:
        def sb(name, shape, dt=F32):
            return ctx.enter_context(nc.sbuf_tensor(name, shape, dt))

        def sem(name):
            return ctx.enter_context(nc.semaphore(name))

        ring = [ctx.enter_context(nc.psum_tensor(f"fring{i}", [P, CH], F32)) for i in range(4)]
        tp = [ctx.enter_context(nc.psum_tensor(f"ftp{i}", [P, CH], F32)) for i in range(DC)]
        yp = [ctx.enter_context(nc.psum_tensor(f"fy{i}", [P, 2, D], F32)) for i in range(2)]

        w_raw = w_raw_all[:, :].rearrange("p (j c) -> p j c", j=2)
        w_hi = sb("fw_hi", [P, 2, WCOLS], F32R)
        w_lo = sb("fw_lo", [P, 2, WCOLS], F32R)
        pair_in = [sb(f"pair_in{i}", [P, Q, 2], I32) for i in range(2)]
        pair_out = [sb(f"pair_out{i}", [P, Q, 2], I32) for i in range(2)]
        xg = [sb(f"xg{i}", [P, Q, D]) for i in range(2)]
        xh = sb("fxh", [P, DC, CH], F32R)
        xl = sb("fxl", [P, DC, CH], F32R)
        silu = sb("silu", [P, 2, CH])
        gated = sb("gated", [P, 2, CH])
        gh = sb("gh", [P, 2, HC, CH], F32R)
        gl = sb("gl", [P, 2, HC, CH], F32R)
        y = [sb(f"fy_sb{i}", [P, Q, D]) for i in range(2)]

        zero = sb("fzero", [P, 1])
        warm = sb("fwarm", [P, 1])

        s_met, s_zero = sem("fwaits_met"), sem("fzero_ready")
        s_pair = [sem("pairs_in0"), sem("pairs_in1")]
        s_pair_out = [sem("pairs_out0"), sem("pairs_out1")]
        s_xg = [sem("rows_gathered0"), sem("rows_gathered1")]
        s_add = [sem("rows_added0"), sem("rows_added1")]
        s_pt, s_xh, s_xl = sem("ftransposed"), sem("fxh_ready"), sem("fxl_ready")
        s_h, s_silu, s_g, s_gh, s_gl = sem("h_product"), sem("silu_ready"), sem("gated_ready"), sem("gh_ready"), sem("gl_ready")
        s_y, s_yv = sem("y_product"), sem("y_weighted")
        s_whi = [sem(f"whi_ready{i}") for i in range(3)]
        s_wlo = [sem(f"wlo_ready{i}") for i in range(3)]

        block = ctx.enter_context(nc.Block())

        def run(eng, step):
            def peeled(first, end):
                for s in range(first, end):
                    step(s, s // 2, s % 2, lambda d: Q if s + d < BIG else Q // 2)

            def loop(first, end, size):
                with eng.Fori(first // 2, end // 2) as it:
                    step(it * 2, it, 0, size)
                    step(it * 2 + 1, it, 1, size)

            last = (BLOCKS - 2) // 2 * 2
            peeled(-1, 4)
            loop(4, BIG - 2, lambda d: Q)
            peeled(BIG - 2, BIG + 4)
            loop(BIG + 4, last, lambda d: Q // 2)
            peeled(last, BLOCKS + 2)

        def moved(half, tiles):
            if tiles == Q:
                return (half + 1) * (16 * Q)
            return (half + 1) * (16 * (Q // 2)) + 16 * (Q - Q // 2) * (BIG // 2)

        @block.sync
        def _(sp):
            def first_row(which, b, bound):
                column = slice(b, b + 1) if isinstance(b, int) else bass.ds(b, 1)
                return sp.value_load(table[0:1, which, column], min_val=0, max_val=bound)

            def pairs(b, dst, j, tiles, done):
                row = first_row(1, b, SLOTS - CH)
                return sp.dma_start(dst[j][:, 0:tiles, :], slot_list[bass.ds(row, tiles * P), :]
                                    .rearrange("(p q) c -> p q c", p=P)).then_inc(done, 16)

            def weights(b, j, i, w_row):
                low, high = PART[i]
                if within(b, 2, BLOCKS):
                    sp.wait_ge(s_whi[i], b - 1)
                    sp.wait_ge(s_wlo[i], b - 1)
                sp.dma_start(w_raw[:, j, low:high], w_ffn[bass.ds(w_row, P), low:high]).then_inc(s_w[i][j], 16)

            def step(s, half, j, size):
                if at(s, -1):
                    for b in range(2):
                        pairs(b, pair_in, b, Q, s_pair[b])
                    w_row = first_row(0, 1, (E - 1) * P)
                    sp.wait_ge(s_xg[0], moved(0, Q))
                    for i in range(3):
                        weights(1, 1, i, w_row)
                if within(s, 0, BLOCKS - 3):
                    w_row = first_row(0, s + 2, (E - 1) * P)
                    for i in range(2):
                        weights(s + 2, j, i, w_row)
                    sp.wait_ge(s_xg[j], moved(half, size(0)))
                    pairs(s + 2, pair_in, j, size(2), s_pair[j])
                    weights(s + 2, j, 2, w_row)
                if within(s, 0, BLOCKS - 1):
                    if within(s, 2, BLOCKS - 1):
                        sp.wait_ge(s_add[j], moved(half - 1, size(-2)))
                    pairs(s, pair_out, j, size(0), s_pair_out[j])

            run(sp, step)
            for par in range(2):
                sp.wait_ge(s_add[par], moved((BLOCKS - 1 - par) // 2, Q // 2))

        @block.gpsimd
        def _(pool):
            def gather(b, half, j, tiles):
                pool.wait_ge(s_pair[j], half * 16 + 16)
                if within(b, 2, BLOCKS):
                    pool.wait_ge(s_pt, b * 2 - 2)
                pool.sem_inc(s_met, 1)
                for q in range(tiles):
                    nc.gpsimd.indirect_dma_start(
                        xg[j][:, q, :], None, x_src,
                        bass.IndirectOffsetOnAxis(pair_in[j][:, q, 0:1].bitcast(U32), 0)).then_inc(s_xg[j], 16)

            def step(s, half, j, size):
                if within(s, -1, BLOCKS - 2):
                    gather(s + 1, half + j, 1 - j, size(1))
                if within(s, 2, BLOCKS + 1):
                    if within(s, 3, BLOCKS + 1):
                        pool.wait_ge(s_add[1 - j], moved(half - 2 + j, size(-3)))
                    pool.wait_ge(s_yv, s * 2 - 2)
                    pool.sem_inc(s_met, 1)
                    for q in range(size(-2)):
                        nc.gpsimd.indirect_dma_start(
                            x_acc, bass.IndirectOffsetOnAxis(pair_out[j][:, q, 0:1].bitcast(U32), 0),
                            y[j][:, q, :], None, compute_op=ALU.add).then_inc(s_add[j], 16)
                if within(s, 0, BLOCKS - 2):
                    low, high = PART[0]
                    pool.wait_ge(s_whi[0], s + 2)
                    nc.gpsimd.tensor_tensor(w_lo[:, 1 - j, low:high], w_raw[:, 1 - j, low:high],
                                            w_hi[:, 1 - j, low:high].bitcast(F32), ALU.subtract).then_inc(s_wlo[0], 1)

            run(pool, step)

        @block.scalar
        def _(act):
            def w_half(i, b, half, j):
                low, high = PART[i]
                act.wait_ge(s_w[i][j], half * 16 + 16)
                if within(b, 2, BLOCKS):
                    if i < 2:
                        act.wait_ge(s_h, b * (2 * HC) - 2 * HC)
                    else:
                        act.wait_ge(s_y, b * 2 - 2)
                nc.scalar.activation(w_hi[:, j, low:high], w_raw[:, j, low:high], ACT.Copy).then_inc(s_whi[i], 1)

            def act_silu(b, hb, n):
                act.wait_ge(s_h, b * (2 * HC) + 2 * hb + 1)
                if hb >= 2 or within(b, 1, BLOCKS):
                    act.wait_ge(s_g, b * HC + hb - 1)
                nc.scalar.activation(silu[:, hb % 2, 0:n], ring[2 * (hb % 2)][:, 0:n], ACT.Silu).then_inc(s_silu, 1)

            def g_hi(b, j, hb, n):
                act.wait_ge(s_g, b * HC + hb + 1)
                if within(b, 2, BLOCKS):
                    act.wait_ge(s_y, b * 2 - 2)
                nc.scalar.activation(gh[:, j, hb, 0:n], gated[:, hb % 2, 0:n], ACT.Copy).then_inc(s_gh, 1)

            def x_hi(b, n):
                for dc in range(DC):
                    act.wait_ge(s_pt, b * 2 + dc + 1)
                    nc.scalar.activation(xh[:, dc, 0:n], tp[dc][:, 0:n], ACT.Copy).then_inc(s_xh, 1)

            def step(s, half, j, size):
                here, nxt, n = within(s, 0, BLOCKS - 1), within(s, -1, BLOCKS - 2), size(0) * P
                if here:
                    w_half(2, s, half, j)
                    act_silu(s, 0, n)
                if nxt:
                    w_half(0, s + 1, half + j, 1 - j)
                if here:
                    act_silu(s, 1, n)
                    g_hi(s, j, 0, n)
                    act_silu(s, 2, n)
                    g_hi(s, j, 1, n)
                if nxt:
                    w_half(1, s + 1, half + j, 1 - j)
                if here:
                    act_silu(s, 3, n)
                    g_hi(s, j, 2, n)
                if nxt:
                    x_hi(s + 1, size(1) * P)
                if here:
                    g_hi(s, j, 3, n)

            act.wait_ge(s_zero, 1)
            nc.scalar.activation(warm[:, :], zero[:, :], ACT.Silu)
            run(act, step)

        @block.vector
        def _(dve):
            nc.vector.memset(zero[:, :], 0.0).then_inc(s_zero, 1)

            def w_low(i, b, half, j):
                low, high = PART[i]
                dve.wait_ge(s_whi[i], b + 1)
                nc.vector.tensor_tensor(w_lo[:, j, low:high], w_raw[:, j, low:high],
                                        w_hi[:, j, low:high].bitcast(F32), ALU.subtract).then_inc(s_wlo[i], 1)

            def gate(b, hb, n):
                dve.wait_ge(s_h, b * (2 * HC) + 2 * hb + 2)
                dve.wait_ge(s_silu, b * HC + hb + 1)
                if hb >= 2 or within(b, 1, BLOCKS):
                    dve.wait_ge(s_gl, b * HC + hb - 1)
                nc.vector.tensor_tensor(gated[:, hb % 2, 0:n], ring[2 * (hb % 2) + 1][:, 0:n], silu[:, hb % 2, 0:n],
                                        ALU.mult).then_inc(s_g, 1)

            def g_lo(b, j, hb, n):
                dve.wait_ge(s_gh, b * HC + hb + 1)
                nc.vector.tensor_tensor(gl[:, j, hb, 0:n], gated[:, hb % 2, 0:n], gh[:, j, hb, 0:n].bitcast(F32),
                                        ALU.subtract).then_inc(s_gl, 1)

            def x_lo(b, n):
                for dc in range(DC):
                    dve.wait_ge(s_xh, b * 2 + dc + 1)
                    nc.vector.tensor_tensor(xl[:, dc, 0:n], tp[dc][:, 0:n], xh[:, dc, 0:n].bitcast(F32),
                                            ALU.subtract).then_inc(s_xl, 1)

            def weigh(b, half, j, tiles):
                dve.wait_ge(s_pair_out[j], half * 16 + 16)
                for q in range(tiles):
                    bank, column = q // (tiles // 2), q % (tiles // 2)
                    dve.wait_ge(s_y, b * 2 + bank + 1)
                    last = nc.vector.tensor_scalar(y[j][:, q, :], yp[bank][:, column, :], pair_out[j][:, q, 1:2].bitcast(F32),
                                                   None, ALU.mult)
                    if column == tiles // 2 - 1:
                        last.then_inc(s_yv, 1)

            def step(s, half, j, size):
                here, nxt, n = within(s, 0, BLOCKS - 1), within(s, -1, BLOCKS - 2), size(0) * P
                if here:
                    w_low(2, s, half, j)
                    gate(s, 0, n)
                    gate(s, 1, n)
                    g_lo(s, j, 0, n)
                    gate(s, 2, n)
                    g_lo(s, j, 1, n)
                if at(s, -1):
                    w_low(0, 0, 0, 0)
                if nxt:
                    w_low(1, s + 1, half + j, 1 - j)
                if here:
                    gate(s, 3, n)
                    g_lo(s, j, 2, n)
                if nxt:
                    x_lo(s + 1, size(1) * P)
                if here:
                    g_lo(s, j, 3, n)
                if within(s, 1, BLOCKS):
                    weigh(s - 1, half - 1 + j, 1 - j, size(-1))

            run(dve, step)

        @block.tensor
        def _(pe):
            def hidden(b, j, hb, n):
                for i in range(2):
                    if hb >= 2 or within(b, 1, BLOCKS):
                        if i == 0:
                            pe.wait_ge(s_silu, b * HC + hb - 1)
                        else:
                            pe.wait_ge(s_g, b * HC + hb - 1)
                    out = ring[2 * (hb % 2) + i][:, 0:n]
                    for dc in range(DC):
                        col = PART[i][0] + dc * H + hb * P
                        hi, lo = w_hi[:, j, col:col + P], w_lo[:, j, col:col + P]
                        nc.tensor.matmul(out, hi, xh[:, dc, 0:n], start=dc == 0, stop=False)
                        nc.tensor.matmul(out, hi, xl[:, dc, 0:n], start=False, stop=False)
                        last = nc.tensor.matmul(out, lo, xh[:, dc, 0:n], start=False, stop=dc == DC - 1)
                    last.then_inc(s_h, 1)

            def step(s, half, j, size):
                if within(s, 0, BLOCKS - 1):
                    pe.wait_ge(s_xh, s * 2 + 2)
                    pe.wait_ge(s_xl, s * 2 + 2)
                    for i in range(2):
                        pe.wait_ge(s_whi[i], s + 1)
                        pe.wait_ge(s_wlo[i], s + 1)
                    for hb in range(HC):
                        hidden(s, j, hb, size(0) * P)
                if within(s, -1, BLOCKS - 2):
                    pe.wait_ge(s_xg[1 - j], moved(half + j, size(1)))
                    if within(s, 0, BLOCKS):
                        pe.wait_ge(s_xl, s * 2 + 2)
                    for dc in range(DC):
                        for q in range(size(1)):
                            last = nc.tensor.transpose(tp[dc][:, q * P:(q + 1) * P], xg[1 - j][:, q, dc * P:(dc + 1) * P],
                                                       ident[:, :])
                        last.then_inc(s_pt, 1)
                if within(s, 1, BLOCKS):
                    b, tiles = s - 1, size(-1)
                    pe.wait_ge(s_gh, b * HC + HC)
                    pe.wait_ge(s_gl, b * HC + HC)
                    pe.wait_ge(s_whi[2], b + 1)
                    pe.wait_ge(s_wlo[2], b + 1)
                    for q in range(tiles):
                        bank, column = q // (tiles // 2), q % (tiles // 2)
                        if within(s, 2, BLOCKS) and column == 0:
                            pe.wait_ge(s_yv, b * 2 - 1 + bank)
                        out = yp[bank][:, column, :]
                        for hc in range(HC):
                            col = PART[2][0] + hc * D
                            hi, lo = w_hi[:, 1 - j, col:col + D], w_lo[:, 1 - j, col:col + D]
                            a, c = gh[:, 1 - j, hc, q * P:(q + 1) * P], gl[:, 1 - j, hc, q * P:(q + 1) * P]
                            nc.tensor.matmul(out, a, hi, start=hc == 0, stop=False)
                            nc.tensor.matmul(out, a, lo, start=False, stop=False)
                            last = nc.tensor.matmul(out, c, hi, start=False, stop=hc == HC - 1)
                        if column == tiles // 2 - 1:
                            last.then_inc(s_y, 1)

            run(pe, step)


def norm_phase(nc, x_acc, out):
    DEPTH = 4
    with ExitStack() as ctx:
        def sb(name, shape, dt=F32):
            return ctx.enter_context(nc.sbuf_tensor(name, shape, dt))

        def sem(name):
            return ctx.enter_context(nc.semaphore(name))

        a = [sb(f"acc{i}", [P, Q, D]) for i in range(DEPTH)]
        o = [sb(f"o{i}", [P, Q, D]) for i in range(DEPTH)]
        stats = sb("nstats", [P, DEPTH, Q, 6])
        mv = sb("nmv", [P, DEPTH, Q, 2])
        ve = sb("nve", [P, DEPTH, Q])
        nm = sb("nnm", [P, DEPTH, Q])
        rs = sb("nrs", [P, DEPTH, Q])
        nb = sb("nnb", [P, DEPTH, Q])
        neg_half = sb("nneg_half", [P, Q])
        warm = sb("nwarm", [P, Q])
        s_in = [sem(f"acc_loaded{i}") for i in range(DEPTH)]
        s_out = [sem(f"out_stored{i}") for i in range(DEPTH)]
        s_half, s_bn, s_mv, s_ve, s_rs, s_nb, s_o = (sem("nneg_half_ready"), sem("nstats_ready"), sem("nmean_var"),
                                                     sem("nvar_eps"), sem("nrstd"), sem("nnorm_bias"), sem("normed_rows"))
        s_met = sem("nwaits_met")
        block = ctx.enter_context(nc.Block())

        def run(eng, step):
            for n in range(DEPTH):
                step(n, 0, n)
            with eng.Fori(1, CHUNKS // DEPTH) as it:
                for j in range(DEPTH):
                    step(it * DEPTH + j, it, j)

        @block.sync
        def _(sp):
            def step(n, turn, j):
                row = n * CH if isinstance(n, int) else sp.snap(n * CH)
                if within(n, DEPTH, CHUNKS):
                    sp.wait_ge(s_o, n - DEPTH + 1)
                sp.dma_start(a[j][:, :, :], x_acc[bass.ds(row, CH), :]
                             .rearrange("(p q) d -> p q d", p=P)).then_inc(s_in[j], 16)

            run(sp, step)

        @block.vector
        def _(dve):
            nc.vector.memset(neg_half[:, :], -0.5).then_inc(s_half, 1)

            def step(n, turn, j):
                dve.wait_ge(s_in[j], turn * 16 + 16)
                for q in range(Q):
                    nc.vector.bn_stats(stats[:, j, q, :], a[j][:, q, :]).then_inc(s_bn, 1)
                dve.wait_ge(s_bn, n * Q + Q)
                if within(n, DEPTH, CHUNKS):
                    dve.wait_ge(s_nb, n - DEPTH + 1)
                dve.sem_inc(s_met, 1)
                for q in range(Q):
                    nc.vector.bn_aggr(mv[:, j, q, :], stats[:, j, q, :]).then_inc(s_mv, 1)
                dve.wait_ge(s_mv, n * Q + Q)
                nc.vector.tensor_scalar(ve[:, j, :], mv[:, j, :, 1], EPS, None, ALU.add).then_inc(s_ve, 1)
                nc.vector.tensor_scalar(nm[:, j, :], mv[:, j, :, 0], -1.0, None, ALU.mult).then_inc(s_ve, 1)

            run(dve, step)

        @block.gpsimd
        def _(pool):
            pool.wait_ge(s_half, 1)

            def step(n, turn, j):
                pool.wait_ge(s_ve, n * 2 + 2)
                if within(n, DEPTH, CHUNKS):
                    pool.wait_ge(s_o, n - DEPTH + 1)
                nc.gpsimd.tensor_tensor(rs[:, j, :], ve[:, j, :], neg_half[:, :], ALU.pow).then_inc(s_rs, 1)
                pool.wait_ge(s_rs, n + 1)
                nc.gpsimd.tensor_tensor(nb[:, j, :], rs[:, j, :], nm[:, j, :], ALU.mult).then_inc(s_nb, 1)

            run(pool, step)

        @block.scalar
        def _(act):
            act.wait_ge(s_half, 1)
            nc.scalar.activation(warm[:, :], neg_half[:, :], ACT.Identity)

            def step(n, turn, j):
                row = n * P if isinstance(n, int) else act.snap(n * P)
                act.wait_ge(s_nb, n + 1)
                if within(n, DEPTH, CHUNKS):
                    act.wait_ge(s_out[j], turn * 16)
                for q in range(Q):
                    last = nc.scalar.activation(o[j][:, q, :], a[j][:, q, :], ACT.Identity,
                                                bias=nb[:, j, q:q + 1], scale=rs[:, j, q:q + 1])
                last.then_inc(s_o, 1)
                act.wait_ge(s_o, n + 1)
                act.dma_start(out[bass.ds(row, P), :], o[j][:, :, :].rearrange("p q d -> p (q d)")).then_inc(s_out[j], 16)

            run(act, step)
            for j in range(DEPTH):
                act.wait_ge(s_out[j], 16 * (CHUNKS // DEPTH))


def build(nc, h, w_att, ln_wb, w_gate, w_ffn, out):
    x_src = nc.dram_tensor("x_src", (TOKENS + CH, D), F32).ap()
    x_acc = nc.dram_tensor("x_acc", (TOKENS + CH, D), F32).ap()
    slot_list = nc.dram_tensor("slot_list", (SLOTS, 2), I32).ap()
    with ExitStack() as ctx:
        ident = ctx.enter_context(nc.sbuf_tensor("ident", [P, P], F32))
        w_raw = ctx.enter_context(nc.sbuf_tensor("w_raw", [P, 2 * WCOLS], F32))
        table = ctx.enter_context(nc.sbuf_tensor("table", [1, 2, BLOCKS], I32))
        s_fw = [[ctx.enter_context(nc.semaphore(f"w{i + 1}_loaded{j}")) for j in range(2)] for i in range(3)]
        attention_phase(nc, h, w_att, ln_wb, w_gate, w_ffn, x_src, x_acc, slot_list, ident, w_raw, table, s_fw)
        expert_phase(nc, w_ffn, x_src, x_acc, slot_list, ident, w_raw, table, s_fw)
        norm_phase(nc, x_acc, out)


def kernel(L0_attn_h, L0_attn_ln_w, L0_attn_ln_b, L0_attn_Wk, L0_attn_Wv, L0_attn_Wr, L0_attn_Wo,
           L0_ffn_Wg, L0_ffn_W1, L0_ffn_W2, L0_ffn_W3):
    import concourse.bacc as bacc
    import numpy as np
    from concourse.bass_utils import run_bass_kernel_spmd

    def by_partition(a, rows):
        a = np.asarray(a)
        a = a.reshape(a.shape[:-2] + (rows // P, P, a.shape[-1]))
        return np.ascontiguousarray(np.moveaxis(a, -2, 0))

    PIECES = T // CH
    x = np.asarray(L0_attn_h).reshape(B, PIECES, Q, P, D).transpose(1, 0, 3, 2, 4).reshape(CHUNKS * P, Q * D)
    att = np.concatenate([np.asarray(w).transpose(0, 2, 1) for w in (L0_attn_Wk, L0_attn_Wv, L0_attn_Wr, L0_attn_Wo)], axis=2)
    wb = np.stack([np.asarray(L0_attn_ln_w), np.asarray(L0_attn_ln_b)]).reshape(2, LAYERS, DC, P).transpose(3, 0, 1, 2)
    w1, w2, w3 = (by_partition(np.asarray(w).transpose(0, 2, 1), rows).transpose(1, 0, 2, 3).reshape(E * P, -1)
                  for w, rows in ((L0_ffn_W1, D), (L0_ffn_W2, D), (L0_ffn_W3, H)))
    arrays = {
        "h": np.ascontiguousarray(x),
        "w_att": by_partition(att, D),
        "ln_wb": np.ascontiguousarray(wb),
        "w_gate": by_partition(np.asarray(L0_ffn_Wg).T, D),
        "w_ffn": np.ascontiguousarray(np.concatenate([w1, w2, w3], axis=1)),
    }
    nc = bacc.Bacc("TRN2", target_bir_lowering=False, num_devices=1)
    args = [nc.dram_tensor(name, a.shape, F32, kind="ExternalInput").ap() for name, a in arrays.items()]
    out = nc.dram_tensor("out", (CHUNKS * P, Q * D), F32, kind="ExternalOutput").ap()
    build(nc, *args, out)
    result = run_bass_kernel_spmd(nc, [arrays], core_ids=[0]).results[0]["out"]
    return result.reshape(PIECES, B, P, Q, D).transpose(1, 0, 3, 2, 4).reshape(B, T, D)
```

```python
from contextlib import ExitStack

import concourse.bass as bass
from concourse import mybir

P = 128
ALU = mybir.AluOpType
ACT = mybir.ActivationFunctionType
F32 = mybir.dt.float32
F32R = mybir.dt.float32r
BF16 = mybir.dt.bfloat16
I32 = mybir.dt.int32
U32 = mybir.dt.uint32
AX_X = mybir.AxisListType.X

B, T, D = 4, 2048, 256
LAYERS = 2
E, H = 8, 512
DECAY, EPS = 0.95, 1e-5
CH = 512
Q = CH // P
DC = D // P
HC = H // P
TOKENS = B * T
CHUNKS = TOKENS // CH
LIST = TOKENS
SLOTS = E * LIST + CH
SMALL = CH // 2
EARLY = CHUNKS - 2
BIG = (EARLY * 2 * CH - E * (CH - 1)) // CH // 2 * 2
BLOCKS = BIG + (2 * TOKENS - E) // SMALL + E - BIG * (CH // SMALL)
WCOLS = 2 * DC * H + HC * D
PART = ((0, DC * H), (DC * H, 2 * DC * H), (2 * DC * H, WCOLS))
SCAT = 16 * 2 * Q
RANK_AT = 64


def within(s, low, high):
    return not isinstance(s, int) or low <= s <= high


def at(s, n):
    return isinstance(s, int) and s == n


class Kept:
    pass


def scatter_pairs(nc, kept, slot_list, j, first, count):
    for i in range(first, first + count):
        q, c = i // 2, i % 2
        nc.gpsimd.indirect_dma_start(
            slot_list, bass.IndirectOffsetOnAxis(kept.slot_u[j][:, q, c:c + 1], 0),
            kept.pairs[j][:, q, c, :].bitcast(I32), None).then_inc(kept.s_sc[j], 16)


def gather_rows(nc, pool, kept, x_src, s_met, half, j, tiles):
    pool.wait_ge(kept.s_pair[j], half * 16 + 16)
    pool.sem_inc(s_met, 1)
    for q in range(tiles):
        nc.gpsimd.indirect_dma_start(
            kept.xg[j][:, q, :], None, x_src,
            bass.IndirectOffsetOnAxis(kept.pair_in[j][:, q, 0:1].bitcast(U32), 0)).then_inc(kept.s_xg[j], 16)



def table_link(dve, k, ins):
    k.table_steps += 1
    ins.then_inc(k.s_tab, 1)
    dve.wait_ge(k.s_tab, k.table_steps)


def running_sum(nc, dve, k, dst, src):
    table_link(dve, k, nc.vector.tensor_tensor_scan(dst, k.one_row[:, :], src, 0.0, ALU.mult, ALU.add))


def whole_blocks(nc, dve, k, add, bits):
    table_link(dve, k, nc.vector.tensor_tensor(k.used[:, :], k.base[0:1, :], k.start[:, :], ALU.subtract))
    table_link(dve, k, nc.vector.tensor_scalar(k.used_i[:, :], k.used[:, :], float(add), None, ALU.add))
    table_link(dve, k, nc.vector.tensor_scalar(k.used_i[:, :], k.used_i[:, :], bits, None, ALU.logical_shift_right))
    table_link(dve, k, nc.vector.tensor_copy(k.full[:, :], k.used_i[:, :]))


def fill_table(nc, dve, k, kind, first, n, slots):
    by_expert = [1, n, E]
    past, hop = k.past[:, first:first + n, :], k.hop[:, first:first + n, :]
    w_row, slot_row = k.rows[:, 0, first:first + n], k.rows[:, 1, first:first + n]
    table_link(dve, k, nc.vector.tensor_tensor(past, k.block_no[:, 0:n].unsqueeze(2).to_broadcast(by_expert),
                                               k.end[:, kind, :].unsqueeze(1).to_broadcast(by_expert), ALU.is_ge))
    table_link(dve, k, nc.vector.tensor_tensor(hop, past, k.skip[:, kind, :].unsqueeze(1).to_broadcast(by_expert), ALU.mult))
    table_link(dve, k, nc.vector.reduce_sum(w_row, past, AX_X))
    table_link(dve, k, nc.vector.tensor_scalar(w_row, w_row, E - 1.0, float(P), ALU.min, ALU.mult))
    nc.vector.tensor_copy(k.table[:, 0, first:first + n], w_row).then_inc(k.s_table, 1)
    table_link(dve, k, nc.vector.reduce_sum(slot_row, hop, AX_X))
    table_link(dve, k, nc.vector.scalar_tensor_tensor(slot_row, k.block_no[:, 0:n], float(slots), slot_row,
                                                      ALU.mult, ALU.add))
    if kind:
        table_link(dve, k, nc.vector.scalar_tensor_tensor(slot_row, k.taken[:, 0:1].to_broadcast([1, n]), float(CH), slot_row,
                                                          ALU.mult, ALU.add))
        table_link(dve, k, nc.vector.tensor_scalar(slot_row, slot_row, float(E * LIST), None, ALU.min))
    nc.vector.tensor_copy(k.table[:, 1, first:first + n], slot_row).then_inc(k.s_table, 1)


def big_table(nc, dve, k):
    dve.wait_ge(k.s_tab, 3)
    whole_blocks(nc, dve, k, 0, CH.bit_length() - 1)
    running_sum(nc, dve, k, k.end[:, 0, :], k.full[:, :])
    table_link(dve, k, nc.vector.memset(k.taken[:, :], 0.0))
    table_link(dve, k, nc.vector.tensor_tensor(k.before[:, :], k.end[:, 0, :], k.full[:, :], ALU.subtract))
    table_link(dve, k, nc.vector.tensor_scalar(k.before[:, :], k.before[:, :], -1.0, float(BIG), ALU.mult, ALU.add))
    table_link(dve, k, nc.vector.tensor_scalar(k.before[:, :], k.before[:, :], 0.0, None, ALU.max))
    table_link(dve, k, nc.vector.tensor_tensor(k.taken[:, 0:E], k.before[:, :], k.full[:, :], ALU.min))
    running_sum(nc, dve, k, k.end[:, 0, :], k.taken[:, 0:E])
    table_link(dve, k, nc.vector.tensor_scalar(k.skip[:, 0, :], k.taken[:, 0:E], -float(CH), float(LIST), ALU.mult, ALU.add))
    fill_table(nc, dve, k, 0, 0, BIG, CH)


def small_counts(nc, dve, k):
    whole_blocks(nc, dve, k, SMALL - 1, SMALL.bit_length() - 1)
    table_link(dve, k, nc.vector.scalar_tensor_tensor(k.used[:, :], k.taken[:, 0:E], -float(CH // SMALL), k.full[:, :],
                                                      ALU.mult, ALU.add))
    running_sum(nc, dve, k, k.end[:, 1, :], k.used[:, :])
    table_link(dve, k, nc.vector.scalar_tensor_tensor(k.skip[:, 1, :], k.taken[:, 1:E + 1], float(CH), k.skip[:, 0, :],
                                                      ALU.mult, ALU.add))
    table_link(dve, k, nc.vector.scalar_tensor_tensor(k.skip[:, 1, :], k.used[:, :], -float(SMALL), k.skip[:, 1, :],
                                                      ALU.mult, ALU.add))


def attention_phase(nc, h, w_att, ln_wb, w_gate, w_ffn, x_src, x_acc, slot_list, kept):
    ident, w_raw_all, base, table = kept.ident, kept.w_raw, kept.base, kept.table
    pairs, slot_u, s_sc = kept.pairs, kept.slot_u, kept.s_sc
    with ExitStack() as ctx:
        def sb(name, shape, dt=F32):
            return ctx.enter_context(nc.sbuf_tensor(name, shape, dt))

        def sem(name):
            return ctx.enter_context(nc.semaphore(name))

        ring = [ctx.enter_context(nc.psum_tensor(f"ring{i}", [P, CH], F32)) for i in range(4)]
        tp = [ctx.enter_context(nc.psum_tensor(f"tp{i}", [P, CH], F32)) for i in range(DC)]
        out1 = [ctx.enter_context(nc.psum_tensor(f"out1_{i}", [P, 2, D], F32)) for i in range(2)]

        before = sb("before", [P, P], BF16)
        ones = sb("ones", [P, P], BF16)
        decay = sb("decay", [P, CH])
        neg_half = sb("neg_half", [P, Q])
        warm = sb("warm", [P, Q])
        expert_no = sb("expert_no", [P, 2, Q, E])
        w_raw = w_raw_all[:, 0:LAYERS * DC * 4 * D].rearrange("p (l c m) -> p l c m", l=LAYERS, c=DC)
        w_hi = sb("w_hi", [P, LAYERS, DC, 4 * D], F32R)
        w_lo = sb("w_lo", [P, LAYERS, DC, 4 * D], F32R)
        lnp = sb("lnp", [P, 2, LAYERS, DC])
        wg = sb("wg", [P, DC, E])
        bias = sb("bias", [P, LAYERS, 3, DC])
        x_in = sb("x_in", [P, 2, Q, D])
        normed = [sb(f"normed{l}", [P, Q, D]) for l in range(2)]
        xh = [sb(f"xh{l}", [P, DC, CH], F32R) for l in range(2)]
        xl = [sb(f"xl{l}", [P, DC, CH], F32R) for l in range(2)]
        k_sb = sb("k_sb", [P, DC, CH])
        kv = sb("kv", [P, DC, CH])
        state = [sb(f"state{l}", [P, DC, CH]) for l in range(2)]
        r_sb = [sb(f"r_sb{l}", [P, DC, CH]) for l in range(2)]
        y = [sb(f"y{l}", [P, DC, CH]) for l in range(2)]
        yh = [sb(f"yh{l}", [P, DC, CH], F32R) for l in range(2)]
        yl = [sb(f"yl{l}", [P, DC, CH], F32R) for l in range(2)]
        carry = sb("carry", [P, LAYERS, DC, CHUNKS + B])
        xr = sb("xr", [P, Q, D])
        u = sb("u", [P, 2, Q, D])
        z = sb("z", [P, Q, D])
        x1 = sb("x1", [P, 2, Q, D])
        x1T = sb("x1T", [P, DC, CH])
        stats = [sb(f"stats{i}", [P, Q, 6]) for i in range(3)]
        mv = [sb(f"mv{i}", [P, Q, 2]) for i in range(3)]
        ve = [sb(f"ve{i}", [P, Q]) for i in range(3)]
        nm = [sb(f"nm{i}", [P, Q]) for i in range(3)]
        rs = [sb(f"rs{i}", [P, Q]) for i in range(3)]
        nb = [sb(f"nb{i}", [P, Q]) for i in range(3)]
        g = sb("g", [P, Q, E])
        top = sb("top", [P, Q, E])
        pick = sb("pick", [P, Q, E], U32)
        pick_f = sb("pick_f", [P, 2, Q])
        sel = sb("sel", [P, 2, Q, E])
        picked = sb("picked", [P, Q, E], BF16)
        gap = sb("gap", [P, Q])
        slot = sb("slot", [P, Q, E])
        own = sb("own", [P, 2, Q, E])
        slot_f = sb("slot_f", [P, 2, Q])
        pad = sb("pad", [P, SLOTS // P, 2], I32)

        s_blank, s_ident, s_before, s_expert_no = (sem("blanks_ready"), sem("identity_ready"), sem("before_ready"),
                                                  sem("expert_no_ready"))
        s_base, s_half, s_ones, s_decay, s_zeros = (sem("base_ready"), sem("neg_half_ready"), sem("ones_ready"),
                                                    sem("decay_ready"), sem("zeros_ready"))
        s_w = [sem("weights_loaded0"), sem("weights_loaded1")]
        s_lnp, s_wg, s_pad, s_padst = sem("ln_loaded"), sem("gate_loaded"), sem("pad_ready"), sem("pad_stored")
        s_bias = sem("bias_products")
        s_biassb = [sem("bias_ready0"), sem("bias_ready1")]
        s_whi = [sem("weights_hi0"), sem("weights_hi1")]
        s_wlo = [sem("weights_lo0"), sem("weights_lo1")]
        s_x = [sem("x_loaded0"), sem("x_loaded1")]
        s_bn = [sem(f"tile_stats{i}") for i in range(3)]
        s_mv = [sem(f"mean_var{i}") for i in range(3)]
        s_ve = [sem(f"var_eps{i}") for i in range(3)]
        s_rs = [sem(f"rstd{i}") for i in range(3)]
        s_nb = [sem(f"norm_bias{i}") for i in range(3)]
        s_n = [sem("normed_0"), sem("normed_1")]
        s_pt = [sem(f"transposed{i}") for i in range(3)]
        s_xh = [sem("xh_ready0"), sem("xh_ready1")]
        s_xl = [sem("xl_ready0"), sem("xl_ready1")]
        s_pg = [sem("projected0"), sem("projected1")]
        s_k = [sem("k_ready0"), sem("k_ready1")]
        s_kv = [sem("kv_ready0"), sem("kv_ready1")]
        s_r = [sem("r_ready0"), sem("r_ready1")]
        s_sn = [sem("scanned0"), sem("scanned1")]
        s_cy = [sem("carried0"), sem("carried1")]
        s_y = [sem("y_ready0"), sem("y_ready1")]
        s_yh = [sem("yh_ready0"), sem("yh_ready1")]
        s_yl = [sem("yl_ready0"), sem("yl_ready1")]
        s_po = [sem("out_product0"), sem("out_product1")]
        s_res, s_u, s_z, s_x1 = sem("residual_ready"), sem("u_ready"), sem("z_ready"), sem("x1_ready")
        s_st = [sem("x1_stored0"), sem("x1_stored1")]
        s_x1T, s_g, s_rt, s_gap, s_prob = sem("x1T_ready"), sem("gates"), sem("router_steps"), sem("gap_ready"), sem("probs_ready")
        s_top = sem("gates_ranked")
        s_picked, s_rank, s_slot = sem("picked_ready"), sem("rank_product"), sem("slots_ready")
        s_ids = sem("ids_ready")
        s_met = sem("waits_met")

        block = ctx.enter_context(nc.Block())

        ROUTER = 6
        LAST = CHUNKS + 4

        def run(eng, step):
            for s in range(6):
                step(s, s // 2, s % 2)
            with eng.Fori(3, CHUNKS // 2 - 1) as it:
                step(it * 2, it, 0)
                step(it * 2 + 1, it, 1)
            for s in range(CHUNKS - 2, LAST):
                step(s, s // 2, s % 2)

        def bank(l, e, m, j):
            return ring[(2 * j + 8 * l + 3 * e + m) % 4][:, :]

        def gated(eng, l, n, e):
            eng.wait_ge(s_sn[l], n * 2 + e + 1)
            eng.wait_ge(s_r[l], n * 2 + e + 1)
            if within(n, 1, CHUNKS):
                eng.wait_ge(s_yh[l], n * 2 + e - 1)
                eng.wait_ge(s_yl[l], n * 2 + e - 1)
            eng.tensor_tensor(y[l][:, e, :], state[l][:, e, :], r_sb[l][:, e, :], ALU.mult).then_inc(s_y[l], 1)

        def y_lo(eng, l, n, e):
            eng.wait_ge(s_y[l], n * 2 + e + 1)
            eng.wait_ge(s_yh[l], n * 2 + e + 1)
            if within(n, 1, CHUNKS):
                eng.wait_ge(s_po[l], n * 2)
            eng.tensor_tensor(yl[l][:, e, :], y[l][:, e, :], yh[l][:, e, :].bitcast(F32),
                              ALU.subtract).then_inc(s_yl[l], 1)

        @block.sync
        def _(sp):
            def load(n, par):
                row = n * P if isinstance(n, int) else sp.snap(n * P)
                if within(n, 2, CHUNKS):
                    sp.wait_ge(s_u, n - 1)
                sp.dma_start(x_in[:, par, :, :], h[bass.ds(row, P), :]
                             .rearrange("p (q d) -> p q d", q=Q)).then_inc(s_x[par], 16)

            load(0, 0)
            sp.dma_start(lnp[:, :, :, :], ln_wb).then_inc(s_lnp, 16)
            for l in range(LAYERS):
                sp.dma_start(w_raw[:, l, :, :], w_att[:, l, :, :]).then_inc(s_w[l], 16)
                if l == 0:
                    load(1, 1)
            sp.dma_start(wg[:, :, :], w_gate).then_inc(s_wg, 16)
            sp.wait_ge(s_pad, 2)
            sp.dma_start(slot_list.rearrange("(p n) c -> p n c", p=P), pad[:, :, :]).then_inc(s_padst, 16)
            sp.wait_ge(s_zeros, 1)
            for dst in (x_src, x_acc):
                sp.dma_start(dst[TOKENS:TOKENS + CH, :].rearrange("(p q) d -> p q d", p=P), z[:, :, :]).then_inc(s_padst, 16)

            def first_block():
                sp.wait_ge(kept.s_table, 2)
                for l in range(LAYERS):
                    sp.wait_ge(s_bias, l + 1)
                    sp.wait_ge(s_whi[l], DC + 1)
                    sp.wait_ge(s_wlo[l], DC + 1)
                w_row = sp.value_load(table[0:1, 0, 0:1], min_val=0, max_val=(E - 1) * P)
                slot_row = sp.value_load(table[0:1, 1, 0:1], min_val=0, max_val=SLOTS - CH)
                for i, (low, high) in enumerate(PART):
                    sp.dma_start(w_raw_all[:, low:high], w_ffn[bass.ds(w_row, P), low:high]).then_inc(kept.s_w[i][0], 16)
                for par in range(2):
                    sp.wait_ge(s_sc[par], SCAT * (EARLY // 2))
                sp.dma_start(kept.pair_in[0][:, :, :], slot_list[bass.ds(slot_row, CH), :]
                             .rearrange("(p q) c -> p q c", p=P)).then_inc(kept.s_pair[0], 16)

            def step(s, half, j):
                if within(s, 1, CHUNKS - 2):
                    load(s + 1, 1 - j)
                if at(s, CHUNKS + 1):
                    first_block()
                if within(s, 2, CHUNKS + 1):
                    row = (s - 2) * CH if isinstance(s, int) else sp.snap(s * CH - 2 * CH)
                    sp.wait_ge(s_x1, s - 1)
                    for dst in (x_src, x_acc):
                        sp.dma_start(dst[bass.ds(row, CH), :].rearrange("(p q) d -> p q d", p=P),
                                     x1[:, j, :, :]).then_inc(s_st[j], 16)

            run(sp, step)
            sp.wait_ge(s_wg, 16)
            sp.wait_ge(s_padst, 48)
            for par in range(2):
                sp.wait_ge(s_st[par], 32 * (CHUNKS // 2))

        @block.scalar
        def _(act):
            act.wait_ge(s_half, 1)
            nc.scalar.activation(warm[:, :], neg_half[:, :], ACT.Sigmoid)

            def split_weights(l):
                act.wait_ge(s_lnp, 16)
                act.wait_ge(s_w[l], 16)
                for dc in range(DC):
                    nc.scalar.activation(w_hi[:, l, dc, 0:3 * D], w_raw[:, l, dc, 0:3 * D], ACT.Copy,
                                         scale=lnp[:, 0, l, dc:dc + 1]).then_inc(s_whi[l], 1)
                nc.scalar.activation(w_hi[:, l, :, 3 * D:4 * D], w_raw[:, l, :, 3 * D:4 * D], ACT.Copy).then_inc(s_whi[l], 1)

            def normalize(i, src, dst, n, done):
                act.wait_ge(s_nb[i], n + 1)
                for q in range(Q):
                    last = nc.scalar.activation(dst[:, q, :], src[:, q, :], ACT.Identity,
                                                bias=nb[i][:, q:q + 1], scale=rs[i][:, q:q + 1])
                last.then_inc(done, 1)

            def x_hi(l, n):
                for dc in range(DC):
                    act.wait_ge(s_pt[l], n * 2 + dc + 1)
                    nc.scalar.activation(xh[l][:, dc, :], tp[dc][:, :], ACT.Copy).then_inc(s_xh[l], 1)

            def keep_k(l, n, e, j, free_sem, free_at):
                act.wait_ge(s_pg[l], n * 6 + 3 * e + 1)
                if free_sem is not None:
                    act.wait_ge(free_sem, free_at)
                nc.scalar.activation(k_sb[:, e, :], bank(l, e, 0, j), ACT.Identity,
                                     bias=bias[:, l, 0, e:e + 1], scale=1.0 - DECAY).then_inc(s_k[l], 1)

            def gate_r(l, n, e, j):
                act.wait_ge(s_pg[l], n * 6 + 3 * e + 3)
                if within(n, 1, CHUNKS):
                    act.wait_ge(s_y[l], n * 2 + e - 1)
                nc.scalar.activation(r_sb[l][:, e, :], bank(l, e, 2, j), ACT.Sigmoid,
                                     bias=bias[:, l, 2, e:e + 1]).then_inc(s_r[l], 1)

            def y_hi(l, n, e):
                act.wait_ge(s_y[l], n * 2 + e + 1)
                if within(n, 1, CHUNKS):
                    act.wait_ge(s_po[l], n * 2)
                nc.scalar.activation(yh[l][:, e, :], y[l][:, e, :], ACT.Copy).then_inc(s_yh[l], 1)

            def keep_x1T(s):
                for dc in range(DC):
                    act.wait_ge(s_pt[2], s * 2 + dc - 5)
                    if within(s, 4, CHUNKS + 2):
                        act.wait_ge(s_g, s - 3)
                    nc.scalar.activation(x1T[:, dc, :], tp[dc][:, :], ACT.Copy).then_inc(s_x1T, 1)

            def normalize3(s, half, j):
                if within(s, 4, CHUNKS + 1):
                    act.wait_ge(s_st[j], half * 32 - 32)
                    act.wait_ge(s_pt[2], s * 2 - 6)
                normalize(2, z, x1[:, j, :, :], s - 2, s_x1)

            split_weights(0)
            x_hi(0, 0)
            act.wait_ge(s_pt[0], 2)
            normalize(0, x_in[:, 1, :, :], normed[0], 1, s_n[0])
            act.wait_ge(s_biassb[0], 2)

            def step(s, half, j):
                layer1, layer2 = within(s, 0, CHUNKS - 1), within(s, 1, CHUNKS)
                if layer1:
                    for e in range(DC):
                        if e == 1 and layer2:
                            if within(s, 2, CHUNKS):
                                act.wait_ge(s_pt[1], s * 2 - 2)
                            normalize(1, xr, normed[1], s - 1, s_n[1])
                        if at(s, 0):
                            keep_k(0, s, e, j, None, 0)
                        elif at(s, 1):
                            keep_k(0, s, e, j, s_kv[0], 2)
                        else:
                            keep_k(0, s, e, j, s_kv[1], s * 2 + e - 3)
                        gate_r(0, s, e, j)
                elif layer2:
                    act.wait_ge(s_pt[1], s * 2 - 2)
                    normalize(1, xr, normed[1], s - 1, s_n[1])
                if at(s, 0):
                    x_hi(0, 1)
                if at(s, CHUNKS):
                    keep_x1T(s)
                if layer2:
                    x_hi(1, s - 1)
                if at(s, CHUNKS):
                    normalize3(s, half, j)
                if layer1:
                    for e in range(DC):
                        y_hi(0, s, e)
                if at(s, 0):
                    split_weights(1)
                    act.wait_ge(s_biassb[1], 2)
                if within(s, 3, CHUNKS + 2) and not at(s, CHUNKS) and not at(s, CHUNKS + 1):
                    keep_x1T(s)
                if within(s, 1, CHUNKS - 2):
                    act.wait_ge(s_pt[0], s * 2 + 2)
                    normalize(0, x_in[:, 1 - j, :, :], normed[0], s + 1, s_n[0])
                if layer2:
                    if at(s, CHUNKS):
                        keep_k(1, s - 1, 0, j, s_kv[1], 2 * s - 3)
                    else:
                        keep_k(1, s - 1, 0, j, s_kv[0], s * 2 + 1)
                if within(s, 2, CHUNKS + 1) and not at(s, CHUNKS):
                    normalize3(s, half, j)
                if layer2:
                    gate_r(1, s - 1, 0, j)
                if within(s, 1, CHUNKS - 2):
                    x_hi(0, s + 1)
                if layer2:
                    if at(s, CHUNKS):
                        keep_k(1, s - 1, 1, j, s_kv[1], 2 * s - 2)
                    else:
                        keep_k(1, s - 1, 1, j, s_kv[0], s * 2 + 2)
                    y_hi(1, s - 1, 0)
                if within(s, 3, CHUNKS + 2):
                    act.wait_ge(s_gap, s - 2)
                    if within(s, 5, CHUNKS + 2):
                        act.wait_ge(s_sc[1 - j], (half - 2 + j) * SCAT)
                    nc.scalar.activation(pairs[1 - j][:, :, 0, 1], gap[:, :], ACT.Sigmoid)
                    nc.scalar.activation(pairs[1 - j][:, :, 1, 1], gap[:, :], ACT.Sigmoid, scale=-1.0).then_inc(s_prob, 1)
                if layer2:
                    gate_r(1, s - 1, 1, j)
                    if at(s, CHUNKS):
                        keep_x1T(s + 1)
                    y_hi(1, s - 1, 1)

            run(act, step)

        @block.gpsimd
        def _(pool):
            nc.gpsimd.memset(ident[:, :], 0.0).then_inc(s_blank, 1)
            nc.gpsimd.memset(before[:, :], 0.0).then_inc(s_blank, 1)
            nc.gpsimd.memset(pad[:, :, :], 0).then_inc(s_blank, 1)
            pool.wait_ge(s_blank, 3)
            nc.gpsimd.affine_select(out=ident[:, :], in_=ident[:, :], compare_op=ALU.not_equal, fill=1.0,
                                    base=0, pattern=[[-1, P]], channel_multiplier=1).then_inc(s_ident, 1)
            nc.gpsimd.affine_select(out=before[:, :], in_=before[:, :], compare_op=ALU.is_ge, fill=1.0,
                                    base=0, pattern=[[-1, P]], channel_multiplier=1).then_inc(s_before, 1)
            nc.gpsimd.iota(pad[:, :, 0], [[1, SLOTS // P]], base=0,
                           channel_multiplier=SLOTS // P).then_inc(s_pad, 1)
            nc.gpsimd.iota(expert_no[:, :, :, :], [[0, 2], [0, Q], [1, E]], base=0, channel_multiplier=0,
                           allow_small_or_imprecise_dtypes=True).then_inc(s_expert_no, 1)
            nc.gpsimd.iota(base[:, :], [[LIST, E]], base=0, channel_multiplier=0,
                           allow_small_or_imprecise_dtypes=True).then_inc(s_base, 1)
            for j in range(2):
                nc.gpsimd.iota(pairs[j][:, :, :, 0].bitcast(I32), [[1, Q], [0, 2]], base=CH * j - 2 * CH,
                               channel_multiplier=Q).then_inc(s_ids, 1)

            nc.gpsimd.iota(kept.block_no[:, :], [[1, BLOCKS]], base=0, channel_multiplier=0,
                           allow_small_or_imprecise_dtypes=True).then_inc(kept.s_tab, 1)
            nc.gpsimd.iota(kept.start[:, :], [[LIST, E]], base=0, channel_multiplier=0,
                           allow_small_or_imprecise_dtypes=True).then_inc(kept.s_tab, 1)

            def rstd(i, n):
                pool.wait_ge(s_ve[i], n * 2 + 2)
                if within(n, 1, CHUNKS):
                    pool.wait_ge((s_n[0], s_n[1], s_x1)[i], n)
                nc.gpsimd.tensor_tensor(rs[i][:, :], ve[i][:, :], neg_half[:, :], ALU.pow).then_inc(s_rs[i], 1)
                pool.wait_ge(s_rs[i], n + 1)
                nc.gpsimd.tensor_tensor(nb[i][:, :], rs[i][:, :], nm[i][:, :], ALU.mult).then_inc(s_nb[i], 1)

            def open_scatter(s, half, j):
                if not within(s, 4, CHUNKS + 3):
                    return
                if within(s, 6, CHUNKS + 3):
                    pool.wait_ge(s_sc[j], (half - 2) * SCAT)
                pool.wait_ge(s_ids, s - 2)
                pool.sem_inc(s_met, 1)
                ids = pairs[j][:, :, :, 0].bitcast(I32)
                nc.gpsimd.tensor_scalar(ids, ids, 2 * CH, None, ALU.add).then_inc(s_ids, 1)
                pool.wait_ge(s_ids, s - 1)
                pool.wait_ge(s_prob, s - 3)
                pool.wait_ge(s_slot, s - 3)
                pool.wait_ge(s_padst, 48)
                pool.sem_inc(s_met, 1)

            def scatter(s, j, first, count):
                if within(s, 4, CHUNKS + 1):
                    scatter_pairs(nc, kept, slot_list, j, first, count)

            pool.wait_ge(s_half, 1)
            rstd(0, 0)
            rstd(0, 1)

            def step(s, half, j):
                layer1, layer2 = within(s, 0, CHUNKS - 1), within(s, 1, CHUNKS)
                if at(s, CHUNKS):
                    rstd(1, s - 1)
                    open_scatter(s, half, j)
                    scatter(s, j, 0, 2)
                    rstd(2, s - 2)
                    scatter(s, j, 2, 6)
                    return
                if at(s, CHUNKS + 1):
                    open_scatter(s, half, j)
                    scatter(s, j, 0, 6)
                    rstd(2, s - 2)
                    scatter(s, j, 6, 2)
                    return
                if layer2:
                    rstd(1, s - 1)
                open_scatter(s, half, j)
                if at(s, CHUNKS + 2):
                    scatter_pairs(nc, kept, slot_list, j, 0, Q)
                    gather_rows(nc, pool, kept, x_src, s_met, 0, 0, Q)
                scatter(s, j, 0, 2)
                if layer1:
                    gated(pool, 0, s, 0)
                scatter(s, j, 2, 2)
                if layer1:
                    gated(pool, 0, s, 1)
                    y_lo(pool, 0, s, 0)
                if within(s, 1, CHUNKS - 2):
                    rstd(0, s + 1)
                if layer1:
                    y_lo(pool, 0, s, 1)
                scatter(s, j, 4, 1)
                if within(s, 2, CHUNKS + 1):
                    rstd(2, s - 2)
                scatter(s, j, 5, 1)
                if layer2:
                    gated(pool, 1, s - 1, 0)
                scatter(s, j, 6, 1)
                if layer2:
                    y_lo(pool, 1, s - 1, 0)
                scatter(s, j, 7, 1)
                if layer2:
                    gated(pool, 1, s - 1, 1)
                    y_lo(pool, 1, s - 1, 1)

            run(pool, step)

        @block.vector
        def _(dve):
            nc.vector.memset(neg_half[:, :], -0.5).then_inc(s_half, 1)
            nc.vector.memset(z[:, :, :], 0.0).then_inc(s_zeros, 1)
            nc.vector.memset(decay[:, :], DECAY).then_inc(s_decay, 1)
            nc.vector.memset(ones[:, :], 1.0).then_inc(s_ones, 1)
            nc.vector.memset(kept.one_row[:, :], 1.0).then_inc(kept.s_tab, 1)
            for l in range(LAYERS):
                nc.vector.memset(carry[:, l, :, :], 0.0).then_inc(s_cy[l], 2)

            def norm_stats(i, src, n):
                for q in range(Q):
                    nc.vector.bn_stats(stats[i][:, q, :], src[:, q, :]).then_inc(s_bn[i], 1)
                dve.wait_ge(s_bn[i], n * Q + Q)
                if within(n, 1, CHUNKS):
                    dve.wait_ge(s_nb[i], n)
                dve.sem_inc(s_met, 1)
                for q in range(Q):
                    nc.vector.bn_aggr(mv[i][:, q, :], stats[i][:, q, :]).then_inc(s_mv[i], 1)
                dve.wait_ge(s_mv[i], n * Q + Q)
                nc.vector.tensor_scalar(ve[i][:, :], mv[i][:, :, 1], EPS, None, ALU.add).then_inc(s_ve[i], 1)
                nc.vector.tensor_scalar(nm[i][:, :], mv[i][:, :, 0], -1.0, None, ALU.mult).then_inc(s_ve[i], 1)

            def x_lo(l, n):
                for dc in range(DC):
                    dve.wait_ge(s_xh[l], n * 2 + dc + 1)
                    nc.vector.tensor_tensor(xl[l][:, dc, :], tp[dc][:, :], xh[l][:, dc, :].bitcast(F32),
                                            ALU.subtract).then_inc(s_xl[l], 1)

            def low_weights(l):
                dve.wait_ge(s_lnp, 16)
                dve.wait_ge(s_w[l], 16)
                for dc in range(DC):
                    dve.wait_ge(s_whi[l], dc + 1)
                    nc.vector.scalar_tensor_tensor(w_lo[:, l, dc, 0:3 * D], w_raw[:, l, dc, 0:3 * D],
                                                   lnp[:, 0, l, dc:dc + 1], w_hi[:, l, dc, 0:3 * D].bitcast(F32),
                                                   ALU.mult, ALU.subtract).then_inc(s_wlo[l], 1)
                dve.wait_ge(s_whi[l], DC + 1)
                nc.vector.tensor_tensor(w_lo[:, l, :, 3 * D:4 * D], w_raw[:, l, :, 3 * D:4 * D],
                                        w_hi[:, l, :, 3 * D:4 * D].bitcast(F32), ALU.subtract).then_inc(s_wlo[l], 1)

            def keep_bias(l):
                dve.wait_ge(s_bias, l + 1)
                nc.vector.tensor_copy(bias[:, l, :, :], out1[1][:, 0, l * 3 * DC:(l + 1) * 3 * DC]
                                      .rearrange("p (m e) -> p m e", m=3)).then_inc(s_biassb[l], 1)
                dve.wait_ge(s_biassb[l], 1)
                nc.vector.tensor_scalar(bias[:, l, 0, :], bias[:, l, 0, :], 1.0 - DECAY, None, ALU.mult).then_inc(s_biassb[l], 1)

            dve.wait_ge(s_x[0], 16)
            norm_stats(0, x_in[:, 0, :, :], 0)
            dve.wait_ge(s_nb[0], 1)
            for q in range(Q):
                last = nc.vector.tensor_scalar(normed[0][:, q, :], x_in[:, 0, q, :], rs[0][:, q:q + 1], nb[0][:, q:q + 1],
                                               ALU.mult, ALU.add)
            last.then_inc(s_n[0], 1)
            low_weights(0)
            x_lo(0, 0)
            keep_bias(0)
            dve.wait_ge(s_x[1], 16)
            norm_stats(0, x_in[:, 1, :, :], 1)
            dve.wait_ge(s_pad, 1)
            nc.vector.tensor_scalar(pad[:, :, 0], pad[:, :, 0], CH - 1, TOKENS, ALU.bitwise_and,
                                    ALU.bitwise_or).then_inc(s_pad, 1)
            dve.wait_ge(s_decay, 1)
            dve.wait_ge(s_expert_no, 1)
            dve.wait_ge(s_base, 1)

            def recur(l, n, e, j):
                dve.wait_ge(s_pg[l], n * 6 + 3 * e + 2)
                dve.wait_ge(s_k[l], n * 2 + e + 1)
                nc.vector.scalar_tensor_tensor(
                    kv[:, e, :], bank(l, e, 1, j), bias[:, l, 1, e:e + 1],
                    k_sb[:, e, :], ALU.add, ALU.mult).then_inc(s_kv[l], 1)
                dve.wait_ge(s_kv[l], n * 2 + e + 1)
                if within(n, 1, CHUNKS):
                    dve.wait_ge(s_y[l], n * 2 + e - 1)
                dve.wait_ge(s_cy[l], n * 2 + 2)
                nc.vector.tensor_tensor_scan(state[l][:, e, :], decay[:, :], kv[:, e, :],
                                             carry[:, l, e, bass.ds(n, 1)], ALU.mult, ALU.add).then_inc(s_sn[l], 1)
                dve.wait_ge(s_sn[l], n * 2 + e + 1)
                nc.vector.tensor_copy(carry[:, l, e, bass.ds(n + B, 1)], state[l][:, e, CH - 1:CH]).then_inc(s_cy[l], 1)

            def link(m, k, ins):
                ins.then_inc(s_rt, 1)
                dve.wait_ge(s_rt, m * ROUTER + k)

            def choose(m):
                dve.wait_ge(s_g, m + 1)
                link(m, 1, nc.vector.tensor_copy(g[:, :, :], out1[0][:, 0, 0:Q * E].rearrange("p (q e) -> p q e", q=Q)))
                dve.sem_inc(s_met, 1)
                for q in range(Q):
                    nc.vector.max(top[:, q, :], g[:, q, :]).then_inc(s_top, 1)
                dve.wait_ge(s_top, m * (2 * Q) + Q)
                dve.sem_inc(s_met, 1)
                for q in range(Q):
                    nc.vector.max_index(pick[:, q, :], top[:, q, :], g[:, q, :]).then_inc(s_top, 1)
                dve.wait_ge(s_top, m * (2 * Q) + 2 * Q)
                link(m, 2, nc.vector.tensor_copy(pick_f[:, :, :], pick[:, :, 0:2].rearrange("p q c -> p c q")))
                if within(m, 1, CHUNKS):
                    dve.wait_ge(s_prob, m)
                nc.vector.tensor_tensor(gap[:, :], top[:, :, 0], top[:, :, 1], ALU.subtract).then_inc(s_gap, 1)
                link(m, 3, nc.vector.tensor_tensor(sel[:, :, :, :], expert_no[:, :, :, :],
                                                   pick_f[:, :, :].unsqueeze(3).to_broadcast([P, 2, Q, E]), ALU.is_equal))
                if within(m, 1, CHUNKS):
                    dve.wait_ge(s_rank, m)
                nc.vector.tensor_tensor(picked[:, :, :], sel[:, 0, :, :], sel[:, 1, :, :], ALU.add).then_inc(s_picked, 1)

            def place(m, half, j):
                ranks = out1[0][:, 0, RANK_AT:RANK_AT + Q * E].rearrange("p (q e) -> p q e", q=Q)
                total = out1[0][:, 0, RANK_AT + Q * E:RANK_AT + Q * E + E]
                dve.wait_ge(s_rank, m + 1)
                link(m, 4, nc.vector.tensor_tensor(slot[:, :, :], ranks, base[:, :].unsqueeze(1).to_broadcast([P, Q, E]), ALU.add))
                nc.vector.tensor_tensor(base[:, :], total, base[:, :], ALU.add).then_inc(s_base, 1)
                link(m, 5, nc.vector.tensor_tensor(own[:, :, :, :], sel[:, :, :, :],
                                                   slot[:, :, :].unsqueeze(1).to_broadcast([P, 2, Q, E]), ALU.mult))
                dve.wait_ge(s_base, m + 2)
                link(m, 6, nc.vector.reduce_sum(slot_f[:, :, :], own[:, :, :, :], AX_X))
                if within(m, 2, CHUNKS):
                    dve.wait_ge(s_sc[1 - j], (half - 2 + j) * SCAT)
                nc.vector.tensor_copy(slot_u[1 - j][:, :, :], slot_f[:, :, :].rearrange("p c q -> p q c")).then_inc(s_slot, 1)

            def residual1(s, j):
                for i, b in enumerate((1, 0)):
                    dve.wait_ge(s_po[0], s * 2 + i - 1)
                    if within(s, 2, CHUNKS):
                        dve.wait_ge(s_u, s - 1)
                    nc.vector.tensor_tensor(xr[:, 2 * b:2 * b + 2, :], out1[b][:, :, :],
                                            x_in[:, 1 - j, 2 * b:2 * b + 2, :], ALU.add).then_inc(s_res, 1)
                dve.wait_ge(s_res, s * 2)

            def add_input(s, j):
                if within(s, 3, CHUNKS):
                    dve.wait_ge(s_z, s * 2 - 4)
                nc.vector.tensor_tensor(u[:, 1 - j, :, :], xr[:, :, :], x_in[:, 1 - j, :, :], ALU.add).then_inc(s_u, 1)

            def residual2(s, j):
                for b in range(2):
                    dve.wait_ge(s_po[1], s * 2 + b - 3)
                    dve.wait_ge(s_u, s - 1)
                    if at(s, 2):
                        dve.wait_ge(s_padst, 48)
                    else:
                        dve.wait_ge(s_x1, s - 2)
                    src = ring[(2 * j + 6 + b) % 4][:, :].rearrange("p (q d) -> p q d", q=2)
                    nc.vector.tensor_tensor(z[:, 2 * b:2 * b + 2, :], src, u[:, j, 2 * b:2 * b + 2, :],
                                            ALU.add).then_inc(s_z, 1)
                dve.wait_ge(s_z, s * 2 - 2)
                norm_stats(2, z, s - 2)

            def step(s, half, j):
                layer1, layer2 = within(s, 0, CHUNKS - 1), within(s, 1, CHUNKS)
                if layer2:
                    residual1(s, j)
                    norm_stats(1, xr, s - 1)
                    if not at(s, CHUNKS):
                        add_input(s, j)
                if at(s, CHUNKS):
                    residual2(s, j)
                if layer1:
                    for e in range(DC):
                        recur(0, s, e, j)
                if at(s, 0):
                    x_lo(0, 1)
                    keep_bias(1)
                    low_weights(1)
                if layer2:
                    x_lo(1, s - 1)
                if within(s, 1, CHUNKS - 2):
                    dve.wait_ge(s_x[1 - j], half * 16 + 16 * (1 + j))
                    norm_stats(0, x_in[:, 1 - j, :, :], s + 1)
                if at(s, CHUNKS):
                    add_input(s, j)
                if within(s, 2, CHUNKS + 1) and not at(s, CHUNKS):
                    residual2(s, j)
                if at(s, CHUNKS):
                    choose(s - 3)
                    for e in range(DC):
                        recur(1, s - 1, e, j)
                        gated(dve, 1, s - 1, e)
                        y_lo(dve, 1, s - 1, e)
                elif layer2:
                    recur(1, s - 1, 0, j)
                if within(s, 3, CHUNKS + 2) and not at(s, CHUNKS):
                    choose(s - 3)
                if within(s, 1, CHUNKS - 2):
                    x_lo(0, s + 1)
                if within(s, 3, CHUNKS + 2):
                    place(s - 3, half, j)
                if at(s, EARLY + 2):
                    dve.wait_ge(s_base, EARLY + 1)
                    big_table(nc, dve, kept)
                if layer2 and not at(s, CHUNKS):
                    recur(1, s - 1, 1, j)

            run(dve, step)
            dve.wait_ge(s_base, CHUNKS + 1)

        @block.tensor
        def _(pe):
            def transpose(i, n, src):
                for dc in range(DC):
                    for q in range(Q):
                        last = nc.tensor.transpose(tp[dc][:, q * P:(q + 1) * P], src[:, q, dc * P:(dc + 1) * P], ident[:, :])
                    last.then_inc(s_pt[i], 1)

            def bias_products(l, products=(0, 1, 2)):
                pe.wait_ge(s_lnp, 16)
                pe.wait_ge(s_w[l], 16)
                for m in products:
                    for e in range(DC):
                        c = (l * 3 + m) * DC + e
                        for dc in range(DC):
                            last = nc.tensor.matmul(out1[1][:, 0, c:c + 1], w_raw[:, l, dc, m * D + e * P:m * D + (e + 1) * P],
                                                    lnp[:, 1, l, dc:dc + 1], start=dc == 0, stop=dc == DC - 1)
                if products[-1] == 2:
                    last.then_inc(s_bias, 1)

            def project(l, s, n, e, j, products=(0, 1, 2)):
                pe.wait_ge(s_xh[l], n * 2 + 2)
                pe.wait_ge(s_xl[l], n * 2 + 2)
                for m in products:
                    slot_no = 8 * l + 3 * e + m
                    if at(s, 0) and slot_no < 4:
                        holder = None
                    elif at(s, 1) and slot_no < 4:
                        holder, count = ((s_r[0], 1), (s_k[0], 2), (s_kv[0], 2), (s_r[0], 2))[slot_no]
                    elif at(s, 1) and slot_no in (10, 11):
                        holder, count = ((s_r[0], 3), (s_k[0], 4))[slot_no - 10]
                    elif at(s, CHUNKS) and slot_no in (8, 9):
                        holder, count = ((s_r[1], 2 * s - 3), (s_k[1], 2 * s - 2))[slot_no - 8]
                    else:
                        holder, count = {
                            0: (s_r[1], s * 2 - 3), 1: (s_k[1], s * 2 - 2), 2: (s_kv[1], s * 2 - 2), 3: (s_r[1], s * 2 - 2),
                            4: (s_k[0], s * 2 + 1), 5: (s_kv[0], s * 2 + 1),
                            8: (s_kv[0], s * 2 + 2), 9: (s_r[0], s * 2 + 2), 10: (s_z, s * 2 - 3), 11: (s_z, s * 2 - 2),
                            12: (s_k[1], s * 2 - 1), 13: (s_kv[1], s * 2 - 1)}[slot_no]
                    if holder is not None:
                        pe.wait_ge(holder, count)
                    out = bank(l, e, m, j)
                    col = m * D + e * P
                    for dc in range(DC):
                        hi, lo = w_hi[:, l, dc, col:col + P], w_lo[:, l, dc, col:col + P]
                        nc.tensor.matmul(out, hi, xh[l][:, dc, :], start=dc == 0, stop=False)
                        nc.tensor.matmul(out, hi, xl[l][:, dc, :], start=False, stop=False)
                        last = nc.tensor.matmul(out, lo, xh[l][:, dc, :], start=False, stop=dc == DC - 1)
                    last.then_inc(s_pg[l], 1)

            def output(l, out, q0):
                for i in range(2):
                    q = q0 + i
                    for dc in range(DC):
                        a, b = yh[l][:, dc, q * P:(q + 1) * P], yl[l][:, dc, q * P:(q + 1) * P]
                        hi, lo = w_hi[:, l, dc, 3 * D:4 * D], w_lo[:, l, dc, 3 * D:4 * D]
                        nc.tensor.matmul(out[:, i * D:(i + 1) * D], a, hi, start=dc == 0, stop=False)
                        nc.tensor.matmul(out[:, i * D:(i + 1) * D], a, lo, start=False, stop=False)
                        last = nc.tensor.matmul(out[:, i * D:(i + 1) * D], b, hi, start=False, stop=dc == DC - 1)
                last.then_inc(s_po[l], 1)

            def rows2(s, last_users):
                pe.wait_ge(s_n[1], s)
                for holder, count in last_users:
                    pe.wait_ge(holder, count)
                transpose(1, s - 1, normed[1])

            def output2(s, j):
                pe.wait_ge(s_yh[1], s * 2 - 2)
                pe.wait_ge(s_yl[1], s * 2 - 2)
                for b in range(2):
                    if within(s, 0, CHUNKS - 1):
                        pe.wait_ge((s_r[0], s_k[0])[b], s * 2 + 1 + b)
                    else:
                        pe.wait_ge((s_kv[1], s_r[1])[b], s * 2 - 2)
                    output(1, ring[(2 * j + 6 + b) % 4][:, :], 2 * b)

            def rows3(s, j, last_user, count):
                pe.wait_ge(s_x1, s - 2)
                pe.wait_ge(last_user, count)
                transpose(2, s - 3, x1[:, 1 - j, :, :])

            def gates(s, last_user, count):
                pe.wait_ge(s_x1T, s * 2 - 4)
                pe.wait_ge(last_user, count)
                for q in range(Q):
                    for dc in range(DC):
                        last = nc.tensor.matmul(out1[0][:, 0, q * E:(q + 1) * E], x1T[:, dc, q * P:(q + 1) * P],
                                                wg[:, dc, :], start=dc == 0, stop=dc == DC - 1)
                last.then_inc(s_g, 1)

            bias_products(0, (0,))
            pe.wait_ge(s_ident, 1)
            pe.wait_ge(s_n[0], 1)
            transpose(0, 0, normed[0])
            bias_products(0, (1, 2))
            pe.wait_ge(s_whi[0], DC + 1)
            pe.wait_ge(s_wlo[0], DC + 1)

            def step(s, half, j):
                layer1, layer2 = within(s, 0, CHUNKS - 1), within(s, 1, CHUNKS)
                if layer1:
                    for e in range(DC):
                        project(0, s, s, e, j)
                if at(s, 0):
                    pe.wait_ge(s_n[0], 2)
                    pe.wait_ge(s_xl[0], 2)
                    transpose(0, 1, normed[0])
                    bias_products(1)
                    pe.wait_ge(s_before, 1)
                    pe.wait_ge(s_ones, 1)
                if at(s, 1):
                    pe.wait_ge(s_whi[1], DC + 1)
                    pe.wait_ge(s_wlo[1], DC + 1)
                if at(s, CHUNKS):
                    output2(s, j)
                    rows3(s, j, s_xl[0], 2 * s)
                    rows2(s, ((s_x1T, s * 2 - 4),))
                    gates(s, s_res, s * 2)
                    project(1, s, s - 1, 0, j)
                elif at(s, CHUNKS + 1):
                    rows3(s, j, s_xl[1], 2 * s - 2)
                    output2(s, j)
                    gates(s, s_slot, s - 3)
                elif at(s, CHUNKS + 2):
                    rows3(s, j, s_x1T, 2 * s - 6)
                    gates(s, s_slot, s - 3)
                else:
                    if layer2:
                        rows2(s, ((s_xl[0], s * 2 + 2),))
                    if within(s, 2, CHUNKS):
                        output2(s, j)
                    if within(s, 3, CHUNKS):
                        rows3(s, j, s_xl[1], s * 2)
                    if layer2:
                        project(1, s, s - 1, 0, j)
                    if at(s, 3):
                        pe.wait_ge(s_wg, 16)
                    if within(s, 3, CHUNKS):
                        gates(s, s_res, s * 2)
                if within(s, 1, CHUNKS - 2):
                    pe.wait_ge(s_n[0], s + 2)
                    if within(s, 1, 2) and isinstance(s, int):
                        pe.wait_ge(s_xl[1], 2 * s)
                    else:
                        pe.wait_ge(s_x1T, s * 2 - 4)
                    transpose(0, s + 1, normed[0])
                if layer2:
                    project(1, s, s - 1, 1, j, (0, 1))
                if within(s, 3, CHUNKS + 2):
                    pe.wait_ge(s_picked, s - 2)
                    ranks = out1[0][:, 0, RANK_AT:RANK_AT + Q * E]
                    flat = picked[:, :, :].rearrange("p q e -> p (q e)")
                    nc.tensor.matmul(ranks, before[:, :], flat, start=True, stop=False)
                    for d in range(1, Q):
                        nc.tensor.matmul(ranks[:, d * E:Q * E], ones[:, :], flat[:, 0:(Q - d) * E], start=False, stop=d == Q - 1)
                    for q in range(Q):
                        last = nc.tensor.matmul(out1[0][:, 0, RANK_AT + Q * E:RANK_AT + Q * E + E], ones[:, :],
                                                picked[:, q, :], start=q == 0, stop=q == Q - 1)
                    last.then_inc(s_rank, 1)
                if layer2:
                    project(1, s, s - 1, 1, j, (2,))
                if layer1:
                    pe.wait_ge(s_yh[0], s * 2 + 2)
                    pe.wait_ge(s_yl[0], s * 2 + 2)
                    if within(s, 1, CHUNKS):
                        pe.wait_ge(s_res, s * 2)
                    else:
                        pe.wait_ge(s_biassb[0], 2)
                        pe.wait_ge(s_biassb[1], 2)
                    output(0, out1[1][:, :, :].rearrange("p q d -> p (q d)"), 2)
                    if within(s, 3, CHUNKS):
                        pe.wait_ge(s_slot, s - 2)
                    output(0, out1[0][:, :, :].rearrange("p q d -> p (q d)"), 0)

            run(pe, step)


def expert_phase(nc, w_ffn, x_src, x_acc, slot_list, kept):
    ident, table, pair_in, xg = kept.ident, kept.table, kept.pair_in, kept.xg
    s_w, s_pair, s_xg = kept.s_w, kept.s_pair, kept.s_xg
    with ExitStack() as ctx:
        def sb(name, shape, dt=F32):
            return ctx.enter_context(nc.sbuf_tensor(name, shape, dt))

        def sem(name):
            return ctx.enter_context(nc.semaphore(name))

        ring = [ctx.enter_context(nc.psum_tensor(f"fring{i}", [P, CH], F32)) for i in range(4)]
        tp = [ctx.enter_context(nc.psum_tensor(f"ftp{i}", [P, CH], F32)) for i in range(DC)]
        yp = [ctx.enter_context(nc.psum_tensor(f"fy{i}", [P, 2, D], F32)) for i in range(2)]

        w_raw = kept.w_raw[:, :].rearrange("p (j c) -> p j c", j=2)
        w_hi = sb("fw_hi", [P, 2, WCOLS], F32R)
        w_lo = sb("fw_lo", [P, 2, WCOLS], F32R)
        pair_out = [sb(f"pair_out{i}", [P, Q, 2], I32) for i in range(2)]
        xh = sb("fxh", [P, DC, CH], F32R)
        xl = sb("fxl", [P, DC, CH], F32R)
        silu = sb("silu", [P, 2, CH])
        gated = sb("gated", [P, 2, CH])
        gh = sb("gh", [P, 2, HC, CH], F32R)
        gl = sb("gl", [P, 2, HC, CH], F32R)
        y = [sb(f"fy_sb{i}", [P, Q, D]) for i in range(2)]

        zero = sb("fzero", [P, 1])
        warm = sb("fwarm", [P, 1])

        s_met, s_zero = sem("fwaits_met"), sem("fzero_ready")
        s_pair_out = [sem("pairs_out0"), sem("pairs_out1")]
        s_add = [sem("rows_added0"), sem("rows_added1")]
        s_pt, s_xh, s_xl = sem("ftransposed"), sem("fxh_ready"), sem("fxl_ready")
        s_h, s_silu, s_g, s_gh, s_gl = sem("h_product"), sem("silu_ready"), sem("gated_ready"), sem("gh_ready"), sem("gl_ready")
        s_y, s_yv = sem("y_product"), sem("y_weighted")
        s_whi = [sem(f"whi_ready{i}") for i in range(3)]
        s_wlo = [sem(f"wlo_ready{i}") for i in range(3)]

        block = ctx.enter_context(nc.Block())

        def run(eng, step):
            def peeled(first, end):
                for s in range(first, end):
                    step(s, s // 2, s % 2, lambda d: Q if s + d < BIG else Q // 2)

            def loop(first, end, size):
                with eng.Fori(first // 2, end // 2) as it:
                    step(it * 2, it, 0, size)
                    step(it * 2 + 1, it, 1, size)

            last = (BLOCKS - 2) // 2 * 2
            peeled(-1, 4)
            loop(4, BIG - 2, lambda d: Q)
            peeled(BIG - 2, BIG + 4)
            loop(BIG + 4, last, lambda d: Q // 2)
            peeled(last, BLOCKS + 2)

        def moved(half, tiles):
            if tiles == Q:
                return (half + 1) * (16 * Q)
            return (half + 1) * (16 * (Q // 2)) + 16 * (Q - Q // 2) * (BIG // 2)

        @block.sync
        def _(sp):
            def first_row(which, b, bound):
                column = slice(b, b + 1) if isinstance(b, int) else bass.ds(b, 1)
                return sp.value_load(table[0:1, which, column], min_val=0, max_val=bound)

            def pairs(b, dst, j, tiles, done):
                row = first_row(1, b, SLOTS - CH)
                return sp.dma_start(dst[j][:, 0:tiles, :], slot_list[bass.ds(row, tiles * P), :]
                                    .rearrange("(p q) c -> p q c", p=P)).then_inc(done, 16)

            def weights(b, j, i, w_row):
                low, high = PART[i]
                if within(b, 2, BLOCKS):
                    sp.wait_ge(s_whi[i], b - 1)
                    sp.wait_ge(s_wlo[i], b - 1)
                sp.dma_start(w_raw[:, j, low:high], w_ffn[bass.ds(w_row, P), low:high]).then_inc(s_w[i][j], 16)

            def step(s, half, j, size):
                if at(s, -1):
                    pairs(1, pair_in, 1, Q, s_pair[1])
                    w_row = first_row(0, 1, (E - 1) * P)
                    for i in range(3):
                        weights(1, 1, i, w_row)
                if at(s, BIG - 2):
                    sp.wait_ge(kept.s_table, 4)
                    for par in range(2):
                        sp.wait_ge(kept.s_sc[par], SCAT * (CHUNKS // 2))
                if within(s, 0, BLOCKS - 3):
                    w_row = first_row(0, s + 2, (E - 1) * P)
                    for i in range(2):
                        weights(s + 2, j, i, w_row)
                    sp.wait_ge(s_xg[j], moved(half, size(0)))
                    pairs(s + 2, pair_in, j, size(2), s_pair[j])
                    weights(s + 2, j, 2, w_row)
                if within(s, 0, BLOCKS - 1):
                    if within(s, 2, BLOCKS - 1):
                        sp.wait_ge(s_add[j], moved(half - 1, size(-2)))
                    pairs(s, pair_out, j, size(0), s_pair_out[j])

            run(sp, step)
            for par in range(2):
                sp.wait_ge(s_add[par], moved((BLOCKS - 1 - par) // 2, Q // 2))

        @block.gpsimd
        def _(pool):
            scatter_pairs(nc, kept, slot_list, 0, Q, Q)

            def step(s, half, j, size):
                if within(s, 0, BLOCKS - 2):
                    if within(s, 1, BLOCKS):
                        pool.wait_ge(s_pt, s * 2)
                    gather_rows(nc, pool, kept, x_src, s_met, half + j, 1 - j, size(1))
                if within(s, 2, BLOCKS + 1):
                    if within(s, 3, BLOCKS + 1):
                        pool.wait_ge(s_add[1 - j], moved(half - 2 + j, size(-3)))
                    pool.wait_ge(s_yv, s * 2 - 2)
                    pool.sem_inc(s_met, 1)
                    for q in range(size(-2)):
                        nc.gpsimd.indirect_dma_start(
                            x_acc, bass.IndirectOffsetOnAxis(pair_out[j][:, q, 0:1].bitcast(U32), 0),
                            y[j][:, q, :], None, compute_op=ALU.add).then_inc(s_add[j], 16)
                if within(s, 0, BLOCKS - 2):
                    low, high = PART[0]
                    pool.wait_ge(s_whi[0], s + 2)
                    nc.gpsimd.tensor_tensor(w_lo[:, 1 - j, low:high], w_raw[:, 1 - j, low:high],
                                            w_hi[:, 1 - j, low:high].bitcast(F32), ALU.subtract).then_inc(s_wlo[0], 1)
                if at(s, 0):
                    scatter_pairs(nc, kept, slot_list, 1, 0, 2 * Q)

            run(pool, step)

        @block.scalar
        def _(act):
            def w_half(i, b, half, j):
                low, high = PART[i]
                act.wait_ge(s_w[i][j], half * 16 + 16)
                if within(b, 2, BLOCKS):
                    if i < 2:
                        act.wait_ge(s_h, b * (2 * HC) - 2 * HC)
                    else:
                        act.wait_ge(s_y, b * 2 - 2)
                nc.scalar.activation(w_hi[:, j, low:high], w_raw[:, j, low:high], ACT.Copy).then_inc(s_whi[i], 1)

            def act_silu(b, hb, n):
                act.wait_ge(s_h, b * (2 * HC) + 2 * hb + 1)
                if hb >= 2 or within(b, 1, BLOCKS):
                    act.wait_ge(s_g, b * HC + hb - 1)
                nc.scalar.activation(silu[:, hb % 2, 0:n], ring[2 * (hb % 2)][:, 0:n], ACT.Silu).then_inc(s_silu, 1)

            def g_hi(b, j, hb, n):
                act.wait_ge(s_g, b * HC + hb + 1)
                if within(b, 2, BLOCKS):
                    act.wait_ge(s_y, b * 2 - 2)
                nc.scalar.activation(gh[:, j, hb, 0:n], gated[:, hb % 2, 0:n], ACT.Copy).then_inc(s_gh, 1)

            def x_hi(b, n):
                for dc in range(DC):
                    act.wait_ge(s_pt, b * 2 + dc + 1)
                    nc.scalar.activation(xh[:, dc, 0:n], tp[dc][:, 0:n], ACT.Copy).then_inc(s_xh, 1)

            def step(s, half, j, size):
                here, nxt, n = within(s, 0, BLOCKS - 1), within(s, -1, BLOCKS - 2), size(0) * P
                if here:
                    w_half(2, s, half, j)
                    act_silu(s, 0, n)
                if nxt:
                    w_half(0, s + 1, half + j, 1 - j)
                if here:
                    act_silu(s, 1, n)
                    g_hi(s, j, 0, n)
                    act_silu(s, 2, n)
                    g_hi(s, j, 1, n)
                if nxt:
                    w_half(1, s + 1, half + j, 1 - j)
                if here:
                    act_silu(s, 3, n)
                    g_hi(s, j, 2, n)
                if nxt:
                    x_hi(s + 1, size(1) * P)
                if at(s, -1):
                    act.wait_ge(s_zero, 1)
                    nc.scalar.activation(warm[:, :], zero[:, :], ACT.Silu)
                if here:
                    g_hi(s, j, 3, n)

            run(act, step)

        @block.vector
        def _(dve):
            nc.vector.memset(zero[:, :], 0.0).then_inc(s_zero, 1)

            def w_low(i, b, half, j):
                low, high = PART[i]
                dve.wait_ge(s_whi[i], b + 1)
                nc.vector.tensor_tensor(w_lo[:, j, low:high], w_raw[:, j, low:high],
                                        w_hi[:, j, low:high].bitcast(F32), ALU.subtract).then_inc(s_wlo[i], 1)

            def gate(b, hb, n):
                dve.wait_ge(s_h, b * (2 * HC) + 2 * hb + 2)
                dve.wait_ge(s_silu, b * HC + hb + 1)
                if hb >= 2 or within(b, 1, BLOCKS):
                    dve.wait_ge(s_gl, b * HC + hb - 1)
                nc.vector.tensor_tensor(gated[:, hb % 2, 0:n], ring[2 * (hb % 2) + 1][:, 0:n], silu[:, hb % 2, 0:n],
                                        ALU.mult).then_inc(s_g, 1)

            def g_lo(b, j, hb, n):
                dve.wait_ge(s_gh, b * HC + hb + 1)
                nc.vector.tensor_tensor(gl[:, j, hb, 0:n], gated[:, hb % 2, 0:n], gh[:, j, hb, 0:n].bitcast(F32),
                                        ALU.subtract).then_inc(s_gl, 1)

            def x_lo(b, n):
                for dc in range(DC):
                    dve.wait_ge(s_xh, b * 2 + dc + 1)
                    nc.vector.tensor_tensor(xl[:, dc, 0:n], tp[dc][:, 0:n], xh[:, dc, 0:n].bitcast(F32),
                                            ALU.subtract).then_inc(s_xl, 1)

            def weigh(b, half, j, tiles):
                dve.wait_ge(s_pair_out[j], half * 16 + 16)
                for q in range(tiles):
                    bank, column = q // (tiles // 2), q % (tiles // 2)
                    dve.wait_ge(s_y, b * 2 + bank + 1)
                    last = nc.vector.tensor_scalar(y[j][:, q, :], yp[bank][:, column, :], pair_out[j][:, q, 1:2].bitcast(F32),
                                                   None, ALU.mult)
                    if column == tiles // 2 - 1:
                        last.then_inc(s_yv, 1)

            def step(s, half, j, size):
                here, nxt, n = within(s, 0, BLOCKS - 1), within(s, -1, BLOCKS - 2), size(0) * P
                if here:
                    w_low(2, s, half, j)
                    gate(s, 0, n)
                    gate(s, 1, n)
                    g_lo(s, j, 0, n)
                    gate(s, 2, n)
                    g_lo(s, j, 1, n)
                if at(s, -1):
                    w_low(0, 0, 0, 0)
                    x_lo(0, size(1) * P)
                if nxt:
                    w_low(1, s + 1, half + j, 1 - j)
                if here:
                    gate(s, 3, n)
                    g_lo(s, j, 2, n)
                if nxt and not at(s, -1):
                    x_lo(s + 1, size(1) * P)
                if here:
                    g_lo(s, j, 3, n)
                if within(s, 1, BLOCKS):
                    weigh(s - 1, half - 1 + j, 1 - j, size(-1))
                if at(s, 2):
                    small_counts(nc, dve, kept)
                if at(s, 3):
                    fill_table(nc, dve, kept, 1, BIG, BLOCKS - BIG, SMALL)

            run(dve, step)

        @block.tensor
        def _(pe):
            def hidden(b, j, hb, n):
                for i in range(2):
                    if hb >= 2 or within(b, 1, BLOCKS):
                        if i == 0:
                            pe.wait_ge(s_silu, b * HC + hb - 1)
                        else:
                            pe.wait_ge(s_g, b * HC + hb - 1)
                    if hb == 0:
                        pe.wait_ge(s_whi[i], b + 1)
                        pe.wait_ge(s_wlo[i], b + 1)
                    out = ring[2 * (hb % 2) + i][:, 0:n]
                    for dc in range(DC):
                        col = PART[i][0] + dc * H + hb * P
                        hi, lo = w_hi[:, j, col:col + P], w_lo[:, j, col:col + P]
                        nc.tensor.matmul(out, hi, xh[:, dc, 0:n], start=dc == 0, stop=False)
                        nc.tensor.matmul(out, hi, xl[:, dc, 0:n], start=False, stop=False)
                        last = nc.tensor.matmul(out, lo, xh[:, dc, 0:n], start=False, stop=dc == DC - 1)
                    last.then_inc(s_h, 1)

            def step(s, half, j, size):
                if within(s, 0, BLOCKS - 1):
                    pe.wait_ge(s_xh, s * 2 + 2)
                    pe.wait_ge(s_xl, s * 2 + 2)
                    for hb in range(HC):
                        hidden(s, j, hb, size(0) * P)
                if within(s, -1, BLOCKS - 2):
                    pe.wait_ge(s_xg[1 - j], moved(half + j, size(1)))
                    if within(s, 0, BLOCKS):
                        pe.wait_ge(s_xl, s * 2 + 2)
                    for dc in range(DC):
                        for q in range(size(1)):
                            last = nc.tensor.transpose(tp[dc][:, q * P:(q + 1) * P], xg[1 - j][:, q, dc * P:(dc + 1) * P],
                                                       ident[:, :])
                        last.then_inc(s_pt, 1)
                if within(s, 1, BLOCKS):
                    b, tiles = s - 1, size(-1)
                    pe.wait_ge(s_gh, b * HC + HC)
                    pe.wait_ge(s_gl, b * HC + HC)
                    pe.wait_ge(s_whi[2], b + 1)
                    pe.wait_ge(s_wlo[2], b + 1)
                    for q in range(tiles):
                        bank, column = q // (tiles // 2), q % (tiles // 2)
                        if within(s, 2, BLOCKS) and column == 0:
                            pe.wait_ge(s_yv, b * 2 - 1 + bank)
                        out = yp[bank][:, column, :]
                        for hc in range(HC):
                            col = PART[2][0] + hc * D
                            hi, lo = w_hi[:, 1 - j, col:col + D], w_lo[:, 1 - j, col:col + D]
                            a, c = gh[:, 1 - j, hc, q * P:(q + 1) * P], gl[:, 1 - j, hc, q * P:(q + 1) * P]
                            nc.tensor.matmul(out, a, hi, start=hc == 0, stop=False)
                            nc.tensor.matmul(out, a, lo, start=False, stop=False)
                            last = nc.tensor.matmul(out, c, hi, start=False, stop=hc == HC - 1)
                        if column == tiles // 2 - 1:
                            last.then_inc(s_y, 1)

            run(pe, step)


def norm_phase(nc, x_acc, out):
    DEPTH = 8
    TILES = 2
    ROWS = TILES * P
    STEPS = TOKENS // ROWS
    out_rows = out.rearrange("r (q d) -> (r q) d", q=Q)
    with ExitStack() as ctx:
        def sb(name, shape, dt=F32):
            return ctx.enter_context(nc.sbuf_tensor(name, shape, dt))

        def sem(name):
            return ctx.enter_context(nc.semaphore(name))

        a = [sb(f"acc{i}", [P, TILES, D]) for i in range(DEPTH)]
        o = [sb(f"o{i}", [P, TILES, D]) for i in range(DEPTH)]
        stats = sb("nstats", [P, DEPTH, TILES, 6])
        mv = sb("nmv", [P, DEPTH, TILES, 2])
        ve = sb("nve", [P, DEPTH, TILES])
        nm = sb("nnm", [P, DEPTH, TILES])
        rs = sb("nrs", [P, DEPTH, TILES])
        nb = sb("nnb", [P, DEPTH, TILES])
        neg_half = sb("nneg_half", [P, TILES])
        warm = sb("nwarm", [P, TILES])
        s_in = [sem(f"acc_loaded{i}") for i in range(DEPTH)]
        s_out = [sem(f"out_stored{i}") for i in range(DEPTH)]
        s_half, s_bn, s_mv, s_ve, s_rs, s_nb, s_o = (sem("nneg_half_ready"), sem("nstats_ready"), sem("nmean_var"),
                                                     sem("nvar_eps"), sem("nrstd"), sem("nnorm_bias"), sem("normed_rows"))
        s_met = sem("nwaits_met")
        block = ctx.enter_context(nc.Block())

        def run(eng, step):
            for n in range(DEPTH):
                step(n, 0, n)
            with eng.Fori(1, STEPS // DEPTH) as it:
                for j in range(DEPTH):
                    step(it * DEPTH + j, it, j)

        @block.sync
        def _(sp):
            def store(n, row, j):
                sp.wait_ge(s_o, n + 1)
                sp.dma_start(out_rows[bass.ds(row, ROWS), :].rearrange("(p q) d -> p q d", p=P),
                             o[j][:, :, :]).then_inc(s_out[j], 16)

            def step(n, turn, j):
                row = n * ROWS if isinstance(n, int) else sp.snap(n * ROWS)
                if within(n, DEPTH, STEPS):
                    store(n - DEPTH, sp.snap(n * ROWS - DEPTH * ROWS), j)
                sp.dma_start(a[j][:, :, :], x_acc[bass.ds(row, ROWS), :]
                             .rearrange("(p q) d -> p q d", p=P)).then_inc(s_in[j], 16)

            run(sp, step)
            for n in range(STEPS - DEPTH, STEPS):
                store(n, n * ROWS, n % DEPTH)
            for j in range(DEPTH):
                sp.wait_ge(s_out[j], 16 * (STEPS // DEPTH))

        @block.vector
        def _(dve):
            nc.vector.memset(neg_half[:, :], -0.5).then_inc(s_half, 1)

            def step(n, turn, j):
                dve.wait_ge(s_in[j], turn * 16 + 16)
                for q in range(TILES):
                    nc.vector.bn_stats(stats[:, j, q, :], a[j][:, q, :]).then_inc(s_bn, 1)
                dve.wait_ge(s_bn, n * TILES + TILES)
                if within(n, DEPTH, STEPS):
                    dve.wait_ge(s_nb, n - DEPTH + 1)
                dve.sem_inc(s_met, 1)
                for q in range(TILES):
                    nc.vector.bn_aggr(mv[:, j, q, :], stats[:, j, q, :]).then_inc(s_mv, 1)
                dve.wait_ge(s_mv, n * TILES + TILES)
                nc.vector.tensor_scalar(ve[:, j, :], mv[:, j, :, 1], EPS, None, ALU.add).then_inc(s_ve, 1)
                nc.vector.tensor_scalar(nm[:, j, :], mv[:, j, :, 0], -1.0, None, ALU.mult).then_inc(s_ve, 1)

            run(dve, step)

        @block.gpsimd
        def _(pool):
            pool.wait_ge(s_half, 1)

            def step(n, turn, j):
                pool.wait_ge(s_ve, n * 2 + 2)
                if within(n, DEPTH, STEPS):
                    pool.wait_ge(s_o, n - DEPTH + 1)
                nc.gpsimd.tensor_tensor(rs[:, j, :], ve[:, j, :], neg_half[:, :], ALU.pow).then_inc(s_rs, 1)
                pool.wait_ge(s_rs, n + 1)
                nc.gpsimd.tensor_tensor(nb[:, j, :], rs[:, j, :], nm[:, j, :], ALU.mult).then_inc(s_nb, 1)

            run(pool, step)

        @block.scalar
        def _(act):
            act.wait_ge(s_half, 1)
            nc.scalar.activation(warm[:, :], neg_half[:, :], ACT.Identity)

            def step(n, turn, j):
                act.wait_ge(s_nb, n + 1)
                if within(n, DEPTH, STEPS):
                    act.wait_ge(s_out[j], turn * 16)
                for q in range(TILES):
                    last = nc.scalar.activation(o[j][:, q, :], a[j][:, q, :], ACT.Identity,
                                                bias=nb[:, j, q:q + 1], scale=rs[:, j, q:q + 1])
                last.then_inc(s_o, 1)

            run(act, step)


def build(nc, h, w_att, ln_wb, w_gate, w_ffn, out):
    x_src = nc.dram_tensor("x_src", (TOKENS + CH, D), F32).ap()
    x_acc = nc.dram_tensor("x_acc", (TOKENS + CH, D), F32).ap()
    slot_list = nc.dram_tensor("slot_list", (SLOTS, 2), I32).ap()
    with ExitStack() as ctx:
        def sb(name, shape, dt=F32):
            return ctx.enter_context(nc.sbuf_tensor(name, shape, dt))

        def sems(name, n):
            return [ctx.enter_context(nc.semaphore(f"{name}{i}")) for i in range(n)]

        kept = Kept()
        kept.ident = sb("ident", [P, P])
        kept.w_raw = sb("w_raw", [P, 2 * WCOLS])
        kept.base = sb("base", [P, E])
        kept.slot_u = [sb(f"slot_u{i}", [P, Q, 2], U32) for i in range(2)]
        kept.pairs = [sb(f"pairs{i}", [P, Q, 2, 2]) for i in range(2)]
        kept.pair_in = [sb(f"pair_in{i}", [P, Q, 2], I32) for i in range(2)]
        kept.xg = [sb(f"xg{i}", [P, Q, D]) for i in range(2)]
        kept.table = sb("table", [1, 2, BLOCKS], I32)
        kept.block_no = sb("block_no", [1, BLOCKS])
        kept.start = sb("start", [1, E])
        kept.one_row = sb("one_row", [1, E])
        kept.used = sb("used", [1, E])
        kept.used_i = sb("used_i", [1, E], I32)
        kept.full = sb("full", [1, E])
        kept.before = sb("before_e", [1, E])
        kept.taken = sb("taken", [1, E + 1])
        kept.end = sb("end", [1, 2, E])
        kept.skip = sb("skip", [1, 2, E])
        kept.past = sb("past", [1, BLOCKS, E])
        kept.hop = sb("hop", [1, BLOCKS, E])
        kept.rows = sb("rows", [1, 2, BLOCKS])
        kept.table_steps = 3
        kept.s_tab = sems("table_steps", 1)[0]
        kept.s_table = sems("table_ready", 1)[0]
        kept.s_sc = sems("scattered", 2)
        kept.s_pair = sems("pairs_in", 2)
        kept.s_xg = sems("rows_gathered", 2)
        kept.s_w = [sems(f"w{i + 1}_loaded", 2) for i in range(3)]
        attention_phase(nc, h, w_att, ln_wb, w_gate, w_ffn, x_src, x_acc, slot_list, kept)
        expert_phase(nc, w_ffn, x_src, x_acc, slot_list, kept)
        norm_phase(nc, x_acc, out)


def kernel(L0_attn_h, L0_attn_ln_w, L0_attn_ln_b, L0_attn_Wk, L0_attn_Wv, L0_attn_Wr, L0_attn_Wo,
           L0_ffn_Wg, L0_ffn_W1, L0_ffn_W2, L0_ffn_W3):
    import concourse.bacc as bacc
    import numpy as np
    from concourse.bass_utils import run_bass_kernel_spmd

    def by_partition(a, rows):
        a = np.asarray(a)
        a = a.reshape(a.shape[:-2] + (rows // P, P, a.shape[-1]))
        return np.ascontiguousarray(np.moveaxis(a, -2, 0))

    PIECES = T // CH
    x = np.asarray(L0_attn_h).reshape(B, PIECES, Q, P, D).transpose(1, 0, 3, 2, 4).reshape(CHUNKS * P, Q * D)
    att = np.concatenate([np.asarray(w).transpose(0, 2, 1) for w in (L0_attn_Wk, L0_attn_Wv, L0_attn_Wr, L0_attn_Wo)], axis=2)
    wb = np.stack([np.asarray(L0_attn_ln_w), np.asarray(L0_attn_ln_b)]).reshape(2, LAYERS, DC, P).transpose(3, 0, 1, 2)
    w1, w2, w3 = (by_partition(np.asarray(w).transpose(0, 2, 1), rows).transpose(1, 0, 2, 3).reshape(E * P, -1)
                  for w, rows in ((L0_ffn_W1, D), (L0_ffn_W2, D), (L0_ffn_W3, H)))
    arrays = {
        "h": np.ascontiguousarray(x),
        "w_att": by_partition(att, D),
        "ln_wb": np.ascontiguousarray(wb),
        "w_gate": by_partition(np.asarray(L0_ffn_Wg).T, D),
        "w_ffn": np.ascontiguousarray(np.concatenate([w1, w2, w3], axis=1)),
    }
    nc = bacc.Bacc("TRN2", target_bir_lowering=False, num_devices=1)
    args = [nc.dram_tensor(name, a.shape, F32, kind="ExternalInput").ap() for name, a in arrays.items()]
    out = nc.dram_tensor("out", (CHUNKS * P, Q * D), F32, kind="ExternalOutput").ap()
    build(nc, *args, out)
    result = run_bass_kernel_spmd(nc, [arrays], core_ids=[0]).results[0]["out"]
    return result.reshape(PIECES, B, P, Q, D).transpose(1, 0, 3, 2, 4).reshape(B, T, D)
```
